# Optimizing a Trainium2 kernel written in Bass

```python
import numpy as np
import jax
import jax.numpy as jnp

def _softmax(x, axis=-1):
    return jax.nn.softmax(x, axis=axis)

def _gelu(x):
    return jax.nn.gelu(x, approximate=True)

def _silu(x):
    return jax.nn.silu(x)

def _sigmoid(x):
    return jax.nn.sigmoid(x)

def _layernorm(x, axis=-1, eps=1e-05):
    m = jnp.mean(x, axis=axis, keepdims=True)
    v = jnp.var(x, axis=axis, keepdims=True)
    return (x - m) / jnp.sqrt(v + eps)

def _scatter_add(tgt, idx, src, axis=0):
    return tgt.at[idx].add(src)

def _segment_sum(src, seg, n):
    return jax.ops.segment_sum(src, seg, n)
kernel_name = 'mk_adaln_ffn_d2_seqx_r8_8a9123'

def setup_inputs(seed: int=0):
    np.random.seed(seed)
    _w = jnp.asarray

    def _rec_inputs():
        import jax
        import jax.numpy as jnp
        _rk = jax.random.key(seed)
        x = -7.109e-05 + 0.9999 * jax.random.normal(jax.random.fold_in(_rk, 1), (128, 32, 256), jnp.float32)
        _lenS = 32 - jax.random.randint(jax.random.fold_in(_rk, 7), (128,), 0, max(1, 32 // 4) + 1, jnp.int32)
        _lenS2 = 32 - jax.random.randint(jax.random.fold_in(_rk, 8), (128,), 0, max(1, 32 // 4) + 1, jnp.int32)
        itok_B_0_6 = jax.random.randint(jax.random.fold_in(_rk, 11), (128,), 0, 7, jnp.int32)
        itok_B_1_198 = jax.random.randint(jax.random.fold_in(_rk, 12), (128,), 1, 199, jnp.int32)
        return (x, itok_B_0_6, itok_B_1_198)
    x, itok_B_0_6, itok_B_1_198 = _rec_inputs()

    def _L0_cond_setup():
        import jax, jax.numpy as jnp
        import numpy as np
        B, T, D_IN, D_OUT = (16, 256, 256, 256)
        N_ADAPTERS, RANK = (8, 16)
        key = jax.random.key(seed)
        k_x, k_w, k_a, k_b, k_s, k_idx = jax.random.split(key, 6)
        x = jax.random.normal(k_x, (B, T, D_IN), dtype=jnp.float32)
        W = jax.random.normal(k_w, (D_OUT, D_IN), dtype=jnp.float32) * (1.0 / np.sqrt(D_IN))
        A = jax.random.normal(k_a, (N_ADAPTERS, RANK, D_IN), dtype=jnp.float32) * 0.02
        Bm = jax.random.normal(k_b, (N_ADAPTERS, D_OUT, RANK), dtype=jnp.float32) * 0.02
        scalings = jnp.ones((N_ADAPTERS,), dtype=jnp.float32)
        adapter_idx = jax.random.randint(k_idx, (B,), 0, N_ADAPTERS, dtype=jnp.int32)
        return {'x': x, 'W': W, 'A': A, 'Bm': Bm, 'scalings': scalings, 'adapter_idx': adapter_idx}
    _L0_cond_all = _L0_cond_setup()
    _L0_cond_in = {k: v for k, v in _L0_cond_all.items() if k in ('W', 'A', 'Bm', 'scalings')}
    del _L0_cond_all

    def _L0_ffn_setup():
        import jax, jax.numpy as jnp
        import numpy as np
        TOP_K = 2
        NUM_EXPERTS = 8
        ROUTE_SCALE = 1.0
        key = jax.random.key(seed)
        ks = jax.random.split(key, 8)
        bs, slen, dim, hidden, E = (4, 128, 256, 128, NUM_EXPERTS)
        s = 0.02
        return {'x': jax.random.normal(ks[0], (bs, slen, dim), jnp.float32), 'gate_w': jax.random.normal(ks[1], (E, dim), jnp.float32) * s, 'w1': jax.random.normal(ks[2], (E, hidden, dim), jnp.float32) * s, 'w2': jax.random.normal(ks[3], (E, dim, hidden), jnp.float32) * s, 'w3': jax.random.normal(ks[4], (E, hidden, dim), jnp.float32) * s, 'ws1': jax.random.normal(ks[5], (hidden, dim), jnp.float32) * s, 'ws2': jax.random.normal(ks[6], (dim, hidden), jnp.float32) * s, 'ws3': jax.random.normal(ks[7], (hidden, dim), jnp.float32) * s}
    _L0_ffn_all = _L0_ffn_setup()
    _L0_ffn_in = {k: v for k, v in _L0_ffn_all.items() if k in ('gate_w', 'w1', 'w2', 'w3', 'ws1', 'ws2', 'ws3')}
    del _L0_ffn_all

    def _L1_cond_setup():
        import jax, jax.numpy as jnp
        import numpy as np
        B, C, T = (128, 32, 256)
        S, D = (200, 32)
        key = jax.random.key(seed)
        k1, k2, k3 = jax.random.split(key, 3)
        x = jax.random.normal(k1, (B, C, T), dtype=jnp.float32)
        conditions = jax.random.randint(k2, (B,), 0, S, dtype=jnp.int64)
        weights = jax.random.normal(k3, (S, C, D), dtype=jnp.float32) / jnp.sqrt(jnp.float32(C))
        return {'x': x, 'conditions': conditions, 'weights': weights}
    _L1_cond_all = _L1_cond_setup()
    _L1_cond_in = {k: v for k, v in _L1_cond_all.items() if k in ('weights',)}
    del _L1_cond_all

    def _L1_ffn_setup():
        import jax, jax.numpy as jnp
        import numpy as np
        ACT_BITS = 8
        HIDDEN = 256
        INTERMEDIATE = 512
        EPS = 1e-05

        def fwht(x):
            shape = x.shape
            n = shape[-1]
            x = x.reshape(-1, n)
            h = 1
            while h < n:
                x = x.reshape(-1, n // (2 * h), 2, h)
                a, b = (x[:, :, 0, :], x[:, :, 1, :])
                x = jnp.stack((a + b, a - b), axis=2).reshape(-1, n)
                h *= 2
            return (x * (1.0 / np.sqrt(n))).reshape(shape)

        def _ste(x, q):
            return x + jax.lax.stop_gradient(q - x)

        def act_quant(x, bits):
            qb = float(2 ** (bits - 1) - 1)
            scale = qb / jnp.clip(jnp.max(jnp.abs(x), axis=-1, keepdims=True), EPS, None)
            q = jnp.clip(jnp.round(x * scale), -qb, qb) / scale
            return _ste(x, q)

        def weight_quant(w):
            scale = jnp.clip(jnp.mean(jnp.abs(w)), EPS, None)
            q = jnp.clip(jnp.round(w / scale), -1.0, 1.0) * scale
            return _ste(w, q)

        def hbitlinear(x, w, bits):
            xq = act_quant(fwht(x), bits)
            wq = weight_quant(w)
            return jnp.einsum('bsd,fd->bsf', xq, wq)
        key = jax.random.key(seed)
        k1, k2, k3 = jax.random.split(key, 3)
        hidden_states = jax.random.normal(k1, (4, 512, HIDDEN), dtype=jnp.float32)
        w_up = jax.random.normal(k2, (INTERMEDIATE, HIDDEN), dtype=jnp.float32) * 0.02
        w_down = jax.random.normal(k3, (HIDDEN, INTERMEDIATE), dtype=jnp.float32) * 0.02
        return {'hidden_states': hidden_states, 'w_up': w_up, 'w_down': w_down}
    _L1_ffn_all = _L1_ffn_setup()
    _L1_ffn_in = {k: v for k, v in _L1_ffn_all.items() if k in ('w_up', 'w_down')}
    del _L1_ffn_all
    return {'x': x, 'itok_B_0_6': itok_B_0_6, 'itok_B_1_198': itok_B_1_198, 'L0_cond_W': _L0_cond_in['W'], 'L0_cond_A': _L0_cond_in['A'], 'L0_cond_Bm': _L0_cond_in['Bm'], 'L0_cond_scalings': _L0_cond_in['scalings'], 'L0_ffn_gate_w': _L0_ffn_in['gate_w'], 'L0_ffn_w1': _L0_ffn_in['w1'], 'L0_ffn_w2': _L0_ffn_in['w2'], 'L0_ffn_w3': _L0_ffn_in['w3'], 'L0_ffn_ws1': _L0_ffn_in['ws1'], 'L0_ffn_ws2': _L0_ffn_in['ws2'], 'L0_ffn_ws3': _L0_ffn_in['ws3'], 'L1_cond_weights': _L1_cond_in['weights'], 'L1_ffn_w_up': _L1_ffn_in['w_up'], 'L1_ffn_w_down': _L1_ffn_in['w_down']}

def reference(x, itok_B_0_6, itok_B_1_198, L0_cond_W, L0_cond_A, L0_cond_Bm, L0_cond_scalings, L0_ffn_gate_w, L0_ffn_w1, L0_ffn_w2, L0_ffn_w3, L0_ffn_ws1, L0_ffn_ws2, L0_ffn_ws3, L1_cond_weights, L1_ffn_w_up, L1_ffn_w_down):
    import jax
    import jax.numpy as jnp

    def _L0_cond_ref(x, W, A, Bm, scalings, adapter_idx):
        import jax, jax.numpy as jnp
        import numpy as np
        B, T, D_IN, D_OUT = (16, 256, 256, 256)
        N_ADAPTERS, RANK = (8, 16)
        H = jnp.einsum('btd,od->bto', x, W)
        A_b = A[adapter_idx]
        B_b = Bm[adapter_idx]
        s_b = scalings[adapter_idx]
        xa = jnp.einsum('btd,brd->btr', x, A_b)
        delta = jnp.einsum('btr,bor->bto', xa, B_b)
        delta = jax.lax.stop_gradient(delta * s_b[:, None, None])
        return H + delta

    def _L0_ffn_ref(x, gate_w, w1, w2, w3, ws1, ws2, ws3):
        import jax, jax.numpy as jnp
        import numpy as np
        TOP_K = 2
        NUM_EXPERTS = 8
        ROUTE_SCALE = 1.0
        bs, slen, dim = x.shape
        xf = x.reshape(-1, dim)
        logits = (xf @ gate_w.T).astype(jnp.float32)
        scores = jax.nn.sigmoid(logits)
        top_scores, sel_idx = jax.lax.top_k(scores, TOP_K)
        top_scores = top_scores * ROUTE_SCALE
        routed = jnp.zeros_like(xf)
        for k in range(TOP_K):
            xs = xf * top_scores[:, k][:, None]
            h1 = jnp.einsum('td,ehd->teh', xs, w1)
            h3 = jnp.einsum('td,ehd->teh', xs, w3)
            h = jax.nn.silu(h1) * h3
            onehot = jax.nn.one_hot(sel_idx[:, k], NUM_EXPERTS, dtype=h.dtype)
            routed = routed + jnp.einsum('teh,te,edh->td', h, onehot, w2)
        shared = jax.nn.silu(xf @ ws1.T) * (xf @ ws3.T) @ ws2.T
        out = (shared + routed).reshape(bs, slen, dim)
        return out

    def _L1_cond_ref(x, conditions, weights):
        import jax, jax.numpy as jnp
        import numpy as np
        B, C, T = (128, 32, 256)
        S, D = (200, 32)
        w = weights[conditions]
        return jnp.einsum('bct,bcd->bdt', x, w)

    def _L1_ffn_ref(hidden_states, w_up, w_down):
        import jax, jax.numpy as jnp
        import numpy as np
        ACT_BITS = 8
        HIDDEN = 256
        INTERMEDIATE = 512
        EPS = 1e-05

        def fwht(x):
            shape = x.shape
            n = shape[-1]
            x = x.reshape(-1, n)
            h = 1
            while h < n:
                x = x.reshape(-1, n // (2 * h), 2, h)
                a, b = (x[:, :, 0, :], x[:, :, 1, :])
                x = jnp.stack((a + b, a - b), axis=2).reshape(-1, n)
                h *= 2
            return (x * (1.0 / np.sqrt(n))).reshape(shape)

        def _ste(x, q):
            return x + jax.lax.stop_gradient(q - x)

        def act_quant(x, bits):
            qb = float(2 ** (bits - 1) - 1)
            scale = qb / jnp.clip(jnp.max(jnp.abs(x), axis=-1, keepdims=True), EPS, None)
            q = jnp.clip(jnp.round(x * scale), -qb, qb) / scale
            return _ste(x, q)

        def weight_quant(w):
            scale = jnp.clip(jnp.mean(jnp.abs(w)), EPS, None)
            q = jnp.clip(jnp.round(w / scale), -1.0, 1.0) * scale
            return _ste(w, q)

        def hbitlinear(x, w, bits):
            xq = act_quant(fwht(x), bits)
            wq = weight_quant(w)
            return jnp.einsum('bsd,fd->bsf', xq, wq)
        h = hbitlinear(hidden_states, w_up, ACT_BITS)
        h = jnp.square(jax.nn.relu(h))
        return hbitlinear(h, w_down, ACT_BITS)
    x = x + _L0_ffn_ref(_L0_cond_ref(x, L0_cond_W, L0_cond_A, L0_cond_Bm, L0_cond_scalings, itok_B_0_6), L0_ffn_gate_w, L0_ffn_w1, L0_ffn_w2, L0_ffn_w3, L0_ffn_ws1, L0_ffn_ws2, L0_ffn_ws3)
    x = x + _L1_ffn_ref(_L1_cond_ref(x, itok_B_1_198, L1_cond_weights), L1_ffn_w_up, L1_ffn_w_down)
    return x

_drawn_inputs = setup_inputs


def setup_inputs(seed=0):
    import zlib

    import numpy as np

    out = dict(_drawn_inputs(seed))
    spreads = {'L0_cond_scalings': (1.0, 0.2)}
    factors = {}
    for name, (base, spread) in spreads.items():
        noise = np.random.default_rng([zlib.crc32(name.encode()), seed]).standard_normal(out[name].shape)
        drawn = base * np.exp(spread * noise) if base else spread * noise
        out[name] = jnp.asarray(drawn.astype(out[name].dtype))
    for name, factor in factors.items():
        out[name] = (out[name] * factor).astype(out[name].dtype)
    return out
```

```python
from contextlib import ExitStack

import concourse.bass as bass
from concourse import mybir

F32 = mybir.dt.float32
F32R = mybir.dt.float32r
BF16 = mybir.dt.bfloat16
I32 = mybir.dt.int32
ALU = mybir.AluOpType
ACT = mybir.ActivationFunctionType
AX = mybir.AxisListType

P = 128
NT = 4096
TB = 512
NBLK = NT // TB
NE = 8
NS = NE + 1
D = 256
HID = 512
MAGIC = 12582912.0
EPS = 1e-5
SAT = 17.4
QB = 127.0

C_W, C_A, C_B, C_G, C_S1, C_S3 = 0, 512, 768, 1024, 1040, 1296
C_1, C_3, C_2, C_S2, C_END = 1552, 3600, 5648, 7696, 7952
PARTS = [(C_W, C_G), (C_G, C_1), (C_1, C_3), (C_3, C_2), (C_2, C_END)]


def adapter_moe_quant_ffn(nc, xT, x, adapter, cond, WT, AT, BmT, scal, gT, w1T, w3T, w2T, ws1T, ws3T, ws2T,
                          cw, wuT, wdT, consts, out):
    with ExitStack() as ctx:
        def sb(name, shape, dt=F32):
            return ctx.enter_context(nc.sbuf_tensor(name, shape, dt))

        def pb(name):
            return ctx.enter_context(nc.psum_tensor(name, [P, 512], F32))

        def sem(name):
            return ctx.enter_context(nc.semaphore(name))

        md = nc.dram_tensor("md", (NBLK, 4 * NE * P), F32, kind="Internal").ap()
        gd = nc.dram_tensor("gd", (P, 1024), F32, kind="Internal").ap()

        WH = sb("WH", [P, C_END], F32R)
        WL = sb("WL", [P, C_END], F32R)
        MBC = sb("MBC", [P, 8192])
        RAW = MBC[:, 0:C_END]
        CON = sb("CON", [P, 272])
        IDENT, HADF, W8, EIDX = CON[:, 0:128], CON[:, 128:256], CON[:, 256:264], CON[:, 264:265]
        IDB = sb("IDB", [P, P], BF16)
        HAD = sb("HAD", [P, P], F32R)
        HAD2 = sb("HAD2", [P, 2, 2, P], F32R)
        MAG = sb("MAG", [P, 1])
        ONES = sb("ONES", [P, P])
        IDXC = sb("IDXC", [P, 1], I32)
        SCAL = sb("SCAL", [P, 1])
        MASK = sb("MASK", [P, P])
        XR = sb("XR", [P, 2, TB])
        XH = sb("XH", [P, 2, TB], F32R)
        XL = sb("XL", [P, 2, TB], F32R)
        XA = sb("XA", [P, TB])
        IDXI = XA[:, 0:P].bitcast(I32)
        XAH = sb("XAH", [P, TB], F32R)
        XAL = sb("XAL", [P, TB], F32R)
        H0H = sb("H0H", [P, 2, 2, TB], F32R)
        H0L = sb("H0L", [P, 2, 2, TB], F32R)
        GS = sb("GS", [P, 12, 32])
        G4 = sb("G4", [P, 4, 4])
        GM = sb("GM", [P, 32])
        MT = sb("MT", [32, P])
        T = sb("T", [P, 3, TB])
        HH = sb("HH", [P, 3, TB], F32R)
        HL = sb("HL", [P, 3, TB], F32R)
        X1 = sb("X1", [P, 2, 4, D])
        BD = sb("BD", [P, 2, 4, P])
        P1H = sb("P1H", [P, 4, TB], F32R)
        P1L = sb("P1L", [P, 4, TB], F32R)
        R = sb("R", [P, 4, TB])
        U = sb("U", [P, 4, TB])
        QF = U[:, 0:2, :].rearrange("p a (b c) -> p (a b) c", b=2)
        GATH = R[:, 0:2, :].rearrange("p a b -> p (a b)")
        Q1T = sb("Q1T", [P, 2, TB], BF16)
        Q2 = sb("Q2", [P, 4, HID], BF16)
        Q1 = Q2[:, :, 0:D]
        Q2T = U[:, 0:2, :].rearrange("p a b -> p (a b)").bitcast(BF16).rearrange("p (c t) -> p c t", c=4)
        WU = sb("WU", [P, 2, HID], BF16)
        WD = sb("WD", [P, 4, D], BF16)
        ST = sb("ST", [P, 16, 4])
        SW = sb("SW", [P, 8])
        WUR = R[:, 2:4, :]
        WDR = U[:, 2:4, :].rearrange("p a (b c) -> p (a b) c", b=2)

        A1 = [pb(f"A1{i}") for i in range(2)]
        A3 = [pb(f"A3{i}") for i in range(2)]
        ACC = [pb(f"ACC{i}") for i in range(2)]
        AUX = [pb(f"AUX{i}") for i in range(2)]

        names = ("con idc idi scl cg gw xr md out wq "
                 "wh wl hadc had2 mag bdz mask "
                 "xh xl xa xam xah xal h0 h0h h0l gate glf gsil gch gm mt mtc "
                 "a1 a3 t1 sil t3 h hh hl acc x1 "
                 "y yh yl f st1 qf q1 q1t q1c up rl sq bf vh vl g st2 q2f q2 q2t q2c dn fin "
                 "wsum wtot sw wt").split()
        S = {n: sem("s_" + n) for n in names}
        s_raw = [sem(f"s_raw{i}") for i in range(len(PARTS))]
        s_x = [sem(f"p_x{i}") for i in range(2)]
        s_bd = [sem(f"p_bd{i}") for i in range(2)]
        s_mb = [sem(f"p_mb{i}") for i in range(2)]

        def parity(sems, b, per):
            return sems[b % 2], per * (b // 2 + 1)

        plan = {e: [] for e in ("sync", "gpsimd", "scalar", "vector", "tensor")}

        def at(engine, t, fn):
            plan[engine].append((t, len(plan[engine]), fn))

        EARLY = -1000

        def load_first(e):
            e.dma_start(XR[:, :, :], xT.rearrange("(k p) t -> p k t", p=P)[:, :, 0:TB]).then_inc(S["xr"], 16)
            for i, (c, w, n) in enumerate(((C_W, WT, 256), (C_A, AT, 128))):
                e.dma_start(RAW[:, c:c + 2 * n].rearrange("p (k n) -> p k n", k=2),
                            w.rearrange("(k p) n -> p k n", p=P)).then_inc(s_raw[0], 16)
            e.dma_start(RAW[:, C_B:C_G], BmT).then_inc(s_raw[0], 16)
            e.dma_start(IDXI, adapter.partition_broadcast(P)).then_inc(S["idi"], 16)
            e.dma_start(CON[:, :], consts).then_inc(S["con"], 16)
            for c, w, n in ((C_G, gT, 8), (C_S1, ws1T, 128), (C_S3, ws3T, 128)):
                e.dma_start(RAW[:, c:c + 2 * n].rearrange("p (k n) -> p k n", k=2),
                            w.rearrange("(k p) n -> p k n", p=P)).then_inc(s_raw[1], 16)
            for i, (c, w) in enumerate(((C_1, w1T), (C_3, w3T))):
                e.dma_start(RAW[:, c:c + 2048].rearrange("p (k n) -> p k n", k=2),
                            w.rearrange("(k p) n -> p k n", p=P)).then_inc(s_raw[2 + i], 16)
            e.dma_start(RAW[:, C_2:C_S2].rearrange("p (e n) -> p e n", e=NE),
                        w2T.rearrange("e p n -> p e n")).then_inc(s_raw[4], 16)
            e.dma_start(RAW[:, C_S2:C_END], ws2T).then_inc(s_raw[4], 16)
            e.dma_start(WUR, wuT.rearrange("(k p) n -> p k n", p=P)).then_inc(S["wq"], 16)
            e.dma_start(WDR, wdT.rearrange("(k p) n -> p k n", p=P)).then_inc(S["wq"], 16)

        RAW_IN = [48, 48, 16, 16, 32]

        at("sync", EARLY, load_first)

        def load_small(e):
            e.dma_start(IDXC[:, :], cond.rearrange("(p a) -> p a", a=1)).then_inc(S["idc"], 16)
            e.dma_start(SCAL[:, :], scal).then_inc(S["scl"], 16)
        at("scalar", EARLY, load_small)

        def gather(e):
            e.memset(BD[:, :, :, :], 0.0).then_inc(S["bdz"], 1)
            e.memset(ONES[:, :], 1.0).then_inc(S["mag"], 1)
            e.memset(MAG[:, :], MAGIC).then_inc(S["mag"], 1)
            e.wait_ge(S["idc"], 16)
            e.indirect_dma_start(GATH, None, cw, bass.IndirectOffsetOnAxis(ap=IDXC[:, 0:1], axis=0))\
             .then_inc(S["cg"], 16)
        at("gpsimd", EARLY, gather)

        def stash(e):
            e.wait_ge(S["cg"], 16)
            e.dma_start(gd, GATH).then_inc(S["gw"], 16)
        at("sync", -40, stash)

        def split_hi(e, i):
            a, b = PARTS[i]
            e.wait_ge(s_raw[i], RAW_IN[i])
            e.activation(WH[:, a:b], RAW[:, a:b], ACT.Copy).then_inc(S["wh"], 1)

        def split_lo(e, i):
            a, b = PARTS[i]
            e.wait_ge(S["wh"], i + 1)
            e.tensor_tensor(WL[:, a:b], RAW[:, a:b], WH[:, a:b].bitcast(F32), ALU.subtract).then_inc(S["wl"], 1)

        for i, t in enumerate((-25.0, -17.0, -14.8, -9.2, -8.6)):
            at("scalar", t, lambda e, i=i: split_hi(e, i))
            at("vector", t + 0.05, lambda e, i=i: split_lo(e, i))

        def make_mask(e):
            e.wait_ge(S["idi"], 16)
            e.wait_ge(S["con"], 16)
            e.wait_ge(S["scl"], 16)
            e.tensor_copy(MASK[:, :], IDXI).then_inc(S["mask"], 1)
            e.wait_ge(S["mask"], 1)
            e.tensor_scalar(MASK[:, :], MASK[:, :], EIDX, SCAL[:, 0:1], ALU.is_equal, ALU.mult).then_inc(S["mask"], 1)
            e.tensor_copy(IDB[:, :], IDENT).then_inc(S["hadc"], 1)
            e.tensor_copy(HAD[:, :], HADF).then_inc(S["hadc"], 1)
            for k in range(2):
                e.tensor_copy(HAD2[:, k, 0, :], HADF).then_inc(S["had2"], 1)
                e.tensor_scalar(HAD2[:, k, 1, :], HADF, 1.0 - 2 * k, None, ALU.mult).then_inc(S["had2"], 1)
        at("vector", -24.0, make_mask)

        def weight_sums(e):
            e.wait_ge(S["wq"], 32)
            e.tensor_reduce(SW[:, 0:1], WUR, AX.XY, ALU.add, apply_absolute_value=True).then_inc(S["wsum"], 1)
            e.tensor_reduce(SW[:, 1:2], WDR, AX.XY, ALU.add, apply_absolute_value=True).then_inc(S["wsum"], 1)
        at("vector", -3.0, weight_sums)

        def weight_total(e):
            e.wait_ge(S["wsum"], 2)
            e.wait_ge(S["mag"], 2)
            aux_free(e, 0, ("wtot",))
            e.matmul(AUX[0][:, 0:2], ONES[:, :], SW[:, 0:2], start=True, stop=True).then_inc(S["wtot"], 1)
        at("tensor", -1.0, weight_total)

        def ternary(e):
            e.wait_ge(S["wtot"], 1)
            e.tensor_scalar(SW[:, 2:4], AUX[0][:, 0:2], 1.0 / (D * HID), EPS, ALU.mult, ALU.max).then_inc(S["sw"], 1)
            e.wait_ge(S["sw"], 1)
            e.reciprocal(SW[:, 4:6], SW[:, 2:4]).then_inc(S["sw"], 1)
            e.wait_ge(S["sw"], 2)
            n = 0
            for raw, q, c in ((WUR, WU, 4), (WDR, WD, 5)):
                e.tensor_scalar(raw, raw, SW[:, c:c + 1], MAGIC, ALU.mult, ALU.add).then_inc(S["wt"], 1)
                e.wait_ge(S["wt"], n + 1)
                e.tensor_scalar(raw, raw, MAGIC, 1.0, ALU.subtract, ALU.min).then_inc(S["wt"], 1)
                e.wait_ge(S["wt"], n + 2)
                e.tensor_scalar(q[:, :, :], raw, -1.0, None, ALU.max).then_inc(S["wt"], 1)
                n += 3
        at("vector", -0.9, ternary)

        def plan_adapter(b):
            t0 = 18 * (b - 1)
            pr = b % 2
            h0h, h0l = H0H[:, pr, :, :], H0L[:, pr, :, :]

            if b > 0:
                def load(e):
                    e.wait_ge(S["xl"], b)
                    e.dma_start(XR[:, :, :], xT.rearrange("(k p) t -> p k t", p=P)[:, :, b * TB:(b + 1) * TB])\
                     .then_inc(S["xr"], 16)
                at("sync", t0 - 12, load)

            def x_hi(e):
                e.wait_ge(S["xr"], 16 * (b + 1))
                if b > 0:
                    e.wait_ge(S["h0"], 2 * b)
                e.activation(XH[:, :, :], XR[:, :, :], ACT.Copy).then_inc(S["xh"], 1)
            at("scalar", t0 - 6.6, x_hi)

            def x_lo(e):
                e.wait_ge(S["xh"], b + 1)
                e.tensor_tensor(XL[:, :, :], XR[:, :, :], XH[:, :, :].bitcast(F32), ALU.subtract).then_inc(S["xl"], 1)
            at("gpsimd" if b else "vector", t0 - 6.2, x_lo)

            def xa(e):
                e.wait_ge(S["xl"], b + 1)
                e.wait_ge(S["wl"], 1)
                if b > 0:
                    aux_free(e, 0, ("adapter", b))
                n = 0
                for k in range(2):
                    for w, xx in ((WH, XH), (WH, XL), (WL, XH)):
                        mm = e.matmul(AUX[0][:, :], w[:, C_A + k * P:C_A + (k + 1) * P], xx[:, k, :],
                                      start=(n == 0), stop=(n == 5))
                        n += 1
                mm.then_inc(S["xa"], 1)
            at("tensor", t0 - 3.5, xa)

            def xam(e):
                e.wait_ge(S["xa"], b + 1)
                if b == 0:
                    e.wait_ge(S["mask"], 2)
                if b > 0:
                    e.wait_ge(S["xal"], b)
                m = MASK[:, 16 * b:16 * b + 16].unsqueeze(2).broadcast_to([P, 16, 32])
                e.tensor_tensor(XA[:, :].rearrange("p (n t) -> p n t", t=32),
                                AUX[0][:, :].rearrange("p (n t) -> p n t", t=32), m, ALU.mult).then_inc(S["xam"], 1)
            at("vector", t0 - 3.2, xam)

            def xa_hi(e):
                e.wait_ge(S["xam"], b + 1)
                if b > 0:
                    e.wait_ge(S["h0"], 2 * b)
                e.activation(XAH[:, :], XA[:, :], ACT.Copy).then_inc(S["xah"], 1)
            at("scalar", t0 - 2.7, xa_hi)

            def xa_lo(e):
                e.wait_ge(S["xah"], b + 1)
                e.tensor_tensor(XAL[:, :], XA[:, :], XAH[:, :].bitcast(F32), ALU.subtract).then_inc(S["xal"], 1)
            at("gpsimd" if b else "vector", t0 - 2.2, xa_lo)

            def h0(e, o):
                e.wait_ge(S["xal"], b + 1)
                aux_free(e, o, ("h0", b))
                n = 0
                for k in range(2):
                    c = C_W + k * D + o * P
                    for w, xx in ((WH, XH), (WH, XL), (WL, XH)):
                        e.matmul(AUX[o][:, :], w[:, c:c + P], xx[:, k, :], start=(n == 0), stop=False)
                        n += 1
                c = C_B + o * P
                e.matmul(AUX[o][:, :], WH[:, c:c + P], XAH[:, :], start=False, stop=False)
                e.matmul(AUX[o][:, :], WH[:, c:c + P], XAL[:, :], start=False, stop=False)
                e.matmul(AUX[o][:, :], WL[:, c:c + P], XAH[:, :], start=False, stop=True).then_inc(S["h0"], 1)

            def h0_hi(e, o):
                e.wait_ge(S["h0"], 2 * b + o + 1)
                if b >= 2:
                    e.wait_ge(S["a3"], NS * (b - 1))
                e.activation(h0h[:, o, :], AUX[o][:, :], ACT.Copy).then_inc(S["h0h"], 1)

            def h0_lo(e, o):
                e.wait_ge(S["h0h"], 2 * b + o + 1)
                e.tensor_tensor(h0l[:, o, :], AUX[o][:, :], h0h[:, o, :].bitcast(F32), ALU.subtract)\
                 .then_inc(S["h0l"], 1)
            for o in range(2):
                at("tensor", t0 + 2.3 + o / 10, lambda e, o=o: h0(e, o))
                at("scalar", t0 + 2.6 + o / 10, lambda e, o=o: h0_hi(e, o))
                at("vector", t0 + 2.9 + o / 10, lambda e, o=o: h0_lo(e, o))

            def gate(e):
                e.wait_ge(S["h0l"], 2 * b + 2)
                e.wait_ge(S["wl"], 2)
                aux_free(e, 0, ("gate", b))
                for t in range(4):
                    n = 0
                    for k in range(2):
                        tok = slice(t * P, (t + 1) * P)
                        g = slice(C_G + k * 8, C_G + k * 8 + 8)
                        for hh, w in ((h0h, WH), (h0l, WH), (h0h, WL)):
                            mm = e.matmul(AUX[0][:, 8 * t:8 * t + 8], hh[:, k, tok], w[:, g],
                                          start=(n == 0), stop=(n == 5))
                            n += 1
                mm.then_inc(S["gate"], 1)
            at("tensor", t0 + 8, gate)

            def logits(e):
                e.wait_ge(S["gate"], b + 1)
                if b > 0:
                    e.wait_ge(S["gm"], b)
                e.tensor_scalar(GS[:, 0, :], AUX[0][:, 0:32], 0.0, 1e-30, ALU.is_equal, ALU.mult)\
                 .then_inc(S["glf"], 1)
                e.wait_ge(S["glf"], 2 * b + 1)
                e.tensor_tensor(GS[:, 1, :], AUX[0][:, 0:32], GS[:, 0, :], ALU.add).then_inc(S["glf"], 1)
            at("vector", t0 + 8.5, logits)

            def gate_silu(e):
                e.wait_ge(S["glf"], 2 * b + 2)
                e.activation(GS[:, 2, :], GS[:, 1, :], ACT.Silu).then_inc(S["gsil"], 1)
            at("scalar", t0 + 8.7, gate_silu)

            def top2(e):
                e.wait_ge(S["gsil"], b + 1)
                n = [16 * b]

                def link(ins):
                    n[0] += 1
                    ins.then_inc(S["gch"], 1)
                    e.wait_ge(S["gch"], n[0])

                def r(i):
                    return GS[:, i, :].rearrange("p (t e) -> p t e", e=NE)

                def c(i):
                    return G4[:, i, :].unsqueeze(2).broadcast_to([P, 4, NE])

                w8 = W8.unsqueeze(1).broadcast_to([P, 4, NE])
                link(e.reciprocal(GS[:, 4, :], GS[:, 1, :]))
                link(e.tensor_tensor(GS[:, 5, :], GS[:, 2, :], GS[:, 4, :], ALU.mult))
                link(e.tensor_scalar(GS[:, 6, :], GS[:, 1, :], SAT, None, ALU.is_ge))
                link(e.scalar_tensor_tensor(out=GS[:, 3, :], in0=GS[:, 5, :], scalar=1.0, in1=GS[:, 6, :],
                                            op0=ALU.min, op1=ALU.max))
                for j, sc, base in ((0, 3, 4), (1, 7, 8)):
                    link(e.tensor_reduce(G4[:, 2 * j, :], r(sc), AX.X, ALU.max))
                    link(e.tensor_tensor(r(base), r(sc), c(2 * j), ALU.is_equal))
                    link(e.tensor_tensor(r(base + 1), r(base), w8, ALU.mult))
                    link(e.tensor_reduce(G4[:, 2 * j + 1, :], r(base + 1), AX.X, ALU.max))
                    link(e.tensor_tensor(r(base + 2), r(base + 1), c(2 * j + 1), ALU.is_equal))
                    if j == 0:
                        link(e.scalar_tensor_tensor(out=GS[:, 7, :], in0=GS[:, 6, :], scalar=-4.0, in1=GS[:, 3, :],
                                                    op0=ALU.mult, op1=ALU.add))
                link(e.tensor_tensor(GS[:, 11, :], GS[:, 6, :], GS[:, 10, :], ALU.add))
                if b > 0:
                    e.wait_ge(S["mt"], b)
                e.tensor_tensor(GM[:, :], GS[:, 11, :], GS[:, 3, :], ALU.mult).then_inc(S["gm"], 1)
                assert n[0] == 16 * (b + 1)
            at("vector", t0 + 9, top2)

            def turn(e):
                e.wait_ge(S["gm"], b + 1)
                aux_free(e, 1, ("turn", b))
                e.transpose(AUX[1][0:32, 0:P], GM[:, :], IDENT).then_inc(S["mt"], 1)
            at("tensor", t0 + 11, turn)

            def turn_out(e):
                e.wait_ge(S["mt"], b + 1)
                if b > 0:
                    e.wait_ge(S["md"], 16 * b)
                e.activation(MT[:, :], AUX[1][0:32, 0:P], ACT.Copy).then_inc(S["mtc"], 1)
            at("scalar", t0 + 11.3, turn_out)

            def spread(e):
                e.wait_ge(S["mtc"], b + 1)
                e.dma_start(md[b].rearrange("(a t) -> a t", t=P), MT[:, :]).then_inc(S["md"], 16)
                e.wait_ge(S["md"], 16 * (b + 1))
                if b < 2:
                    e.wait_ge(S["wl"], 5)
                else:
                    e.wait_ge(S["h"], NE * (b - 1))
                e.dma_start(MBC[:, pr * 4096:(pr + 1) * 4096], md[b].partition_broadcast(P))\
                 .then_inc(s_mb[pr], 16)
            at("sync", t0 + 11.5, spread)

        def plan_experts(b):
            pr = b % 2
            h0h, h0l = H0H[:, pr, :, :], H0L[:, pr, :, :]
            mbc = MBC[:, pr * 4096:(pr + 1) * 4096].rearrange("p (t e n) -> p t e n", t=4, e=NE)

            def load(e):
                if b >= 2:
                    e.wait_ge(S["out"], 16 * (b - 1))
                sm, _ = parity(s_x, b, 16)
                e.dma_start(X1[:, pr, :, :], x[b * TB:(b + 1) * TB, :].rearrange("(t p) d -> p t d", p=P))\
                 .then_inc(sm, 16)
                sm, _ = parity(s_bd, b, 64)
                if b == 0:
                    e.wait_ge(S["gw"], 16)
                    e.wait_ge(S["bdz"], 1)
                if b >= 2:
                    e.wait_ge(S["y"], 2 * (b - 1))
                src = gd[16 * b:16 * b + 16, :].rearrange("(t j) (c d) -> j c t d", j=4, c=32)
                for j in range(4):
                    s32 = slice(32 * j, 32 * j + 32)
                    e.dma_start(BD[s32, pr, :, s32], src[j]).then_inc(sm, 16)
            at("sync", 18 * b + 8.5, load)

            for q in range(NS):
                s = NS * b + q
                t0 = 2 * s
                eb = s % 2
                rb = s % 3
                ex = q - 1
                if q == 0:
                    c1, c3, kc, c2 = C_S1, C_S3, P, C_S2
                else:
                    c1, c3, kc, c2 = C_1 + ex * P, C_3 + ex * P, 1024, C_2 + ex * D
                hidden = s - b
                routed = NE * b + ex

                def up(e, s=s, q=q, eb=eb, c1=c1, c3=c3, kc=kc):
                    if q == 0:
                        e.wait_ge(S["h0l"], 2 * b + 2)
                        if b == 0:
                            e.wait_ge(S["wl"], 2)
                    if q == 1 and b == 0:
                        e.wait_ge(S["wl"], 4)
                    if s >= 2:
                        e.wait_ge(S["t3"], s - 1)
                    for ps, c, done in ((A1[eb], c1, "a1"), (A3[eb], c3, "a3")):
                        n = 0
                        for k in range(2):
                            cc = c + k * kc
                            for w, hh in ((WH, h0h), (WH, h0l), (WL, h0h)):
                                mm = e.matmul(ps[:, :], w[:, cc:cc + P], hh[:, k, :], start=(n == 0), stop=(n == 5))
                                n += 1
                        mm.then_inc(S[done], 1)
                at("tensor", t0, up)

                tv = T[:, rb, :].rearrange("p (t n) -> p t n", t=4)
                if q > 0:
                    def scale1(e, s=s, q=q, eb=eb, tv=tv, ex=ex):
                        e.wait_ge(S["a1"], s + 1)
                        if q == 1:
                            sm, v = parity(s_mb, b, 16)
                            e.wait_ge(sm, v)
                        if s >= 3:
                            e.wait_ge(S["hl"], s - 2)
                        e.tensor_tensor(tv, A1[eb][:, :].rearrange("p (t n) -> p t n", t=4), mbc[:, :, ex, :],
                                        ALU.mult).then_inc(S["t1"], 1)
                    at("vector", t0 + 0.1, scale1)

                def silu(e, s=s, q=q, eb=eb, rb=rb, routed=routed):
                    if q > 0:
                        e.wait_ge(S["t1"], routed + 1)
                        e.activation(T[:, rb, :], T[:, rb, :], ACT.Silu).then_inc(S["sil"], 1)
                    else:
                        e.wait_ge(S["a1"], s + 1)
                        if s >= 3:
                            e.wait_ge(S["hl"], s - 2)
                        e.activation(T[:, rb, :], A1[eb][:, :], ACT.Silu).then_inc(S["sil"], 1)
                at("scalar", t0 + 0.2, silu)

                def times3(e, s=s, eb=eb, rb=rb):
                    e.wait_ge(S["a3"], s + 1)
                    e.wait_ge(S["sil"], s + 1)
                    e.tensor_tensor(T[:, rb, :], A3[eb][:, :], T[:, rb, :], ALU.mult).then_inc(S["t3"], 1)
                at("vector", t0 + 0.8, times3)

                if q > 0:
                    def scale3(e, s=s, tv=tv, ex=ex):
                        e.wait_ge(S["t3"], s + 1)
                        e.tensor_tensor(tv, tv, mbc[:, :, ex, :], ALU.mult).then_inc(S["h"], 1)
                    at("gpsimd", t0 + 1, scale3)

                def h_hi(e, s=s, q=q, rb=rb, routed=routed):
                    if q > 0:
                        e.wait_ge(S["h"], routed + 1)
                    else:
                        e.wait_ge(S["t3"], s + 1)
                    if s >= 3:
                        e.wait_ge(S["acc"], s - 2)
                    e.activation(HH[:, rb, :], T[:, rb, :], ACT.Copy).then_inc(S["hh"], 1)
                at("scalar", t0 + 1.5, h_hi)

                def h_lo(e, s=s, rb=rb):
                    e.wait_ge(S["hh"], s + 1)
                    e.tensor_tensor(HL[:, rb, :], T[:, rb, :], HH[:, rb, :].bitcast(F32), ALU.subtract)\
                     .then_inc(S["hl"], 1)
                at("gpsimd", t0 + 2, h_lo)

                def down(e, s=s, q=q, rb=rb, c2=c2):
                    e.wait_ge(S["hl"], s + 1)
                    if s == 0:
                        e.wait_ge(S["wl"], 5)
                    for t in range(4):
                        if q == 0 and b > 0 and t % 2 == 0:
                            e.wait_ge(S["x1"], 2 * (b - 1) + t // 2 + 1)
                        tok = slice(t * P, (t + 1) * P)
                        dst = ACC[t // 2][:, (t % 2) * D:(t % 2 + 1) * D]
                        for n, (hh, w) in enumerate(((HH, WH), (HL, WH), (HH, WL))):
                            mm = e.matmul(dst, hh[:, rb, tok], w[:, c2:c2 + D],
                                          start=(q == 0 and n == 0 and t % 2 == 0),
                                          stop=(q == NS - 1 and n == 2), skip_group_check=True)
                    mm.then_inc(S["acc"], 1)
                at("tensor", t0 + 5, down)

            def residual(e, j):
                e.wait_ge(S["acc"], NS * (b + 1))
                sm, v = parity(s_x, b, 16)
                e.wait_ge(sm, v)
                v = X1[:, pr, 2 * j:2 * j + 2, :].rearrange("p t d -> p (t d)")
                e.tensor_tensor(v, ACC[j][:, :], v, ALU.add).then_inc(S["x1"], 1)
            for j in range(2):
                at("vector", 18 * b + 21.5 + j / 10, lambda e, j=j: residual(e, j))

        def plan_layer2(b):
            t0 = 18 * b + 18
            pr = b % 2
            x1 = X1[:, pr, :, :]

            def st(i):
                return ST[:, i, :]

            def mix(e, k):
                if k == 0:
                    e.wait_ge(S["x1"], 2 * b + 2)
                    sm, v = parity(s_bd, b, 64)
                    e.wait_ge(sm, v)
                aux_free(e, k, ("mix", b))
                for t in range(4):
                    mm = e.matmul(AUX[k][:, t * P:(t + 1) * P], x1[:, t, k * P:(k + 1) * P], BD[:, pr, t, :],
                                  start=True, stop=True)
                mm.then_inc(S["y"], 1)

            def y_hi(e, k):
                e.wait_ge(S["y"], 2 * b + k + 1)
                if b > 0:
                    e.wait_ge(S["g"], 4 * b)
                e.activation(P1H[:, k, :], AUX[k][:, :], ACT.Copy).then_inc(S["yh"], 1)

            def y_lo(e, k):
                e.wait_ge(S["yh"], 2 * b + k + 1)
                e.tensor_tensor(P1L[:, k, :], AUX[k][:, :], P1H[:, k, :].bitcast(F32), ALU.subtract)\
                 .then_inc(S["yl"], 1)
            for k in range(2):
                at("tensor", t0 + 4 + k / 10, lambda e, k=k: mix(e, k))
                at("scalar", t0 + 4.5 + k / 10, lambda e, k=k: y_hi(e, k))
                at("vector", t0 + 5 + k / 10, lambda e, k=k: y_lo(e, k))

            def had1(e, j):
                e.wait_ge(S["yl"], 2 * b + 2)
                if b == 0:
                    e.wait_ge(S["had2"], 4)
                aux_free(e, j, ("had1", b))
                for t in (2 * j, 2 * j + 1):
                    tok = slice(t * P, (t + 1) * P)
                    n = 0
                    for k in range(2):
                        for src in (P1H, P1L):
                            mm = e.matmul(AUX[j][:, (t % 2) * D:(t % 2 + 1) * D], src[:, k, tok],
                                          HAD2[:, k, :, :].rearrange("p a n -> p (a n)"),
                                          start=(n == 0), stop=(n == 3))
                            n += 1
                mm.then_inc(S["f"], 1)

            def stats1(e):
                k = 8 * b
                for j in range(2):
                    e.wait_ge(S["f"], 2 * b + j + 1)
                    if j == 0 and b > 0:
                        e.wait_ge(S["fin"], 4 * b)
                    e.tensor_reduce(ST[:, 0, 2 * j:2 * j + 2], AUX[j][:, :].rearrange("p (t d) -> p t d", t=2),
                                    AX.X, ALU.max, apply_absolute_value=True).then_inc(S["st1"], 1)
                e.wait_ge(S["st1"], k + 2)
                e.tensor_scalar(st(1), st(0), 1.0 / 16, EPS, ALU.mult, ALU.max).then_inc(S["st1"], 1)
                e.wait_ge(S["st1"], k + 3)
                e.reciprocal(st(2), st(1)).then_inc(S["st1"], 1)
                e.wait_ge(S["st1"], k + 4)
                e.tensor_scalar(st(3), st(2), QB, 1.0 / 16, ALU.mult, ALU.mult).then_inc(S["st1"], 1)
                if b == 0:
                    e.wait_ge(S["sw"], 1)
                e.tensor_scalar(st(4), st(1), 1.0 / QB, SW[:, 2:3], ALU.mult, ALU.mult).then_inc(S["st1"], 1)
                e.wait_ge(S["st1"], k + 6)
                e.tensor_tensor(st(5), st(4), st(4), ALU.mult).then_inc(S["st1"], 1)
                e.wait_ge(S["st1"], k + 7)
                e.tensor_scalar(st(6), st(5), float(HID) ** -0.5, None, ALU.mult).then_inc(S["st1"], 1)

            def round1(e, t):
                e.wait_ge(S["st1"], 8 * b + 5)
                if t == 0 and b > 0:
                    e.wait_ge(S["dn"], 2 * b)
                if t == 0 and b == 0:
                    e.wait_ge(S["mag"], 2)
                e.activation(QF[:, t, :], AUX[t // 2][:, (t % 2) * D:(t % 2 + 1) * D], ACT.Identity,
                             bias=MAG[:, 0:1], scale=st(3)[:, t:t + 1]).then_inc(S["qf"], 1)

            def quant1(e):
                e.wait_ge(S["qf"], 4 * b + 4)
                if b > 0:
                    e.wait_ge(S["q2t"], 2 * b)
                e.tensor_scalar(Q1, QF, MAGIC, None, ALU.subtract).then_inc(S["q1"], 1)
            for j in range(2):
                at("tensor", t0 + 6.5 + j / 10, lambda e, j=j: had1(e, j))
            at("vector", t0 + 7, stats1)
            for t in range(4):
                at("scalar", t0 + 7.5 + t / 10, lambda e, t=t: round1(e, t))
            at("vector", t0 + 8.5, quant1)

            bank0 = AUX[0][:, :].bitcast(BF16).rearrange("p (k t) -> p k t", k=2)

            def turn1(e):
                e.wait_ge(S["q1"], b + 1)
                if b == 0:
                    e.wait_ge(S["hadc"], 1)
                aux_free(e, 0, ("turn1", b))
                for t in range(4):
                    for k in range(2):
                        mm = e.transpose(bank0[:, k, t * P:(t + 1) * P], Q1[:, t, k * P:(k + 1) * P], IDB[:, :])
                mm.then_inc(S["q1t"], 1)
            at("tensor", t0 + 9.5, turn1)

            def turn1_out(e):
                e.wait_ge(S["q1t"], b + 1)
                if b > 0:
                    e.wait_ge(S["up"], 4 * b)
                e.activation(Q1T[:, :, :], bank0, ACT.Copy).then_inc(S["q1c"], 1)
            at("scalar", t0 + 10, turn1_out)

            def wide(e, c):
                if c == 0:
                    e.wait_ge(S["q1c"], b + 1)
                    if b == 0:
                        e.wait_ge(S["wt"], 6)
                aux_free(e, c % 2, ("wide", b, c))
                for k in range(2):
                    mm = e.matmul(AUX[c % 2][:, :], WU[:, k, c * P:(c + 1) * P], Q1T[:, k, :],
                                  start=(k == 0), stop=(k == 1))
                mm.then_inc(S["up"], 1)

            def relu(e, c):
                e.wait_ge(S["up"], 4 * b + c + 1)
                if c == 0 and b > 0:
                    e.wait_ge(S["vl"], 2 * b)
                if c == 0 and b == 0:
                    e.wait_ge(S["gw"], 16)
                    e.wait_ge(S["wt"], 6)
                e.activation(R[:, c, :], AUX[c % 2][:, :], ACT.Relu).then_inc(S["rl"], 1)

            def square(e, c):
                e.wait_ge(S["rl"], 4 * b + c + 1)
                e.tensor_tensor(R[:, c, :], R[:, c, :], R[:, c, :], ALU.mult).then_inc(S["sq"], 1)
            for c in range(4):
                t = t0 + 11.5 + c // 2 + (c % 2) / 10
                at("tensor", t, lambda e, c=c: wide(e, c))
                at("scalar", t + 0.3, lambda e, c=c: relu(e, c))
                at("vector", t + 0.9, lambda e, c=c: square(e, c))

            def stages(e):
                k = 4 * b
                e.wait_ge(S["sq"], 4 * b + 4)
                e.wait_ge(S["q1"], b + 1)
                e.tensor_tensor(U[:, 0::2, :], R[:, 0::2, :], R[:, 1::2, :], ALU.add).then_inc(S["bf"], 1)
                e.tensor_tensor(U[:, 1::2, :], R[:, 0::2, :], R[:, 1::2, :], ALU.subtract).then_inc(S["bf"], 1)
                e.wait_ge(S["bf"], k + 2)
                e.tensor_tensor(R[:, 0:2, :], U[:, 0:2, :], U[:, 2:4, :], ALU.add).then_inc(S["bf"], 1)
                e.tensor_tensor(R[:, 2:4, :], U[:, 0:2, :], U[:, 2:4, :], ALU.subtract).then_inc(S["bf"], 1)
            at("vector", t0 + 14, stages)

            def v_hi(e, j):
                e.wait_ge(S["bf"], 4 * b + 3 + j)
                e.wait_ge(S["f"], 2 * b + 2)
                e.activation(P1H[:, 2 * j:2 * j + 2, :], R[:, 2 * j:2 * j + 2, :], ACT.Copy).then_inc(S["vh"], 1)

            def v_lo(e, j):
                e.wait_ge(S["vh"], 2 * b + j + 1)
                e.tensor_tensor(P1L[:, 2 * j:2 * j + 2, :], R[:, 2 * j:2 * j + 2, :],
                                P1H[:, 2 * j:2 * j + 2, :].bitcast(F32), ALU.subtract).then_inc(S["vl"], 1)
            for j in range(2):
                at("scalar", t0 + 15.5 + j / 2, lambda e, j=j: v_hi(e, j))
                at("gpsimd", t0 + 16 + j / 2, lambda e, j=j: v_lo(e, j))

            def had2(e, t):
                e.wait_ge(S["vl"], 2 * b + 2)
                if b == 0:
                    e.wait_ge(S["hadc"], 2)
                aux_free(e, t % 2, ("had2", b, t))
                tok = slice(t * P, (t + 1) * P)
                for c in range(4):
                    for n, src in enumerate((P1H, P1L)):
                        mm = e.matmul(AUX[t % 2][:, c * P:(c + 1) * P], src[:, c, tok], HAD[:, :],
                                      start=(n == 0), stop=(n == 1))
                mm.then_inc(S["g"], 1)

            def stats2(e, j):
                k = 12 * b + 6 * j
                w = slice(2 * j, 2 * j + 2)
                for t in (2 * j, 2 * j + 1):
                    e.wait_ge(S["g"], 4 * b + t + 1)
                    e.tensor_reduce(ST[:, 7, t:t + 1], AUX[t % 2][:, :], AX.X, ALU.max,
                                    apply_absolute_value=True).then_inc(S["st2"], 1)
                e.wait_ge(S["st2"], k + 2)
                e.wait_ge(S["st1"], 8 * b + 8)
                e.tensor_tensor(st(8)[:, w], st(7)[:, w], st(6)[:, w], ALU.mult).then_inc(S["st2"], 1)
                e.wait_ge(S["st2"], k + 3)
                e.tensor_scalar(st(9)[:, w], st(8)[:, w], EPS, 1.0 / QB, ALU.max, ALU.mult).then_inc(S["st2"], 1)
                e.wait_ge(S["st2"], k + 4)
                e.reciprocal(st(10)[:, w], st(9)[:, w]).then_inc(S["st2"], 1)
                e.wait_ge(S["st2"], k + 5)
                e.tensor_tensor(st(11)[:, w], st(10)[:, w], st(6)[:, w], ALU.mult).then_inc(S["st2"], 1)

            def round2(e, t):
                e.wait_ge(S["st2"], 12 * b + 6 * (t // 2) + 6)
                if t == 0:
                    e.wait_ge(S["bf"], 4 * b + 4)
                e.activation(U[:, t, :], AUX[t % 2][:, :], ACT.Identity, bias=MAG[:, 0:1],
                             scale=st(11)[:, t:t + 1]).then_inc(S["q2f"], 1)

            def quant2(e, j):
                e.wait_ge(S["q2f"], 4 * b + 2 * j + 2)
                e.tensor_scalar(Q2[:, 2 * j:2 * j + 2, :], U[:, 2 * j:2 * j + 2, :], MAGIC, None, ALU.subtract)\
                 .then_inc(S["q2"], 1)
            for t in range(4):
                at("tensor", t0 + 17.5 + t // 2 * 1.5 + t % 2 / 10, lambda e, t=t: had2(e, t))
                at("scalar", t0 + 18.2 + t // 2 * 1.5 + t % 2 / 10, lambda e, t=t: round2(e, t))
            for j in range(2):
                at("vector", t0 + 17.9 + j * 1.5, lambda e, j=j: stats2(e, j))
                at("vector", t0 + 18.9 + j * 1.5, lambda e, j=j: quant2(e, j))

            def turn2(e, j):
                e.wait_ge(S["q2"], 2 * b + 2)
                aux_free(e, j, ("turn2", b))
                bank = AUX[j][:, :].bitcast(BF16).rearrange("p (k t) -> p k t", k=2)
                for t in range(4):
                    for k in range(2):
                        c = 2 * j + k
                        mm = e.transpose(bank[:, k, t * P:(t + 1) * P], Q2[:, t, c * P:(c + 1) * P], IDB[:, :])
                mm.then_inc(S["q2t"], 1)

            def turn2_out(e, j):
                e.wait_ge(S["q2t"], 2 * b + j + 1)
                bank = AUX[j][:, :].bitcast(BF16).rearrange("p (k t) -> p k t", k=2)
                e.activation(Q2T[:, 2 * j:2 * j + 2, :], bank, ACT.Copy).then_inc(S["q2c"], 1)

            def narrow(e, j):
                e.wait_ge(S["q2c"], 2 * b + 2)
                aux_free(e, j, ("narrow", b))
                for t in (2 * j, 2 * j + 1):
                    for c in range(4):
                        mm = e.matmul(AUX[j][:, (t % 2) * D:(t % 2 + 1) * D], Q2T[:, c, t * P:(t + 1) * P],
                                      WD[:, c, :], start=(c == 0), stop=(c == 3))
                mm.then_inc(S["dn"], 1)

            def finish(e):
                e.wait_ge(S["st2"], 12 * b + 12)
                e.tensor_scalar(st(12), st(9), SW[:, 3:4], None, ALU.mult).then_inc(S["sw"], 1)
                e.wait_ge(S["sw"], b + 3)
                for t in range(4):
                    if t % 2 == 0:
                        e.wait_ge(S["dn"], 2 * b + t // 2 + 1)
                    e.scalar_tensor_tensor(out=x1[:, t, :], in0=AUX[t // 2][:, (t % 2) * D:(t % 2 + 1) * D],
                                           scalar=st(12)[:, t:t + 1], in1=x1[:, t, :],
                                           op0=ALU.mult, op1=ALU.add).then_inc(S["fin"], 1)
            for j in range(2):
                at("tensor", t0 + 21.5 + j / 10, lambda e, j=j: turn2(e, j))
                at("scalar", t0 + 21.8 + j / 10, lambda e, j=j: turn2_out(e, j))
                at("tensor", t0 + 23.2 + j / 10, lambda e, j=j: narrow(e, j))
            at("vector", t0 + 23.6, finish)

            def store(e):
                e.wait_ge(S["fin"], 4 * b + 4)
                e.dma_start(out[b * TB:(b + 1) * TB, :].rearrange("(t p) d -> p t d", p=P), x1)\
                 .then_inc(S["out"], 16)
            at("sync", t0 + 24, store)

        last_reader = {}

        def uses():
            out = [[], []]
            for b in range(NBLK):
                t0 = 18 * (b - 1)
                out[0].append((t0 - 3.5, ("adapter", b), "xam", b + 1))
                for o in range(2):
                    out[o].append((t0 + 2.3 + o / 10, ("h0", b), "h0l", 2 * b + o + 1))
                out[0].append((t0 + 8, ("gate", b), "glf", 2 * b + 2))
                out[1].append((t0 + 11, ("turn", b), "mtc", b + 1))
                t0 = 18 * b + 18
                for k in range(2):
                    out[k].append((t0 + 4 + k / 10, ("mix", b), "yl", 2 * b + k + 1))
                    out[k].append((t0 + 6.5 + k / 10, ("had1", b), "qf", 4 * b + 2 * k + 2))
                out[0].append((t0 + 9.5, ("turn1", b), "q1c", b + 1))
                for c in range(4):
                    out[c % 2].append((t0 + 11.5 + c // 2 + (c % 2) / 10, ("wide", b, c), "rl", 4 * b + c + 1))
                    out[c % 2].append((t0 + 17.5 + c // 2 * 1.5 + c % 2 / 10, ("had2", b, c), "q2f", 4 * b + c + 1))
                for k in range(2):
                    out[k].append((t0 + 21.5 + k / 10, ("turn2", b), "q2c", 2 * b + k + 1))
                    out[k].append((t0 + 23.2 + k / 10, ("narrow", b), "fin", 4 * b + 2 * k + 2))
            out[0].append((-1.0, ("wtot",), "sw", 1))
            return out

        for bank, lst in enumerate(uses()):
            lst.sort()
            for prev, this in zip(lst, lst[1:]):
                last_reader[(bank, this[1])] = prev[2:]

        def aux_free(e, bank, use):
            got = last_reader.get((bank, use))
            if got:
                e.wait_ge(S[got[0]], got[1])

        for b in range(NBLK):
            plan_adapter(b)
            plan_experts(b)
            plan_layer2(b)

        def last(e):
            e.wait_ge(S["out"], 16 * NBLK)
        at("sync", 10000, last)

        block = ctx.enter_context(nc.Block())

        def run(engine, e):
            for _, _, fn in sorted(plan[engine], key=lambda v: v[:2]):
                fn(e)

        @block.sync
        def _(e):
            run("sync", e)

        @block.gpsimd
        def _(e):
            run("gpsimd", e)

        @block.scalar
        def _(e):
            run("scalar", e)

        @block.vector
        def _(e):
            run("vector", e)

        @block.tensor
        def _(e):
            run("tensor", e)


def kernel(x, itok_B_0_6, itok_B_1_198, L0_cond_W, L0_cond_A, L0_cond_Bm, L0_cond_scalings, L0_ffn_gate_w,
           L0_ffn_w1, L0_ffn_w2, L0_ffn_w3, L0_ffn_ws1, L0_ffn_ws2, L0_ffn_ws3, L1_cond_weights,
           L1_ffn_w_up, L1_ffn_w_down):
    import numpy as np
    import concourse.bacc as bacc
    from concourse import mybir as mb
    from concourse.bass_utils import run_bass_kernel_spmd

    consts = np.zeros((128, 272), np.float32)
    consts[:, 0:128] = np.eye(128)
    had = np.ones((1, 1), np.float32)
    while had.shape[0] < 128:
        had = np.block([[had, had], [had, -had]])
    consts[:, 128:256] = had
    consts[:, 256:264] = 8 - np.arange(8)
    consts[:, 264] = np.arange(128) // 16

    x2 = np.asarray(x).reshape(4096, 256)
    ins = [
        ("xT", x2.T), ("x", x2),
        ("adapter", np.asarray(itok_B_0_6)), ("cond", np.asarray(itok_B_1_198)),
        ("WT", np.asarray(L0_cond_W).T), ("AT", np.asarray(L0_cond_A).reshape(128, 256).T),
        ("BmT", np.asarray(L0_cond_Bm).transpose(0, 2, 1).reshape(128, 256)),
        ("scal", np.repeat(np.asarray(L0_cond_scalings), 16).reshape(128, 1)),
        ("gT", np.asarray(L0_ffn_gate_w).T),
        ("w1T", np.asarray(L0_ffn_w1).reshape(1024, 256).T), ("w3T", np.asarray(L0_ffn_w3).reshape(1024, 256).T),
        ("w2T", np.asarray(L0_ffn_w2).transpose(0, 2, 1)),
        ("ws1T", np.asarray(L0_ffn_ws1).T), ("ws3T", np.asarray(L0_ffn_ws3).T), ("ws2T", np.asarray(L0_ffn_ws2).T),
        ("cw", np.asarray(L1_cond_weights).reshape(200, 1024)),
        ("wuT", np.asarray(L1_ffn_w_up).T), ("wdT", np.asarray(L1_ffn_w_down).T),
        ("consts", consts),
    ]
    nc = bacc.Bacc("TRN2", target_bir_lowering=False, num_devices=1)
    arrays, args = {}, []
    for name, a in ins:
        a = np.ascontiguousarray(a)
        arrays["in_" + name] = a
        args.append(nc.dram_tensor("in_" + name, a.shape, mb.dt.from_np(a.dtype), kind="ExternalInput").ap())
    out = nc.dram_tensor("out_0", (4096, 256), mb.dt.float32, kind="ExternalOutput").ap()
    adapter_moe_quant_ffn(nc, *args, out)
    r = run_bass_kernel_spmd(nc, [arrays], core_ids=[0])
    return r.results[0]["out_0"].reshape(128, 32, 256)
```

```python
from contextlib import ExitStack

import concourse.bass as bass
from concourse import mybir

F32 = mybir.dt.float32
F32R = mybir.dt.float32r
BF16 = mybir.dt.bfloat16
I32 = mybir.dt.int32
ALU = mybir.AluOpType
ACT = mybir.ActivationFunctionType
AX = mybir.AxisListType

P = 128
NT = 4096
TB = 512
NBLK = NT // TB
NSB = 2
BPS = NBLK // NSB
TPS = 4 * BPS
NE = 8
STILES = 2 * TPS + NE - 1
SPAIRS = (STILES + 1) // 2
NSH = 2 * NBLK
NST = NSH + NSB * SPAIRS
D = 256
HID = 512
MAGIC = 12582912.0
EPS = 1e-5
SAT = 17.4
QB = 127.0

C_W, C_A, C_B, C_G, C_S, C_E = 0, 512, 768, 1024, 1040, 1808
EW = 768
C_END = C_E + NE * EW

TIME = {
    "load_expert": [6.40, 6.46, 23.49, 23.55, 31.17, 31.23, 31.29, 34.57],
    "load_wq": [41.26],
    "stash": [12.10],
    "split_hi": [5.74, 8.53, 22.22, 23.54, 30.19, 31.40, 36.58, 37.72, 40.81, 42.09],
    "split_lo": [6.85, 9.45, 23.95, 24.82, 33.60, 35.25, 37.48, 38.69, 43.75, 45.40],
    "gate_weights": [10.51],
    "make_mask": [8.66],
    "make_identity": [7.99],
    "weight_sums": [46.99],
    "weight_total": [57.14],
    "ternary": [57.91],
    "clear_bd": [98.40],
    "load_x": [0.30, 0.36, 0.42, 0.48, 46.63, 46.69, 46.75, 46.81],
    "x_hi": [3.99, 21.07, 28.76, 38.91, 49.53, 67.36, 85.51, 95.30],
    "x_lo": [5.11, 22.19, 29.88, 40.03, 50.65, 73.92, 87.41, 97.11],
    "xa": [8.19, 24.59, 31.53, 41.68, 55.13, 77.70, 88.91, 102.00],
    "xam": [10.95, 26.12, 33.00, 43.15, 56.60, 82.44, 92.24, 103.47],
    "xa_hi": [11.73, 26.90, 33.78, 43.93, 57.38, 83.22, 93.02, 104.90],
    "xa_lo": [12.43, 27.59, 34.47, 44.62, 64.31, 86.81, 95.84, 105.72],
    "h0w": [
        10.78, 14.44, 25.99, 27.28, 36.13, 37.43, 45.81, 48.05, 63.88, 65.88, 82.21, 84.03, 91.41, 93.64, 110.16,
        114.46],
    "h0": [
        13.58, 15.94, 28.58, 29.94, 38.73, 39.38, 52.18, 52.83, 67.18, 67.83, 87.61, 88.26, 96.64, 99.46, 120.11,
        121.00],
    "h0_hi": [
        14.62, 16.77, 29.71, 30.92, 39.86, 40.34, 53.01, 53.93, 68.31, 68.79, 88.44, 89.09, 97.47, 100.29, 124.79,
        126.93],
    "h0_lo": [
        15.27, 17.42, 31.01, 31.62, 41.16, 41.76, 53.66, 55.29, 72.05, 72.65, 90.61, 92.84, 98.25, 100.94, 125.44,
        127.75],
    "gate": [19.64, 32.83, 42.98, 58.21, 74.39, 100.11, 106.37, 128.55],
    "logits_lo": [25.28, 34.90, 45.05, 60.28, 79.68, 102.18, 108.44, 130.61],
    "logits": [25.68, 35.15, 45.29, 63.02, 81.31, 102.43, 108.69, 130.86],
    "tok": [
        21.53, 30.59, 40.03, 44.87, 47.11, 54.19, 57.27, 62.93, 73.45, 78.99, 95.46, 98.00, 103.30, 105.43, 140.14,
        143.44],
    "tok_out": [
        22.96, 32.13, 41.55, 45.99, 48.23, 55.31, 58.39, 64.18, 74.57, 80.12, 96.59, 99.12, 104.42, 106.55, 142.21,
        144.57],
    "hd_put": [32.71, 46.57, 55.89, 64.76, 80.70, 99.70, 107.13, 145.14],
    "s_up": [
        18.22, 23.18, 34.72, 49.35, 50.77, 60.10, 61.52, 68.48, 76.28, 79.94, 118.22, 122.93, 154.28, 159.35,
        184.11, 186.71],
    "s_silu": [
        19.82, 24.77, 36.31, 50.95, 52.60, 61.70, 63.51, 70.07, 77.88, 81.53, 119.81, 124.53, 155.88, 160.95,
        185.70, 188.31],
    "s_times3": [
        20.25, 25.79, 36.75, 51.78, 53.11, 62.69, 73.25, 73.58, 94.48, 96.78, 120.25, 124.96, 156.31, 161.39,
        186.14, 188.74],
    "s_h_hi": [
        20.77, 26.30, 37.31, 52.30, 53.62, 63.20, 73.76, 74.10, 94.99, 97.95, 121.45, 125.48, 157.79, 161.90,
        187.37, 189.26],
    "s_h_lo": [
        21.24, 26.78, 38.35, 52.77, 54.96, 63.97, 80.97, 83.64, 96.44, 99.85, 121.95, 126.04, 158.97, 162.38,
        188.14, 189.73],
    "s_down": [
        22.47, 29.23, 40.97, 53.48, 56.43, 65.17, 81.51, 85.33, 97.29, 104.24, 130.43, 132.80, 163.60, 165.97,
        189.78, 193.33],
    "s_out": [
        23.35, 32.22, 42.36, 54.36, 57.31, 71.44, 83.04, 86.21, 98.85, 105.12, 131.81, 138.95, 164.48, 166.84,
        190.92, 194.39],
    "load_xT": [6.34, 23.43, 31.11, 41.38, 51.88, 75.15, 88.65],
    "nonzero": [63.30, 131.13],
    "gate_silu": [63.98, 131.82],
    "top2": [64.91, 132.41],
    "rank": [71.47, 138.98],
    "place": [75.05, 141.01],
    "hot_lane": [
        79.65, 81.32, 84.18, 86.71, 88.38, 90.88, 92.55, 94.23, 147.80, 151.56, 158.41, 162.16, 169.62, 173.38,
        177.14, 180.89],
    "hot": [
        81.41, 83.98, 85.01, 88.55, 89.58, 91.21, 93.44, 94.81, 149.36, 151.00, 157.94, 159.31, 168.08, 170.24,
        174.76, 180.38],
    "sum": [
        83.51, 86.04, 86.56, 90.21, 90.81, 92.75, 94.94, 98.94, 157.13, 157.65, 167.39, 168.62, 172.33, 178.53,
        181.64, 183.59],
    "slot_out": [99.63, 184.28],
    "load_slots": [
        100.00, 102.08, 105.58, 110.31, 114.61, 120.26, 122.37, 126.39, 128.58, 134.14, 145.72, 149.48, 153.23,
        156.33, 160.08, 167.54, 171.30, 175.06, 178.81, 183.50, 186.86, 189.93, 192.78, 195.29, 198.78, 201.03,
        204.14, 213.54, 217.70, 219.78, 224.98, 228.43, 236.55, 240.71, 243.83, 246.95, 252.15, 259.99, 264.33,
        268.53],
    "xt": [
        104.95, 109.68, 113.98, 119.63, 121.74, 125.76, 127.95, 133.51, 145.09, 148.59, 151.44, 155.70, 158.87,
        166.91, 170.19, 172.85, 178.05, 182.87, 186.23, 189.54, 192.15, 194.66, 198.15, 200.40, 203.51, 206.35,
        209.19, 218.58, 223.55, 225.81, 230.99, 235.38, 241.85, 245.45, 251.29, 256.35, 262.07, 267.90, 273.49,
        282.96],
    "xt_hi": [
        105.61, 110.36, 114.64, 120.29, 122.40, 126.45, 128.85, 134.17, 146.26, 149.34, 152.12, 156.36, 162.87,
        167.57, 170.85, 173.51, 178.77, 184.03, 186.89, 190.23, 193.10, 195.32, 198.81, 201.56, 204.84, 207.07,
        210.20, 219.24, 224.21, 227.05, 231.69, 236.06, 242.53, 246.19, 252.98, 257.04, 262.73, 268.56, 274.62,
        284.36],
    "xt_lo": [
        106.32, 111.06, 115.29, 120.94, 123.05, 127.14, 129.55, 139.89, 147.79, 150.40, 152.89, 157.01, 163.57,
        169.12, 171.50, 174.15, 179.42, 184.83, 187.54, 191.52, 193.79, 195.97, 199.46, 202.21, 205.49, 207.72,
        210.85, 220.08, 225.01, 227.70, 232.33, 237.25, 243.18, 248.91, 254.07, 257.96, 264.94, 272.60, 276.73,
        285.45],
    "up": [
        108.26, 111.86, 116.09, 124.35, 126.24, 131.14, 133.99, 145.81, 149.07, 151.92, 160.77, 162.19, 164.55,
        170.67, 173.33, 175.69, 180.22, 188.13, 190.49, 192.63, 196.02, 198.63, 201.12, 203.99, 206.83, 209.67,
        212.04, 220.88, 226.29, 228.69, 233.96, 240.43, 247.62, 253.34, 256.83, 262.55, 269.32, 275.40, 277.70,
        288.11],
    "silu": [
        109.86, 113.46, 117.69, 125.94, 128.35, 133.24, 135.58, 147.41, 150.67, 153.51, 162.37, 163.78, 166.15,
        172.77, 174.92, 177.79, 181.82, 189.72, 192.59, 193.57, 197.62, 200.22, 202.71, 206.09, 208.93, 211.27,
        213.63, 222.48, 227.89, 232.43, 235.56, 243.67, 250.14, 254.94, 258.56, 264.15, 273.21, 278.76, 279.29,
        289.50],
    "times3": [
        110.53, 114.13, 118.36, 126.62, 129.02, 140.49, 147.27, 148.39, 152.03, 154.19, 163.04, 165.08, 169.72,
        173.44, 175.79, 178.46, 182.49, 190.40, 193.27, 195.33, 198.29, 200.90, 203.39, 206.76, 209.61, 211.94,
        214.31, 223.15, 229.80, 237.85, 238.98, 249.85, 250.92, 256.83, 264.42, 265.55, 274.87, 279.44, 280.30,
        290.34],
    "ht": [
        111.46, 115.76, 120.76, 127.66, 132.56, 145.57, 148.17, 151.20, 153.33, 156.18, 164.31, 166.67, 172.09,
        175.45, 177.11, 179.19, 183.35, 191.91, 194.04, 195.90, 200.88, 203.24, 205.40, 208.25, 211.80, 213.45,
        216.72, 224.03, 231.47, 240.19, 244.50, 253.10, 259.12, 264.91, 267.66, 272.30, 280.54, 286.21, 288.81,
        293.29],
    "h_hi": [
        111.88, 116.18, 121.18, 128.08, 132.98, 145.99, 148.59, 151.86, 154.02, 156.84, 164.73, 167.09, 172.51,
        175.87, 177.53, 179.61, 183.77, 192.33, 194.46, 196.56, 201.30, 203.66, 205.82, 208.67, 212.46, 214.14,
        217.14, 224.69, 232.16, 240.85, 246.67, 253.52, 259.54, 265.98, 268.08, 275.10, 280.96, 286.63, 289.23,
        293.59],
    "h_lo": [
        112.31, 116.62, 121.62, 128.52, 139.55, 146.93, 149.03, 152.56, 154.71, 157.61, 165.61, 167.53, 172.94,
        176.31, 177.96, 180.05, 184.49, 192.76, 194.99, 196.89, 201.73, 204.10, 206.26, 209.10, 212.89, 214.83,
        217.57, 225.61, 232.94, 242.28, 249.51, 254.67, 261.29, 266.75, 271.65, 277.40, 283.42, 287.07, 290.61,
        295.38],
    "down": [
        113.28, 117.51, 122.22, 142.03, 144.39, 147.47, 150.49, 153.57, 156.42, 158.17, 167.91, 169.48, 174.74,
        177.35, 179.43, 182.16, 185.52, 195.19, 197.44, 200.04, 202.53, 205.64, 208.49, 211.09, 213.69, 216.01,
        219.06, 227.99, 235.86, 244.74, 255.20, 259.36, 265.15, 270.74, 281.23, 284.56, 287.40, 289.05, 293.41,
        296.52],
    "y_out": [
        114.16, 118.40, 123.11, 143.62, 145.27, 148.86, 151.38, 154.46, 157.31, 159.05, 168.80, 170.37, 176.13,
        178.29, 180.64, 184.51, 186.41, 196.08, 198.33, 200.88, 204.36, 206.59, 209.72, 211.98, 214.58, 217.40,
        219.95, 228.87, 238.16, 246.94, 256.09, 260.25, 266.25, 276.06, 283.88, 285.45, 288.29, 291.25, 294.29,
        297.06],
    "y_put": [
        114.74, 118.98, 123.69, 144.20, 145.85, 149.44, 151.96, 155.04, 157.89, 159.63, 169.38, 170.95, 176.71,
        178.87, 181.22, 185.09, 186.99, 196.66, 198.91, 201.24, 204.94, 207.17, 210.30, 212.56, 215.16, 217.98,
        220.53, 229.45, 238.74, 247.51, 256.67, 260.83, 266.83, 276.64, 284.46, 286.03, 288.87, 291.83, 294.87,
        297.42],
    "collect": [
        206.22, 207.26, 208.30, 209.34, 216.66, 221.86, 223.94, 234.14, 242.79, 245.91, 250.07, 255.46, 266.41,
        267.45, 269.57, 272.69, 300.07, 301.11, 302.15, 303.19, 312.06, 314.47, 315.51, 316.55, 321.75, 322.79,
        323.83, 324.87, 329.03, 332.41, 334.49, 339.02],
    "collect2": [
        210.38, 211.46, 212.50, 215.62, 222.90, 233.10, 238.63, 239.67, 249.03, 251.11, 256.50, 263.29, 270.61,
        271.65, 273.73, 276.33, 305.45, 306.49, 307.53, 311.02, 317.59, 318.63, 319.67, 320.71, 325.91, 326.95,
        327.99, 330.07, 333.45, 337.98, 340.06, 343.41],
    "load_bd": [99.39, 99.76, 220.72, 244.60, 272.40, 297.83, 322.77, 325.98],
    "mix": [
        215.15, 219.77, 239.34, 243.64, 265.86, 271.45, 292.43, 296.88, 316.32, 321.82, 323.62, 325.03, 345.23,
        352.69, 358.94, 363.81],
    "y_hi": [
        216.19, 220.88, 240.37, 244.68, 266.89, 272.73, 293.74, 297.91, 317.35, 322.85, 332.54, 333.68, 346.26,
        353.78, 359.98, 365.08],
    "y_lo": [216.84, 221.53, 241.68, 245.33, 267.54, 273.38, 294.78, 298.62, 318.00, 323.50],
    "had1": [
        217.64, 222.33, 242.48, 246.13, 268.38, 274.18, 295.58, 300.04, 322.68, 328.51, 333.21, 335.80, 347.02,
        355.25, 360.79, 366.09],
    "stats1": [
        218.75, 223.68, 243.78, 247.25, 270.32, 275.39, 296.69, 301.16, 324.10, 329.63, 335.45, 338.10, 349.37,
        357.13, 362.66, 368.27],
    "stats1_value": [
        220.68, 225.95, 246.53, 251.44, 274.32, 277.73, 299.23, 302.66, 325.60, 331.56, 336.95, 344.68, 355.78,
        358.63, 364.79, 370.40],
    "round1": [
        220.43, 221.36, 225.19, 225.64, 245.29, 245.74, 248.76, 249.21, 271.83, 272.28, 276.90, 277.36, 298.39,
        298.84, 302.67, 304.08, 326.11, 326.56, 331.14, 331.59, 336.96, 337.41, 339.61, 340.07, 350.88, 351.33,
        358.64, 359.09, 364.18, 364.63, 369.78, 370.23],
    "quant1": [
        222.13, 226.50, 248.58, 250.58, 273.98, 279.96, 300.21, 305.64, 327.18, 332.21, 339.43, 340.97, 354.85,
        361.42, 366.73, 372.54],
    "turn1": [
        223.27, 227.71, 249.11, 251.77, 275.13, 280.95, 301.33, 306.57, 327.72, 332.75, 339.97, 341.63, 356.96,
        367.80, 371.54, 374.07],
    "turn1_out": [
        223.73, 228.39, 249.66, 252.51, 275.58, 281.41, 301.78, 307.28, 328.18, 333.20, 340.52, 342.09, 357.42,
        368.26, 371.99, 374.53],
    "wide": [
        224.41, 224.85, 230.11, 230.55, 250.41, 250.85, 254.76, 255.91, 276.82, 277.26, 282.09, 282.52, 302.46,
        302.90, 307.95, 308.39, 329.46, 329.89, 334.92, 335.36, 341.20, 341.91, 342.77, 343.21, 359.80, 362.49,
        368.95, 369.39, 374.35, 374.79, 375.23, 375.66],
    "relu": [
        226.10, 226.57, 230.73, 231.21, 251.55, 252.03, 255.44, 256.57, 277.81, 278.29, 282.93, 283.41, 303.12,
        303.60, 308.57, 309.05, 330.07, 330.55, 335.54, 336.02, 342.57, 343.05, 344.99, 345.47, 360.46, 363.20,
        370.68, 371.16, 375.01, 375.49, 375.96, 376.44],
    "square": [
        226.83, 231.38, 252.20, 257.35, 278.46, 283.76, 303.77, 309.22, 330.96, 337.50, 344.08, 350.70, 361.76,
        371.33, 376.56, 377.17],
    "square2": [
        227.20, 231.88, 254.23, 257.54, 278.92, 284.30, 304.23, 309.80, 331.18, 336.75, 344.45, 346.10, 363.83,
        371.79, 376.11, 377.34],
    "stage": [
        228.60, 229.20, 233.27, 233.87, 255.63, 256.23, 259.29, 259.89, 280.83, 281.43, 285.78, 286.38, 305.97,
        306.57, 311.19, 311.79, 332.58, 333.18, 339.77, 340.37, 345.85, 346.45, 351.47, 352.07, 367.07, 367.67,
        373.19, 373.79, 377.77, 378.37, 378.97, 379.57],
    "v_hi": [
        229.38, 229.98, 234.05, 234.65, 257.52, 258.04, 260.73, 261.25, 281.89, 282.41, 286.90, 287.42, 306.75,
        307.75, 311.97, 312.58, 334.16, 334.68, 341.00, 341.52],
    "v_lo": [230.33, 236.65, 258.56, 261.62, 282.82, 289.74, 307.45, 314.57, 334.85, 343.48],
    "v_lo2": [230.65, 235.32, 258.76, 262.07, 283.08, 288.09, 308.57, 313.25, 335.53, 342.19],
    "had2": [
        232.08, 233.02, 237.45, 238.39, 260.19, 261.13, 263.97, 266.71, 285.27, 286.45, 290.54, 291.49, 310.13,
        311.07, 315.37, 317.17, 337.51, 338.45, 344.28, 346.08, 348.73, 350.44, 353.55, 357.24, 369.83, 372.37,
        376.10, 378.69, 380.39, 382.10, 383.94, 386.20],
    "round2": [
        236.83, 237.49, 241.86, 243.01, 264.65, 265.32, 270.50, 271.16, 289.92, 290.59, 294.96, 295.62, 314.75,
        315.42, 320.95, 321.62, 343.66, 344.32, 349.55, 350.21, 355.03, 355.69, 361.87, 362.54, 376.92, 377.59,
        383.13, 383.79, 387.29, 387.95, 390.43, 391.10],
    "stats2": [
        234.47, 239.51, 262.24, 268.14, 287.57, 292.60, 312.40, 318.60, 341.31, 347.19, 352.67, 359.18, 374.39,
        380.77, 383.98, 388.08],
    "quant2": [
        238.38, 245.93, 266.15, 272.00, 291.42, 298.02, 316.25, 322.48, 345.23, 355.18, 356.53, 365.34, 380.17,
        386.15, 390.25, 391.93],
    "turn2": [
        247.07, 249.86, 272.93, 279.11, 299.49, 304.73, 318.80, 324.47, 352.14, 360.24, 365.54, 371.81, 385.65,
        387.91, 391.05, 392.73],
    "turn2_out": [
        247.80, 250.64, 273.72, 279.85, 300.22, 305.46, 319.53, 325.21, 352.87, 360.97, 366.27, 372.55, 386.38,
        388.64, 391.78, 393.46],
    "narrow": [
        252.23, 258.24, 279.67, 283.61, 303.80, 309.25, 320.64, 326.31, 362.93, 364.66, 368.08, 377.81, 388.46,
        389.74, 393.28, 394.57],
    "finish_scale": [
        242.62, 242.69, 267.09, 277.33, 290.94, 295.58, 315.17, 320.94, 356.33, 356.40, 361.36, 362.36, 386.75,
        386.82, 386.89, 391.65],
    "finish": [
        253.27, 260.49, 282.03, 284.65, 304.85, 310.30, 321.68, 327.52, 364.00, 365.94, 369.60, 382.95, 390.85,
        392.53, 394.33, 395.62],
    "store": [
        254.17, 261.39, 282.92, 285.55, 305.74, 311.19, 322.58, 328.41, 364.89, 366.83, 370.50, 383.84, 391.75,
        393.42, 395.22, 396.51],
}
SET = [0, 1, 0, 1, 0, 1, 0, 1, 0, 1, 2, 3, 0, 1, 2, 3]
PAIRS_AFTER = (0,0,0,0,3,7,7,3)
STEPS = []
for _b in range(NBLK):
    STEPS += [(True, 2 * _b), (True, 2 * _b + 1)]
    _n = sum(PAIRS_AFTER[:_b])
    STEPS += [(False, _n + _j) for _j in range(PAIRS_AFTER[_b] if _b < NBLK - 1 else NSB * SPAIRS - _n)]
PLACE = {v: _i for _i, v in enumerate(STEPS)}
LD = 8
NATIVE = range(10, 16)


def adapter_moe_quant_ffn(nc, xT, x, adapter, cond, WA, WE, scal, cw, wuT, wdT, consts, consts16, out):
    with ExitStack() as ctx:
        def sb(name, shape, dt=F32):
            return ctx.enter_context(nc.sbuf_tensor(name, shape, dt))

        def pb(name):
            return ctx.enter_context(nc.psum_tensor(name, [P, 512], F32))

        def sem(name):
            return ctx.enter_context(nc.semaphore(name))

        gd = nc.dram_tensor("gd", (P, 1024), F32, kind="Internal").ap()
        hd = [nc.dram_tensor(f"hd{i}", (TPS * P, D), F32, kind="Internal").ap() for i in range(NSB)]
        ys = [nc.dram_tensor(f"ys{i}", (STILES * P, D), F32, kind="Internal").ap() for i in range(NSB)]

        WH = sb("WH", [P, C_END], F32R)
        WL = sb("WL", [P, C_END], F32R)
        X1 = sb("X1", [P, 4 * NBLK, D])
        CON = sb("CON", [P, 728])
        IDENT, HADF = CON[:, 0:128], CON[:, 128:256]
        W8, EIDX, SLOT0 = CON[:, 256:264], CON[:, 264:265], CON[:, 265:265 + STILES]
        LANE = CON[:, 568:696]
        TOKEN = CON[:, 696:728].rearrange("p (k t) -> p k t", k=2)
        HADP = [HADF.unsqueeze(1).broadcast_to([P, 2, P]), CON[:, 312:568].rearrange("p (a n) -> p a n", a=2)]
        C16 = sb("C16", [P, 3, P], BF16)
        LOWER, ONES16, IDB = C16[:, 0, :], C16[:, 1, :], C16[:, 2, :]
        IDR = sb("IDR", [P, P], F32R)
        HAD2 = sb("HAD2", [P, 2, 2, P], F32R)
        MAG = sb("MAG", [P, 1])
        ONES = sb("ONES", [P, P])
        IDXC = sb("IDXC", [P, 1], I32)
        SCAL = sb("SCAL", [P, 1])
        MASK = sb("MASK", [P, P])
        GS = sb("GS", [P, 12, P])
        GATH = GS[:, 0:8, :].rearrange("p a b -> p (a b)")
        GS_HOT = GS[:, 3:10, :].rearrange("p a b -> p (a b)")[:, 0:16 * STILES]\
            .rearrange("p (r j a n) -> p r j a n", r=2, j=4, a=2)
        G4 = sb("G4", [P, NSB, 4, TPS])
        MCB = sb("MCB", [P, P], BF16)
        SM = sb("SM", [P, 16])
        PB = sb("PB", [P, 4, 12])
        POSF = sb("POSF", [P, 2, TPS])
        POS = sb("POS", [P, NSB, 2, TPS], I32)
        ROW = sb("ROW", [P, 3, 2, TPS])
        SLOT = sb("SLOT", [P, NSB, STILES], I32)
        SLOTS = sb("SLOTS", [P, NSB, STILES])
        EXF = sb("EXF", [P, 2, STILES])
        EX = sb("EX", [P, NSB, STILES], I32)
        WU = sb("WU", [P, 2, HID], BF16)
        WD = sb("WD", [P, 4, D], BF16)
        SW = sb("SW", [P, 8])

        XIN = sb("XIN", [P, 2, 2, D])
        YS = sb("YS", [P, 2, 2, D])
        XSH = sb("XSH", [P, 2, 2, 2 * P], F32R)
        XSL = sb("XSL", [P, 2, 2, 2 * P], F32R)
        T = sb("T", [P, 3, 2 * P])
        HH = sb("HH", [P, 3, 2 * P], F32R)
        HL = sb("HL", [P, 3, 2 * P], F32R)
        WUR = XIN[:, :, :, :].rearrange("p a b d -> p (a b d)").rearrange("p (k n) -> p k n", k=2)
        WDR = YS[:, :, :, :].rearrange("p a b d -> p (a b) d")
        RAWE = X1[:, 4 * BPS:, :].rearrange("p t d -> p (t d)")[:, 0:5 * EW].rearrange("p (e n) -> p e n", e=5)

        ZR = sb("ZR", [P, 7168], F32R)
        ZF = sb("ZF", [P, 6656])

        def zr(a, n):
            return ZR[:, a:a + n]

        def zf(a, n):
            return ZF[:, a:a + n]

        H0H = zr(0, 2048).rearrange("p (a k t) -> p a k t", a=2, k=2)
        H0L = zr(2048, 2048).rearrange("p (a k t) -> p a k t", a=2, k=2)
        XH = zr(4096, 1024).rearrange("p (k t) -> p k t", k=2)
        XL = zr(5120, 1024).rearrange("p (k t) -> p k t", k=2)
        XAH, XAL = zr(6144, 512), zr(6656, 512)
        HT = zf(0, 4096).rearrange("p (t d) -> p t d", d=D)
        RAWA, RAWB = zf(0, C_G), zf(C_G, C_E - C_G)
        HOTL = zf(4096, 1024).rearrange("p (r j n) -> p r j n", r=2, j=4)
        XR = zf(5120, 1024).rearrange("p (k t) -> p k t", k=2)
        XA = zf(6144, 512)
        IDXI = XA[:, 0:P].bitcast(I32)

        def cut(v, c):
            return v.rearrange("p (c t) -> p c t", c=c)

        BD = zf(5120, 1024).rearrange("p (a t d) -> p a t d", a=2, t=4)
        SETS = [(cut(zr(1024 * i, 1024), 4), cut(zr(2048 + 1024 * i, 1024), 4),
                 cut(zf(1024 * i, 1024), 4), cut(zf(2048 + 1024 * i, 1024), 4),
                 cut(zf(6144 + 256 * i, 256).bitcast(BF16), 2), cut(zf(4096 + 512 * i, 512).bitcast(BF16), 2),
                 sb(f"ST{i}", [P, 13, 2])) for i in range(2)]
        first4 = X1[:, 0:16, :].rearrange("p t d -> p (t d)")
        tiles = T[:, :, :].rearrange("p a n -> p (a n)")
        slots = XIN[:, :, :, :].rearrange("p a b d -> p (a b d)")
        SETS += [(cut(WH[:, C_E + 2048 * i:C_E + 2048 * i + 1024], 4),
                  cut(WH[:, C_E + 2048 * i + 1024:C_E + 2048 * i + 2048], 4),
                  cut(first4[:, 2048 * i:2048 * i + 1024], 4), cut(first4[:, 2048 * i + 1024:2048 * i + 2048], 4),
                  cut(tiles[:, 256 * i:256 * i + 256].bitcast(BF16), 2),
                  cut(slots[:, 512 * i:512 * i + 512].bitcast(BF16), 2), sb(f"ST{2 + i}", [P, 13, 2])) for i in range(2)]

        UP = [pb(f"UP{i}") for i in range(2)]
        DN, LB, TR, HT2 = pb("DN"), pb("LB"), pb("TR"), pb("HT2")
        AUX = [pb(f"AUX{i}") for i in range(2)]

        names = ("con c16 idc idi scl cg gw xr mag out wq "
                 "wh wl gwc had2 mask idr "
                 "xh xl xa xam xah xal h0w h0 h0h h0l gate glc glf tk tko gsil gch rank pl pos ext hot hotl slt tab xt xth xtl "
                 "a sil t3 ht hh hl acc x1s ye bdz "
                 "y yh yl f st1 qf q1 q1t q1c up rl sq sq2 bf vh vl vl2 g st2 q2f q2 q2t q2c dn fs fin "
                 "wsum wtot sw wt").split()
        S = {n: sem("s_" + n) for n in names}
        s_wa = [sem(f"s_wa{i}") for i in range(2)]
        s_we = [sem(f"s_we{i}") for i in range(NE)]
        s_x = [sem(f"p_x{i}") for i in range(NBLK)]
        s_bd = [sem(f"p_bd{i}") for i in range(2)]
        s_hd = [sem(f"p_hd{i}") for i in range(NBLK)]
        s_xi = [sem(f"p_xi{i}") for i in range(2)]
        s_y = [sem(f"p_y{i}") for i in range(2)]
        s_g = [[sem(f"p_g{k}{i}") for i in range(4)] for k in range(2)]
        s_o = [sem(f"p_o{i}") for i in range(2 * NBLK)]

        plan = {e: [] for e in ("sync", "gpsimd", "scalar", "vector", "tensor")}

        def put(engine, t, fn):
            plan[engine].append((t, len(plan[engine]), fn))

        used, when = {}, {}

        def at(engine, name, key, fn, i=0):
            k = used.get(name, 0)
            used[name] = k + 1
            t = when[(name, key, i)] = TIME[name][k]
            put(engine, t, fn)

        EARLY = -1000

        def load_first(e):
            e.dma_start(XR, xT.rearrange("(k p) t -> p k t", p=P)[:, :, 0:TB]).then_inc(S["xr"], 16)
            e.dma_start(RAWA, WA[:, 0:C_G]).then_inc(s_wa[0], 16)
            e.dma_start(IDXI, adapter.partition_broadcast(P)).then_inc(S["idi"], 16)
            e.dma_start(CON[:, :], consts).then_inc(S["con"], 16)
            e.dma_start(RAWB[:, 0:C_E - C_G], WA[:, C_G:C_E]).then_inc(s_wa[1], 16)
        put("sync", EARLY, load_first)

        def load_small(e):
            e.dma_start(IDXC[:, :], cond.rearrange("(p a) -> p a", a=1)).then_inc(S["idc"], 16)
            e.dma_start(SCAL[:, :], scal).then_inc(S["scl"], 16)
            e.dma_start(C16[:, :, :], consts16).then_inc(S["c16"], 16)
        put("scalar", EARLY, load_small)

        def load_expert(e, i):
            if i >= 5:
                e.wait_ge(S["wl"], 2 + i - 5 + 1)
            elif i % 2 == 0:
                e.wait_ge(S["xl"], 1 + i // 2)
            e.dma_start(RAWE[:, i % 5, :], WE[i]).then_inc(s_we[i], 16)
        for i in range(NE):
            at("sync", "load_expert", 0, lambda e, i=i: load_expert(e, i))

        def load_wq(e):
            e.wait_ge(S["xl"], 4)
            e.dma_start(WUR, wuT.rearrange("(k p) n -> p k n", p=P)).then_inc(S["wq"], 16)
            e.dma_start(WDR, wdT.rearrange("(k p) n -> p k n", p=P)).then_inc(S["wq"], 16)
        at("sync", "load_wq", 0, load_wq)

        def gather(e):
            e.memset(ONES[:, :], 1.0).then_inc(S["mag"], 1)
            e.memset(MAG[:, :], MAGIC).then_inc(S["mag"], 1)
            e.memset(PB[:, :, :], 0.0).then_inc(S["mag"], 1)
            e.wait_ge(S["idc"], 16)
            e.indirect_dma_start(GATH, None, cw, bass.IndirectOffsetOnAxis(ap=IDXC[:, 0:1], axis=0))\
             .then_inc(S["cg"], 16)
        put("gpsimd", EARLY, gather)

        def stash(e):
            e.wait_ge(S["cg"], 16)
            e.dma_start(gd, GATH).then_inc(S["gw"], 16)
        at("sync", "stash", 0, stash)

        def split_hi(e, i):
            if i < 2:
                e.wait_ge(s_wa[i], 16)
                a, b, raw = ((0, C_G, RAWA), (C_G, C_E, RAWB[:, 0:C_E - C_G]))[i]
            else:
                e.wait_ge(s_we[i - 2], 16)
                a = C_E + (i - 2) * EW
                b, raw = a + EW, RAWE[:, (i - 2) % 5, :]
            e.activation(WH[:, a:b], raw, ACT.Copy).then_inc(S["wh"], 1)

        def split_lo(e, i):
            if i < 2:
                a, b, raw = ((0, C_G, RAWA), (C_G, C_E, RAWB[:, 0:C_E - C_G]))[i]
            else:
                a = C_E + (i - 2) * EW
                b, raw = a + EW, RAWE[:, (i - 2) % 5, :]
            e.wait_ge(S["wh"], i + 1)
            e.tensor_tensor(WL[:, a:b], raw, WH[:, a:b].bitcast(F32), ALU.subtract).then_inc(S["wl"], 1)

        for i in range(NE + 2):
            at("scalar", "split_hi", 0, lambda e, i=i: split_hi(e, i))
            at("vector", "split_lo", 0, lambda e, i=i: split_lo(e, i))

        GW = sb("GW", [P, 2, 2, NE], F32R)

        def gate_weights(e):
            e.wait_ge(S["wl"], 2)
            for i, w in enumerate((WH, WL)):
                e.tensor_copy(GW[:, :, i, :], w[:, C_G:C_S].bitcast(F32).rearrange("p (k e) -> p k e", k=2))\
                 .then_inc(S["gwc"], 1)
        at("vector", "gate_weights", 0, gate_weights)

        def make_mask(e):
            e.wait_ge(S["idi"], 16)
            e.wait_ge(S["con"], 16)
            e.wait_ge(S["scl"], 16)
            e.tensor_copy(MASK[:, :], IDXI).then_inc(S["mask"], 1)
            e.wait_ge(S["mask"], 1)
            e.tensor_scalar(MASK[:, :], MASK[:, :], EIDX, SCAL[:, 0:1], ALU.is_equal, ALU.mult).then_inc(S["mask"], 1)
        at("vector", "make_mask", 0, make_mask)

        def make_identity(e):
            e.wait_ge(S["con"], 16)
            e.tensor_copy(IDR[:, :], IDENT).then_inc(S["idr"], 1)
            for k in range(2):
                e.tensor_copy(HAD2[:, k, 0, :], HADF).then_inc(S["had2"], 1)
                e.tensor_scalar(HAD2[:, k, 1, :], HADF, 1.0 - 2 * k, None, ALU.mult).then_inc(S["had2"], 1)
        at("vector", "make_identity", 0, make_identity)

        def weight_sums(e):
            e.wait_ge(S["wq"], 32)
            e.tensor_reduce(SW[:, 0:1], WUR, AX.XY, ALU.add, apply_absolute_value=True).then_inc(S["wsum"], 1)
            e.tensor_reduce(SW[:, 1:2], WDR, AX.XY, ALU.add, apply_absolute_value=True).then_inc(S["wsum"], 1)
        at("vector", "weight_sums", 0, weight_sums)

        def weight_total(e):
            e.wait_ge(S["wsum"], 2)
            e.wait_ge(S["mag"], 1)
            bank_free(e, "AUX0", ("weight_total", 0, 0))
            e.matmul(AUX[0][:, 0:2], ONES[:, :], SW[:, 0:2], start=True, stop=True).then_inc(S["wtot"], 1)
        at("tensor", "weight_total", 0, weight_total)

        def ternary(e):
            e.wait_ge(S["wtot"], 1)
            e.tensor_scalar(SW[:, 2:4], AUX[0][:, 0:2], 1.0 / (D * HID), EPS, ALU.mult, ALU.max).then_inc(S["sw"], 1)
            e.wait_ge(S["sw"], 1)
            e.reciprocal(SW[:, 4:6], SW[:, 2:4]).then_inc(S["sw"], 1)
            e.wait_ge(S["sw"], 2)
            n = 0
            for raw, q, c in ((WUR, WU, 4), (WDR, WD, 5)):
                e.tensor_scalar(raw, raw, SW[:, c:c + 1], MAGIC, ALU.mult, ALU.add).then_inc(S["wt"], 1)
                e.wait_ge(S["wt"], n + 1)
                e.tensor_scalar(raw, raw, MAGIC, 1.0, ALU.subtract, ALU.min).then_inc(S["wt"], 1)
                e.wait_ge(S["wt"], n + 2)
                e.tensor_scalar(q[:, :, :], raw, -1.0, None, ALU.max).then_inc(S["wt"], 1)
                n += 3
        at("vector", "ternary", 0, ternary)

        def down_free(e, s):
            if s > 0:
                shared, i = STEPS[s - 1]
                e.wait_ge(S["x1s" if shared else "ye"], i + 1)

        def plan_adapter(b):
            pr = b % 2
            h0h, h0l = H0H[:, pr, :, :], H0L[:, pr, :, :]

            def load_x(e):
                if b >= BPS:
                    e.wait_ge(S["wl"], NE + 2)
                e.dma_start(X1[:, 4 * b:4 * b + 4, :], x[b * TB:(b + 1) * TB, :].rearrange("(t p) d -> p t d", p=P))\
                 .then_inc(s_x[b], 16)
            at("sync", "load_x", b, load_x)

            if b > 0:
                def load(e):
                    e.wait_ge(S["xl"], b)
                    e.dma_start(XR, xT.rearrange("(k p) t -> p k t", p=P)[:, :, b * TB:(b + 1) * TB])\
                     .then_inc(S["xr"], 16)
                at("sync", "load_xT", b, load)

            def x_hi(e):
                e.wait_ge(S["xr"], 16 * (b + 1))
                if b > 0:
                    e.wait_ge(S["xa"], b)
                    e.wait_ge(S["h0w"], 2 * b)
                e.activation(XH, XR, ACT.Copy).then_inc(S["xh"], 1)
            at("scalar", "x_hi", b, x_hi)

            def x_lo(e):
                e.wait_ge(S["xh"], b + 1)
                e.tensor_tensor(XL, XR, XH.bitcast(F32), ALU.subtract).then_inc(S["xl"], 1)
            at("vector", "x_lo", b, x_lo)

            def xa(e):
                e.wait_ge(S["xl"], b + 1)
                e.wait_ge(S["wl"], 1)
                bank_free(e, "TR", ("xa", b, 0))
                n = 0
                for k in range(2):
                    for w, xx in ((WH, XH), (WH, XL), (WL, XH)):
                        mm = e.matmul(TR[:, :], w[:, C_A + k * P:C_A + (k + 1) * P], xx[:, k, :],
                                      start=(n == 0), stop=(n == 5))
                        n += 1
                mm.then_inc(S["xa"], 1)
            at("tensor", "xa", b, xa)

            def xam(e):
                e.wait_ge(S["xa"], b + 1)
                if b == 0:
                    e.wait_ge(S["mask"], 2)
                if b > 0:
                    e.wait_ge(S["xal"], b)
                m = MASK[:, 16 * b:16 * b + 16].unsqueeze(2).broadcast_to([P, 16, 32])
                e.tensor_tensor(XA.rearrange("p (n t) -> p n t", t=32),
                                TR[:, :].rearrange("p (n t) -> p n t", t=32), m, ALU.mult).then_inc(S["xam"], 1)
            at("vector", "xam", b, xam)

            def xa_hi(e):
                e.wait_ge(S["xam"], b + 1)
                if b > 0:
                    e.wait_ge(S["h0"], 2 * b)
                e.activation(XAH, XA, ACT.Copy).then_inc(S["xah"], 1)
            at("scalar", "xa_hi", b, xa_hi)

            def xa_lo(e):
                e.wait_ge(S["xah"], b + 1)
                e.tensor_tensor(XAL, XA, XAH.bitcast(F32), ALU.subtract).then_inc(S["xal"], 1)
            at("vector", "xa_lo", b, xa_lo)

            def h0w(e, o):
                e.wait_ge(S["xl"], b + 1)
                if b == 0:
                    e.wait_ge(S["wl"], 1)
                bank_free(e, f"AUX{o}", ("h0w", b, o))
                n = 0
                for k in range(2):
                    c = C_W + k * D + o * P
                    for w, xx in ((WH, XH), (WH, XL), (WL, XH)):
                        mm = e.matmul(AUX[o][:, :], w[:, c:c + P], xx[:, k, :], start=(n == 0), stop=False,
                                      skip_group_check=True)
                        n += 1
                mm.then_inc(S["h0w"], 1)

            def h0(e, o):
                e.wait_ge(S["xal"], b + 1)
                e.wait_ge(S["h0w"], 2 * b + o + 1)
                c = C_B + o * P
                e.matmul(AUX[o][:, :], WH[:, c:c + P], XAH, start=False, stop=False, skip_group_check=True)
                e.matmul(AUX[o][:, :], WH[:, c:c + P], XAL, start=False, stop=False, skip_group_check=True)
                e.matmul(AUX[o][:, :], WL[:, c:c + P], XAH, start=False, stop=True, skip_group_check=True)\
                 .then_inc(S["h0"], 1)

            def h0_hi(e, o):
                e.wait_ge(S["h0"], 2 * b + o + 1)
                if b >= 2 and o == 0:
                    e.wait_ge(S["a"], PLACE[True, 2 * b - 3] + 1)
                    e.wait_ge(S["gate"], b - 1)
                    e.wait_ge(S["tk"], 2 * (b - 1))
                e.activation(h0h[:, o, :], AUX[o][:, :], ACT.Copy).then_inc(S["h0h"], 1)

            def h0_lo(e, o):
                e.wait_ge(S["h0h"], 2 * b + o + 1)
                e.tensor_tensor(h0l[:, o, :], AUX[o][:, :], h0h[:, o, :].bitcast(F32), ALU.subtract)\
                 .then_inc(S["h0l"], 1)
            for o in range(2):
                at("tensor", "h0w", b, lambda e, o=o: h0w(e, o), o)
                at("tensor", "h0", b, lambda e, o=o: h0(e, o), o)
                at("scalar", "h0_hi", b, lambda e, o=o: h0_hi(e, o), o)
                at("vector", "h0_lo", b, lambda e, o=o: h0_lo(e, o), o)

            def gate(e):
                e.wait_ge(S["h0l"], 2 * b + 2)
                if b == 0:
                    e.wait_ge(S["gwc"], 2)
                bank_free(e, "AUX0", ("gate", b, 0))
                for t in range(4):
                    tok = slice(t * P, (t + 1) * P)
                    for k in range(2):
                        e.matmul(AUX[0][:, 16 * t:16 * t + 16], h0h[:, k, tok],
                                 GW[:, k, :, :].rearrange("p a e -> p (a e)"),
                                 start=(k == 0), stop=False, skip_group_check=True)
                    for k in range(2):
                        mm = e.matmul(AUX[0][:, 16 * t:16 * t + 8], h0l[:, k, tok], GW[:, k, 0, :],
                                      start=False, stop=(k == 1), skip_group_check=True)
                mm.then_inc(S["gate"], 1)
            at("tensor", "gate", b, gate)

            c4 = slice(32 * (b % BPS), 32 * (b % BPS) + 32)

            def logits_lo(e):
                e.wait_ge(S["gate"], b + 1)
                if b == 0:
                    e.wait_ge(S["gw"], 16)
                if b % BPS == 0 and b > 0:
                    e.wait_ge(S["pos"], b // BPS)
                e.activation(GS[:, 0, c4].rearrange("p (t e) -> p t e", e=NE),
                             AUX[0][:, 0:64].rearrange("p (t a e) -> p t a e", a=2, e=NE)[:, :, 1, :],
                             ACT.Copy).then_inc(S["glc"], 1)
            at("scalar", "logits_lo", b, logits_lo)

            def logits(e):
                e.wait_ge(S["glc"], b + 1)
                e.tensor_tensor(GS[:, 2, c4].rearrange("p (t e) -> p t e", e=NE),
                                AUX[0][:, 0:64].rearrange("p (t a e) -> p t a e", a=2, e=NE)[:, :, 0, :],
                                GS[:, 0, c4].rearrange("p (t e) -> p t e", e=NE), ALU.add).then_inc(S["glf"], 1)
            at("vector", "logits", b, logits)

            def tok(e, j):
                if j == 0:
                    e.wait_ge(S["h0l"], 2 * b + 2)
                    if b == 0:
                        e.wait_ge(S["idr"], 1)
                bank_free(e, "HT2", ("tok", b, j))
                for t in range(2):
                    tok = slice((2 * j + t) * P, (2 * j + t + 1) * P)
                    for k in range(2):
                        dst = HT2[:, t * D + k * P:t * D + (k + 1) * P]
                        e.matmul(dst, h0h[:, k, tok], IDR[:, :], start=True, stop=False)
                        mm = e.matmul(dst, h0l[:, k, tok], IDR[:, :], start=False, stop=True)
                mm.then_inc(S["tk"], 1)

            def tok_out(e, j):
                e.wait_ge(S["tk"], 2 * b + j + 1)
                t = 4 * (b % BPS) + 2 * j
                if b == 0:
                    e.wait_ge(S["wl"], 2)
                if b >= BPS:
                    e.wait_ge(s_hd[b - BPS], 16)
                e.activation(HT[:, t:t + 2, :], HT2[:, :].rearrange("p (t d) -> p t d", t=2), ACT.Copy)\
                 .then_inc(S["tko"], 1)
            for j in range(2):
                at("tensor", "tok", b, lambda e, j=j: tok(e, j), j)
                at("scalar", "tok_out", b, lambda e, j=j: tok_out(e, j), j)

            def hd_put(e):
                p, t = b // BPS, 4 * (b % BPS)
                e.wait_ge(S["tko"], 2 * b + 2)
                e.dma_start(hd[p][t * P:(t + 4) * P, :].rearrange("(t p) d -> p t d", p=P), HT[:, t:t + 4, :])\
                 .then_inc(s_hd[b], 16)
            at("sync", "hd_put", b, hd_put)

            for h in range(2):
                m = 2 * b + h
                s = PLACE[True, m]
                tk = slice(h * 256, h * 256 + 256)

                def s_up(e, s=s, tk=tk):
                    e.wait_ge(S["h0l"], 2 * b + 2)
                    if b == 0:
                        e.wait_ge(S["wl"], 2)
                    if s >= 2:
                        e.wait_ge(S["t3"], s - 1)
                    for i in range(2):
                        n = 0
                        for k in range(2):
                            c = C_S + 2 * k * P + i * P
                            for w, hh in ((WH, h0h), (WH, h0l), (WL, h0h)):
                                mm = e.matmul(UP[s % 2][:, i * 256:i * 256 + 256], w[:, c:c + P], hh[:, k, tk],
                                              start=(n == 0), stop=(n == 5))
                                n += 1
                    mm.then_inc(S["a"], 1)

                def s_silu(e, s=s):
                    e.wait_ge(S["a"], s + 1)
                    if s >= 3:
                        e.wait_ge(S["hl"], s - 2)
                    e.activation(T[:, s % 3, :], UP[s % 2][:, 0:256], ACT.Silu).then_inc(S["sil"], 1)

                def s_times3(e, s=s):
                    e.wait_ge(S["sil"], s + 1)
                    e.tensor_tensor(T[:, s % 3, :], UP[s % 2][:, 256:512], T[:, s % 3, :], ALU.mult).then_inc(S["t3"], 1)

                def s_h_hi(e, s=s):
                    e.wait_ge(S["t3"], s + 1)
                    if s >= 3:
                        e.wait_ge(S["acc"], s - 2)
                    e.activation(HH[:, s % 3, :], T[:, s % 3, :], ACT.Copy).then_inc(S["hh"], 1)

                def s_h_lo(e, s=s):
                    e.wait_ge(S["hh"], s + 1)
                    e.tensor_tensor(HL[:, s % 3, :], T[:, s % 3, :], HH[:, s % 3, :].bitcast(F32), ALU.subtract)\
                     .then_inc(S["hl"], 1)

                def s_down(e, s=s):
                    e.wait_ge(S["hl"], s + 1)
                    down_free(e, s)
                    for c in range(2):
                        for n, (hh, w) in enumerate(((HH, WH), (HL, WH), (HH, WL))):
                            mm = e.matmul(DN[:, c * D:(c + 1) * D], hh[:, s % 3, c * P:(c + 1) * P],
                                          w[:, C_S + 512:C_E], start=(n == 0), stop=(n == 2))
                    mm.then_inc(S["acc"], 1)

                def s_out(e, s=s, m=m, h=h):
                    e.wait_ge(S["acc"], s + 1)
                    if h == 0:
                        e.wait_ge(s_x[b], 16)
                    v = X1[:, 2 * m:2 * m + 2, :].rearrange("p t d -> p (t d)")
                    e.tensor_tensor(v, DN[:, :], v, ALU.add).then_inc(S["x1s"], 1)
                at("tensor", "s_up", b, s_up, h)
                at("scalar", "s_silu", b, s_silu, h)
                at("vector", "s_times3", b, s_times3, h)
                at("scalar", "s_h_hi", b, s_h_hi, h)
                at("vector", "s_h_lo", b, s_h_lo, h)
                at("tensor", "s_down", b, s_down, h)
                at("vector", "s_out", b, s_out, h)

        def plan_route(p):
            n = [18 * p]

            def link(e, ins):
                n[0] += 1
                ins.then_inc(S["gch"], 1)
                e.wait_ge(S["gch"], n[0])

            def r(i):
                return GS[:, i, :].rearrange("p (t e) -> p t e", e=NE)

            def g4(i):
                return G4[:, p, i, :]

            def c(i):
                return g4(i).unsqueeze(2).broadcast_to([P, TPS, NE])

            def nonzero(e):
                e.wait_ge(S["glf"], BPS * (p + 1))
                if p > 0:
                    e.wait_ge(S["ext"], p)
                    e.wait_ge(S["tab"], 8 * p)
                link(e, e.tensor_scalar(GS[:, 0, :], GS[:, 2, :], 0.0, 1e-30, ALU.is_equal, ALU.mult))
                link(e, e.tensor_tensor(GS[:, 1, :], GS[:, 2, :], GS[:, 0, :], ALU.add))
            at("vector", "nonzero", p, nonzero)

            def gate_silu(e):
                e.wait_ge(S["gch"], 18 * p + 2)
                e.activation(GS[:, 2, :], GS[:, 1, :], ACT.Silu).then_inc(S["gsil"], 1)
            at("scalar", "gate_silu", p, gate_silu)

            def top2(e):
                w8 = W8.unsqueeze(1).broadcast_to([P, TPS, NE])
                link(e, e.reciprocal(GS[:, 4, :], GS[:, 1, :]))
                e.wait_ge(S["gsil"], p + 1)
                link(e, e.tensor_tensor(GS[:, 5, :], GS[:, 2, :], GS[:, 4, :], ALU.mult))
                link(e, e.tensor_scalar(GS[:, 6, :], GS[:, 1, :], SAT, None, ALU.is_ge))
                link(e, e.scalar_tensor_tensor(out=GS[:, 3, :], in0=GS[:, 5, :], scalar=1.0, in1=GS[:, 6, :],
                                               op0=ALU.min, op1=ALU.max))
                for j, sc, base in ((0, 3, 4), (1, 7, 8)):
                    link(e, e.tensor_reduce(g4(2 * j), r(sc), AX.X, ALU.max))
                    link(e, e.tensor_tensor(r(base), r(sc), c(2 * j), ALU.is_equal))
                    link(e, e.tensor_tensor(r(base + 1), r(base), w8, ALU.mult))
                    link(e, e.tensor_reduce(g4(2 * j + 1), r(base + 1), AX.X, ALU.max))
                    link(e, e.tensor_tensor(r(base + 2), r(base + 1), c(2 * j + 1), ALU.is_equal))
                    if j == 0:
                        link(e, e.scalar_tensor_tensor(out=GS[:, 7, :], in0=GS[:, 6, :], scalar=-4.0, in1=GS[:, 3, :],
                                                       op0=ALU.mult, op1=ALU.add))
                link(e, e.tensor_tensor(MCB[:, :], GS[:, 6, :], GS[:, 10, :], ALU.add))
            at("vector", "top2", p, top2)

            def rank(e):
                e.wait_ge(S["gch"], 18 * p + 18)
                if p == 0:
                    e.wait_ge(S["c16"], 16)
                bank_free(e, "LB", ("rank", p, 0))
                e.matmul(LB[:, 0:P], LOWER, MCB[:, :], start=True, stop=False, skip_group_check=True)
                for t in range(TPS):
                    m = MCB[:, t * NE:(t + 1) * NE]
                    mm = e.matmul(LB[:, P:P + NE], ONES16, m, start=False, stop=(t == TPS - 1),
                                  skip_group_check=True)
                    if t < TPS - 1:
                        k = TPS - 1 - t
                        e.matmul(LB[:, (t + 1) * NE:P].rearrange("p (t e) -> p t e", e=NE), ONES16,
                                 m.unsqueeze(1).broadcast_to([P, k, NE]), start=False, stop=(t == TPS - 2),
                                 skip_group_check=True)
                mm.then_inc(S["rank"], 1)
            at("tensor", "rank", p, rank)

            def place(e):
                k = [18 * p]

                def link(ins):
                    k[0] += 1
                    ins.then_inc(S["pl"], 1)
                    e.wait_ge(S["pl"], k[0])
                e.wait_ge(S["rank"], p + 1)
                if p == 0:
                    e.wait_ge(S["mag"], 3)
                chosen = LB[:, P:P + NE]
                link(e.tensor_scalar(SM[:, 0:8], chosen, 63.5, 1.0 / P, ALU.add, ALU.mult))
                link(e.tensor_scalar(SM[:, 8:16], SM[:, 0:8], MAGIC, None, ALU.add))
                link(e.tensor_scalar(PB[:, 0, 4:12], SM[:, 8:16], MAGIC, float(P), ALU.subtract, ALU.mult))
                for i, d in enumerate((1, 2, 4)):
                    link(e.tensor_tensor(PB[:, i + 1, 4:12], PB[:, i, 4:12], PB[:, i, 4 - d:12 - d], ALU.add))
                start = PB[:, 3, 3:11].unsqueeze(1).broadcast_to([P, TPS, NE])
                link(e.tensor_tensor(r(0), LB[:, 0:P].rearrange("p (t e) -> p t e", e=NE), start, ALU.add))
                for j, m in ((0, 6), (1, 10)):
                    link(e.tensor_tensor(r(4 + j), r(0), r(m), ALU.mult))
                    link(e.tensor_reduce(POSF[:, j, :], r(4 + j), AX.X, ALU.add))
                link(e.tensor_scalar(ROW[:, 0, :, :], POSF[:, :, :], -63.5, 1.0 / P, ALU.add, ALU.mult))
                link(e.tensor_scalar(ROW[:, 2, :, :], ROW[:, 0, :, :], MAGIC, None, ALU.add))
                link(e.tensor_scalar(ROW[:, 0, :, :], ROW[:, 2, :, :], MAGIC, float(P), ALU.subtract, ALU.mult))
                link(e.tensor_tensor(ROW[:, 1, :, :], POSF[:, :, :], ROW[:, 0, :, :], ALU.subtract))
                e.tensor_copy(POS[:, p, :, :], POSF[:, :, :]).then_inc(S["pos"], 1)
                v = GS[:, 7:10, :].rearrange("p a b -> p (a b)")[:, 0:STILES * NE].rearrange("p (i e) -> p i e", e=NE)
                link(e.tensor_tensor(v, PB[:, 3, 4:12].unsqueeze(1).broadcast_to([P, STILES, NE]),
                                     SLOT0.unsqueeze(2).broadcast_to([P, STILES, NE]), ALU.is_le))
                link(e.tensor_reduce(EXF[:, 0, :], v, AX.X, ALU.add))
                link(e.tensor_scalar(EXF[:, 1, :], EXF[:, 0, :], float(NE - 1), float(EW), ALU.min, ALU.mult))
                e.tensor_copy(EX[:, p, :], EXF[:, 1, :]).then_inc(S["ext"], 1)
                assert k[0] == 18 * (p + 1)
            at("vector", "place", p, place)

            def hot_lane(e, i):
                n = 8 * p + i
                k, t = divmod(4 * i, TPS)
                if i == 0:
                    e.wait_ge(S["pos"], p + 1)
                if n >= 2:
                    e.wait_ge(S["tab"], n - 1)
                for j in range(4):
                    ins = e.tensor_scalar(HOTL[:, n % 2, j, :], LANE, ROW[:, 1, k, t + j:t + j + 1], None, ALU.is_equal)
                ins.then_inc(S["hotl"], 1)

            def hot(e, i):
                n = 8 * p + i
                k, t = divmod(4 * i, TPS)
                if i == 0:
                    e.wait_ge(S["ext"], p + 1)
                if n >= 2:
                    e.wait_ge(S["tab"], n - 1)
                ht = GS_HOT[:, n % 2, :, :, :]
                e.tensor_tensor(ht[:, :, 1, :], ROW[:, 0, k, t:t + 4].unsqueeze(2).broadcast_to([P, 4, STILES]),
                                SLOT0.unsqueeze(1).broadcast_to([P, 4, STILES]), ALU.is_equal).then_inc(S["hot"], 1)
                e.wait_ge(S["hot"], 3 * n + 1)
                e.tensor_tensor(ht[:, :, 0, :], ht[:, :, 1, :],
                                TOKEN[:, k, t:t + 4].unsqueeze(2).broadcast_to([P, 4, STILES]), ALU.mult)\
                 .then_inc(S["hot"], 1)
                e.wait_ge(S["hot"], 3 * n + 2)
                e.tensor_tensor(ht[:, :, 1, :], ht[:, :, 1, :],
                                G4[:, p, 2 * k, t:t + 4].unsqueeze(2).broadcast_to([P, 4, STILES]), ALU.mult)\
                 .then_inc(S["hot"], 1)

            tv = LB[:, 0:2 * STILES]

            def sum_up(e, i):
                n = 8 * p + i
                e.wait_ge(S["hot"], 3 * n + 3)
                e.wait_ge(S["hotl"], n + 1)
                if i == 0:
                    bank_free(e, "LB", ("sum", p, 0))
                for j in range(4):
                    mm = e.matmul(tv, HOTL[:, n % 2, j, :], GS_HOT[:, n % 2, j, :, :].rearrange("p a n -> p (a n)"),
                                  start=(4 * i + j == 0), stop=(4 * i + j == 2 * TPS - 1))
                mm.then_inc(S["tab"], 1)

            def slot_out(e):
                e.wait_ge(S["tab"], 8 * p + 8)
                e.tensor_copy(SLOT[:, p, :], LB[:, 0:STILES]).then_inc(S["slt"], 1)
                e.tensor_copy(SLOTS[:, p, :], LB[:, STILES:2 * STILES]).then_inc(S["slt"], 1)
            for i in range(8):
                at("gpsimd", "hot_lane", p, lambda e, i=i: hot_lane(e, i), i)
                at("vector", "hot", p, lambda e, i=i: hot(e, i), i)
                at("tensor", "sum", p, lambda e, i=i: sum_up(e, i), i)
            at("vector", "slot_out", p, slot_out)

        first = {}

        def plan_pair(r):
            p, i = divmod(r, SPAIRS)
            s = PLACE[False, r]
            tiles = min(2, STILES - 2 * i)
            rows = slice(2 * i * P, (2 * i + tiles) * P)
            n = tiles * P

            def load_slots(e):
                if i == 0:
                    for b in range(BPS):
                        e.wait_ge(s_hd[BPS * p + b], 16)
                    e.wait_ge(S["slt"], 2 * p + 2)
                if r == 0:
                    e.wait_ge(S["wt"], 6)
                if r >= 2:
                    e.wait_ge(S["xt"], r - 1)
                for c in range(tiles):
                    e.indirect_dma_start(XIN[:, r % 2, c, :], None, hd[p],
                                         bass.IndirectOffsetOnAxis(ap=SLOT[:, p, 2 * i + c:2 * i + c + 1], axis=0))\
                     .then_inc(s_xi[r % 2], 16)
            at("gpsimd", "load_slots", r + 0, load_slots)

            arrived = 16 * sum(min(2, STILES - 2 * (q % SPAIRS)) for q in range(r % 2, r + 1, 2))

            def expert_numbers(e):
                if i == 0:
                    e.wait_ge(S["ext"], p + 1)
                a, b = 2 * i, min(2 * i + LD, STILES)
                _, got = nc.values_load_multi_w_load_instructions(
                    EX[0:1, p, a:b], engines=[mybir.EngineType.PE], min_val=0, max_val=(NE - 1) * EW,
                    skip_runtime_bounds_check_because="place() takes the minimum with the last expert's column")
                first.update({(p, a + j): v for j, v in enumerate(got)})

            def xt(e):
                e.wait_ge(s_xi[r % 2], arrived)
                bank_free(e, "TR", ("xt", r, 0))
                for k in range(2):
                    for c in range(tiles):
                        mm = e.transpose(TR[:, k * 256 + c * P:k * 256 + (c + 1) * P],
                                         XIN[:, r % 2, c, k * P:(k + 1) * P], IDENT)
                mm.then_inc(S["xt"], 1)
                if 2 * i % LD == 0:
                    expert_numbers(e)
            at("tensor", "xt", r + 0, xt)

            trv = TR[:, :].rearrange("p (k n) -> p k n", k=2)[:, :, 0:n]

            def xt_hi(e):
                e.wait_ge(S["xt"], r + 1)
                if r >= 2:
                    e.wait_ge(S["a"], PLACE[False, r - 2] + 1)
                e.activation(XSH[:, r % 2, :, 0:n], trv, ACT.Copy).then_inc(S["xth"], 1)
            at("scalar", "xt_hi", r + 0, xt_hi)

            def xt_lo(e):
                e.wait_ge(S["xth"], r + 1)
                e.tensor_tensor(XSL[:, r % 2, :, 0:n], trv, XSH[:, r % 2, :, 0:n].bitcast(F32), ALU.subtract)\
                 .then_inc(S["xtl"], 1)
            at("vector", "xt_lo", r + 0, xt_lo)

            def up(e):
                if r == 0:
                    e.wait_ge(S["wl"], NE + 2)
                e.wait_ge(S["xtl"], r + 1)
                e.wait_ge(S["t3"], s - 1)
                for c in range(tiles):
                    n = 0
                    for k in range(2):
                        cols = bass.ds(first[p, 2 * i + c] + (C_E + k * 256), 256)
                        for w, v in ((WH, XSH), (WH, XSL), (WL, XSH)):
                            mm = e.matmul(UP[s % 2][:, c * 256:c * 256 + 256], v[:, r % 2, k, c * P:(c + 1) * P],
                                          w[:, cols], start=(n == 0), stop=(n == 5))
                            n += 1
                mm.then_inc(S["a"], 1)
            at("tensor", "up", r + 1, up)

            score = [SLOTS[:, p, 2 * i + c:2 * i + c + 1] for c in range(tiles)]
            upv = UP[s % 2][:, :].rearrange("p (c a n) -> p c a n", c=2, a=2)[:, 0:tiles, :, :]
            tv = T[:, s % 3, 0:n].rearrange("p (c n) -> p c n", c=tiles)

            def silu(e):
                e.wait_ge(S["a"], s + 1)
                e.wait_ge(S["hl"], s - 2)
                for c in range(tiles):
                    ins = e.activation(tv[:, c, :], upv[:, c, 0, :], ACT.Silu, scale=score[c])
                ins.then_inc(S["sil"], 1)
            at("scalar", "silu", r + 1, silu)

            def times3(e):
                e.wait_ge(S["sil"], s + 1)
                for c in range(tiles):
                    ins = e.scalar_tensor_tensor(out=tv[:, c, :], in0=upv[:, c, 1, :], scalar=score[c], in1=tv[:, c, :],
                                                 op0=ALU.mult, op1=ALU.mult)
                ins.then_inc(S["t3"], 1)
            at("vector", "times3", r + 1, times3)

            hb = HT2[:, 0:n]

            def ht(e):
                e.wait_ge(S["t3"], s + 1)
                bank_free(e, "HT2", ("ht", r + 1, 0))
                for c in range(tiles):
                    mm = e.transpose(hb[:, c * P:(c + 1) * P], T[:, s % 3, c * P:(c + 1) * P], IDENT)
                mm.then_inc(S["ht"], 1)
            at("tensor", "ht", r + 1, ht)

            def h_hi(e):
                e.wait_ge(S["ht"], r + 1)
                e.wait_ge(S["acc"], s - 2)
                e.activation(HH[:, s % 3, 0:n], hb, ACT.Copy).then_inc(S["hh"], 1)
            at("scalar", "h_hi", r + 2, h_hi)

            def h_lo(e):
                e.wait_ge(S["hh"], s + 1)
                e.tensor_tensor(HL[:, s % 3, 0:n], hb, HH[:, s % 3, 0:n].bitcast(F32), ALU.subtract)\
                 .then_inc(S["hl"], 1)
            at("vector", "h_lo", r + 2, h_lo)

            def down(e):
                e.wait_ge(S["hl"], s + 1)
                down_free(e, s)
                for c in range(tiles):
                    cols = bass.ds(first[p, 2 * i + c] + (C_E + 512), 256)
                    for j, (hh, w) in enumerate(((HH, WH), (HL, WH), (HH, WL))):
                        mm = e.matmul(DN[:, c * D:(c + 1) * D], hh[:, s % 3, c * P:(c + 1) * P],
                                      w[:, cols], start=(j == 0), stop=(j == 2))
                mm.then_inc(S["acc"], 1)
            at("tensor", "down", r + 2, down)

            def y_out(e):
                e.wait_ge(S["acc"], s + 1)
                if r == 0:
                    e.wait_ge(S["wt"], 6)
                if r >= 2:
                    e.wait_ge(s_y[r % 2], 16 * (r // 2))
                e.activation(YS[:, r % 2, 0:tiles, :], DN[:, 0:tiles * D].rearrange("p (c d) -> p c d", c=tiles),
                             ACT.Copy).then_inc(S["ye"], 1)
            at("scalar", "y_out", r + 2, y_out)

            def y_put(e):
                e.wait_ge(S["ye"], r + 1)
                e.dma_start(ys[p][rows, :].rearrange("(c q) d -> q c d", q=P), YS[:, r % 2, 0:tiles, :])\
                 .then_inc(s_y[r % 2], 16)
            at("sync", "y_put", r + 2, y_put)

        def plan_collect(p):
            for t in range(TPS):
                tt = TPS * p + t
                q, n = tt % 4, tt // 4

                def collect(e, k, t=t, tt=tt, q=q, n=n):
                    if k == 0:
                        if t == 0:
                            for j in range(2):
                                e.wait_ge(s_y[j], 16 * ((SPAIRS * (p + 1) + 1 - j) // 2))
                        e.wait_ge(S["x1s"], tt // 2 + 1)
                        if n > 0:
                            e.wait_ge(s_g[0][q], 16 * n)
                    else:
                        e.wait_ge(s_g[0][q], 16 * (n + 1))
                        if n > 0:
                            e.wait_ge(s_g[1][q], 16 * n)
                    e.indirect_dma_start(X1[:, tt, :], None, ys[p],
                                         bass.IndirectOffsetOnAxis(ap=POS[:, p, k, t:t + 1], axis=0),
                                         compute_op=ALU.add).then_inc(s_g[k][q], 16)
                at("gpsimd", "collect", p, lambda e, f=collect: f(e, 0))
                at("gpsimd", "collect2", p, lambda e, f=collect: f(e, 1))

        def clear_bd(e):
            e.wait_ge(S["xl"], NBLK)
            e.memset(BD, 0.0).then_inc(S["bdz"], 1)
        at("gpsimd", "clear_bd", 1, clear_bd)

        def plan_layer2(b):
            x1 = X1[:, 2 * b:2 * b + 2, :]
            blk, pr, bt = b // 2, b // 2 % 2, 2 * (b % 2)
            ss = SET[b]
            P1H, P1L, R, U, Q1T, Q2, ST = SETS[ss]
            (pa, pa_name), (pc, pc_name) = BANKS[ss]
            QF = U[:, 0:2, :]
            UF = U[:, :, :].rearrange("p (t c) n -> p t (c n)", t=2)
            Q1 = Q2[:, :, 0:D]
            Q2T = U[:, 2:4, :].rearrange("p a b -> p (a b)").bitcast(BF16).rearrange("p (c t) -> p c t", c=4)
            before = [c for c in range(b) if SET[c] == ss]
            pv = before[-1] + 1 if before else 0

            split = len([c for c in range(b) if c not in NATIVE])

            def st(i):
                return ST[:, i, :]

            def load_bd(e):
                if blk == 0:
                    e.wait_ge(S["gw"], 16)
                    e.wait_ge(S["bdz"], 1)
                if blk >= 2:
                    e.wait_ge(S["y"], 2 * (blk - 1))
                src = gd[16 * blk:16 * blk + 16, :].rearrange("(t j) (c d) -> j c t d", j=4, c=32)
                for j in range(4):
                    s32 = slice(32 * j, 32 * j + 32)
                    e.dma_start(BD[s32, pr, :, s32], src[j]).then_inc(s_bd[pr], 16)
            if b % 2 == 0:
                at("sync", "load_bd", b, load_bd)

            def mix(e):
                for t in (2 * b, 2 * b + 1):
                    e.wait_ge(s_g[1][t % 4], 16 * (t // 4 + 1))
                e.wait_ge(s_bd[pr], 64 * (blk // 2 + 1))
                if pv:
                    e.wait_ge(S["g"], 2 * pv)
                bank_free(e, pa_name, ("mix", b, 0))
                for k in range(2):
                    for t in range(2):
                        mm = e.matmul(pa[:, k * 256 + t * P:k * 256 + (t + 1) * P], x1[:, t, k * P:(k + 1) * P],
                                      BD[:, pr, bt + t, :], start=True, stop=True)
                mm.then_inc(S["y"], 1)

            yv = pa[:, :].rearrange("p (k t) -> p k t", k=2)

            def y_hi(e):
                e.wait_ge(S["y"], b + 1)
                if pv:
                    e.wait_ge(S["g"], 2 * pv)
                elif ss < 2:
                    e.wait_ge(S["a"], PLACE[True, NSH - 1] + 1)
                    e.wait_ge(S["gate"], NBLK)
                    e.wait_ge(S["tk"], 2 * NBLK)
                else:
                    e.wait_ge(S["acc"], NST)
                e.activation(P1H[:, 0:2, :], yv, ACT.Copy).then_inc(S["yh"], 1)

            def y_out(e):
                e.wait_ge(S["y"], b + 1)
                if pv:
                    e.wait_ge(S["bf"], 2 * pv)
                elif ss < 2:
                    for c in range(BPS, NBLK):
                        e.wait_ge(s_hd[c], 16)
                else:
                    for c in range(8):
                        e.wait_ge(s_o[c], 16)
                e.activation(R[:, 0:2, :], yv, ACT.Copy).then_inc(S["yh"], 1)

            def y_lo(e):
                e.wait_ge(S["yh"], b + 1)
                e.tensor_tensor(P1L[:, 0:2, :], yv, P1H[:, 0:2, :].bitcast(F32), ALU.subtract).then_inc(S["yl"], 1)
            at("tensor", "mix", b, mix)
            native = b in NATIVE
            at("scalar", "y_hi", b, y_out if native else y_hi)
            if not native:
                at("vector", "y_lo", b, y_lo)

            def had1(e):
                if native:
                    e.wait_ge(S["yh"], b + 1)
                else:
                    e.wait_ge(S["yl"], split + 1)
                if b == 0:
                    e.wait_ge(S["had2"], 4)
                bank_free(e, pa_name, ("had1", b, 0))
                for t in range(2):
                    n = 0
                    if native:
                        for k in range(2):
                            mm = e.matmul(pa[:, t * D:(t + 1) * D], R[:, k, t * P:(t + 1) * P], HADP[k],
                                          start=(k == 0), stop=(k == 1))
                        continue
                    for k in range(2):
                        for src in (P1H, P1L):
                            mm = e.matmul(pa[:, t * D:(t + 1) * D], src[:, k, t * P:(t + 1) * P],
                                          HAD2[:, k, :, :].rearrange("p a n -> p (a n)"),
                                          start=(n == 0), stop=(n == 3))
                            n += 1
                mm.then_inc(S["f"], 1)

            def stats1(e):
                k = 7 * b
                e.wait_ge(S["f"], b + 1)
                if b > 0:
                    e.wait_ge(S["st1"], k)
                if pv:
                    e.wait_ge(S["st2"], 6 * pv)
                e.tensor_reduce(st(0), pa[:, :].rearrange("p (t d) -> p t d", t=2),
                                AX.X, ALU.max, apply_absolute_value=True).then_inc(S["st1"], 1)
                e.wait_ge(S["st1"], k + 1)
                e.tensor_scalar(st(1), st(0), 1.0 / 16, EPS, ALU.mult, ALU.max).then_inc(S["st1"], 1)
                e.wait_ge(S["st1"], k + 2)
                e.reciprocal(st(2), st(1)).then_inc(S["st1"], 1)
                e.wait_ge(S["st1"], k + 3)
                e.tensor_scalar(st(3), st(2), QB, 1.0 / 16, ALU.mult, ALU.mult).then_inc(S["st1"], 1)

            def stats1_value(e):
                k = 7 * b
                e.wait_ge(S["st1"], k + 4)
                if b == 0:
                    e.wait_ge(S["sw"], 1)
                e.tensor_scalar(st(4), st(1), 1.0 / QB, SW[:, 2:3], ALU.mult, ALU.mult).then_inc(S["st1"], 1)
                e.wait_ge(S["st1"], k + 5)
                e.tensor_tensor(st(5), st(4), st(4), ALU.mult).then_inc(S["st1"], 1)
                e.wait_ge(S["st1"], k + 6)
                e.tensor_scalar(st(6), st(5), float(HID) ** -0.5, None, ALU.mult).then_inc(S["st1"], 1)

            def round1(e, t):
                e.wait_ge(S["st1"], 7 * b + 4)
                if t == 0 and pv:
                    e.wait_ge(S["q2"], pv)
                elif t == 0 and ss < 2:
                    for c in range(BPS, NBLK):
                        e.wait_ge(s_hd[c], 16)
                elif t == 0:
                    for c in range(8):
                        e.wait_ge(s_o[c], 16)
                if t == 0 and b == 0:
                    e.wait_ge(S["mag"], 2)
                e.activation(QF[:, t, :], pa[:, t * D:(t + 1) * D], ACT.Identity,
                             bias=MAG[:, 0:1], scale=st(3)[:, t:t + 1]).then_inc(S["qf"], 1)

            def quant1(e):
                e.wait_ge(S["qf"], 2 * b + 2)
                if pv:
                    e.wait_ge(S["q2t"], pv)
                elif ss < 2:
                    e.wait_ge(S["tab"], 8 * NSB)
                else:
                    e.wait_ge(S["acc"], NST)
                e.tensor_scalar(Q1, QF, MAGIC, None, ALU.subtract).then_inc(S["q1"], 1)
            at("tensor", "had1", b, had1)
            at("vector", "stats1", b, stats1)
            at("vector", "stats1_value", b, stats1_value)
            for t in range(2):
                at("scalar", "round1", b, lambda e, t=t: round1(e, t), t)
            at("vector", "quant1", b, quant1)

            turned1 = pa[:, 0:256].bitcast(BF16).rearrange("p (k t) -> p k t", k=2)

            def turn1(e):
                e.wait_ge(S["q1"], b + 1)
                if b == 0:
                    e.wait_ge(S["c16"], 16)
                bank_free(e, pa_name, ("turn1", b, 0))
                for t in range(2):
                    for k in range(2):
                        mm = e.transpose(turned1[:, k, t * P:(t + 1) * P], Q1[:, t, k * P:(k + 1) * P], IDB)
                mm.then_inc(S["q1t"], 1)
            at("tensor", "turn1", b, turn1)

            def turn1_out(e):
                e.wait_ge(S["q1t"], b + 1)
                if pv:
                    e.wait_ge(S["up"], 2 * pv)
                elif ss < 2:
                    e.wait_ge(S["xal"], NBLK)
                else:
                    e.wait_ge(S["acc"], NST)
                e.activation(Q1T[:, :, :], turned1, ACT.Copy).then_inc(S["q1c"], 1)
            at("scalar", "turn1_out", b, turn1_out)

            both = ((pa, pa_name), (pc, pc_name))

            def wide(e, j):
                e.wait_ge(S["q1c"], b + 1)
                if b == 0:
                    e.wait_ge(S["wt"], 6)
                bank_free(e, both[j][1], ("wide", b, j))
                for c in (2 * j, 2 * j + 1):
                    for k in range(2):
                        mm = e.matmul(both[j][0][:, (c % 2) * 256:(c % 2 + 1) * 256], WU[:, k, c * P:(c + 1) * P],
                                      Q1T[:, k, :], start=(k == 0), stop=(k == 1))
                mm.then_inc(S["up"], 1)

            def relu(e, j):
                e.wait_ge(S["up"], 2 * b + j + 1)
                if j == 0 and native:
                    e.wait_ge(S["f"], b + 1)
                elif j == 0 and pv:
                    e.wait_ge(S["bf"], 2 * pv)
                elif j == 0 and ss < 2:
                    for c in range(BPS, NBLK):
                        e.wait_ge(s_hd[c], 16)
                elif j == 0:
                    for c in range(8):
                        e.wait_ge(s_o[c], 16)
                e.activation(R[:, 2 * j:2 * j + 2, :], both[j][0][:, :].rearrange("p (c t) -> p c t", c=2), ACT.Relu)\
                 .then_inc(S["rl"], 1)

            def square(e, j):
                e.wait_ge(S["rl"], 2 * b + j + 1)
                v = R[:, 2 * j:2 * j + 2, :]
                e.tensor_tensor(v, v, v, ALU.mult).then_inc(S["sq2"] if j else S["sq"], 1)
            for j in range(2):
                at("tensor", "wide", b, lambda e, j=j: wide(e, j), j)
                at("scalar", "relu", b, lambda e, j=j: relu(e, j), j)
            at("vector", "square", b, lambda e: square(e, 0))
            at("gpsimd", "square2", b, lambda e: square(e, 1))

            def stage(e, j):
                e.wait_ge(S["sq"], b + 1)
                e.wait_ge(S["sq2"], b + 1)
                e.wait_ge(S["q1"], b + 1)
                if pv:
                    e.wait_ge(S["dn"], pv)
                e.tensor_tensor(U[:, 2 * j:2 * j + 2, :], R[:, 0:2, :], R[:, 2:4, :],
                                ALU.subtract if j else ALU.add).then_inc(S["bf"], 1)
            for j in range(2):
                at("vector", "stage", b, lambda e, j=j: stage(e, j), j)

            def v_hi(e, j):
                e.wait_ge(S["bf"], 2 * b + 1 + j)
                e.wait_ge(S["f"], b + 1)
                e.activation(P1H[:, 2 * j:2 * j + 2, :], U[:, 2 * j:2 * j + 2, :], ACT.Copy).then_inc(S["vh"], 1)

            def v_lo(e, j):
                e.wait_ge(S["vh"], 2 * split + j + 1)
                e.tensor_tensor(P1L[:, 2 * j:2 * j + 2, :], U[:, 2 * j:2 * j + 2, :],
                                P1H[:, 2 * j:2 * j + 2, :].bitcast(F32), ALU.subtract).then_inc(S["vl2"] if j else S["vl"], 1)
            if not native:
                for j in range(2):
                    at("scalar", "v_hi", b, lambda e, j=j: v_hi(e, j), j)
                at("vector", "v_lo", b, lambda e: v_lo(e, 0))
                at("gpsimd", "v_lo2", b, lambda e: v_lo(e, 1))

            def had2(e, t):
                if native:
                    e.wait_ge(S["bf"], 2 * b + 2)
                else:
                    e.wait_ge(S["vl"], split + 1)
                    e.wait_ge(S["vl2"], split + 1)
                bank_free(e, both[t][1], ("had2", b, t))
                for half in range(2):
                    n = 0
                    if native:
                        for k in range(2):
                            mm = e.matmul(both[t][0][:, half * D:(half + 1) * D], U[:, 2 * half + k, t * P:(t + 1) * P],
                                          HADP[k], start=(k == 0), stop=(k == 1))
                        continue
                    for k in range(2):
                        for src in (P1H, P1L):
                            mm = e.matmul(both[t][0][:, half * D:(half + 1) * D], src[:, 2 * half + k, t * P:(t + 1) * P],
                                          HAD2[:, k, :, :].rearrange("p a n -> p (a n)"),
                                          start=(n == 0), stop=(n == 3))
                            n += 1
                mm.then_inc(S["g"], 1)

            def stats2(e):
                k = 6 * b
                if pv:
                    e.wait_ge(S["fin"], 2 * pv)
                for t in range(2):
                    e.wait_ge(S["g"], 2 * b + t + 1)
                    e.tensor_reduce(ST[:, 7, t:t + 1], both[t][0][:, :], AX.X, ALU.max,
                                    apply_absolute_value=True).then_inc(S["st2"], 1)
                e.wait_ge(S["st2"], k + 2)
                e.wait_ge(S["st1"], 7 * b + 7)
                e.tensor_tensor(st(8), st(7), st(6), ALU.mult).then_inc(S["st2"], 1)
                e.wait_ge(S["st2"], k + 3)
                e.tensor_scalar(st(9), st(8), EPS, 1.0 / QB, ALU.max, ALU.mult).then_inc(S["st2"], 1)
                e.wait_ge(S["st2"], k + 4)
                e.reciprocal(st(10), st(9)).then_inc(S["st2"], 1)
                e.wait_ge(S["st2"], k + 5)
                e.tensor_tensor(st(11), st(10), st(6), ALU.mult).then_inc(S["st2"], 1)

            def round2(e, t):
                e.wait_ge(S["st2"], 6 * b + 6)
                e.activation(UF[:, t, :], both[t][0][:, :], ACT.Identity, bias=MAG[:, 0:1],
                             scale=st(11)[:, t:t + 1]).then_inc(S["q2f"], 1)

            def quant2(e):
                e.wait_ge(S["q2f"], 2 * b + 2)
                e.tensor_scalar(Q2[:, :, :], UF, MAGIC, None, ALU.subtract).then_inc(S["q2"], 1)
            for t in range(2):
                at("tensor", "had2", b, lambda e, t=t: had2(e, t), t)
                at("scalar", "round2", b, lambda e, t=t: round2(e, t), t)
            at("vector", "stats2", b, stats2)
            at("vector", "quant2", b, quant2)

            turned2 = pa[:, :].bitcast(BF16).rearrange("p (c t) -> p c t", c=4)

            def turn2(e):
                e.wait_ge(S["q2"], b + 1)
                bank_free(e, pa_name, ("turn2", b, 0))
                for t in range(2):
                    for c in range(4):
                        mm = e.transpose(turned2[:, c, t * P:(t + 1) * P], Q2[:, t, c * P:(c + 1) * P], IDB)
                mm.then_inc(S["q2t"], 1)

            def turn2_out(e):
                e.wait_ge(S["q2t"], b + 1)
                e.activation(Q2T, turned2, ACT.Copy).then_inc(S["q2c"], 1)

            def narrow(e):
                e.wait_ge(S["q2c"], b + 1)
                bank_free(e, pa_name, ("narrow", b, 0))
                for t in range(2):
                    for c in range(4):
                        mm = e.matmul(pa[:, t * D:(t + 1) * D], Q2T[:, c, t * P:(t + 1) * P],
                                      WD[:, c, :], start=(c == 0), stop=(c == 3))
                mm.then_inc(S["dn"], 1)

            def finish_scale(e):
                e.wait_ge(S["st2"], 6 * b + 6)
                if pv:
                    e.wait_ge(S["fin"], 2 * pv)
                e.tensor_scalar(st(12), st(9), SW[:, 3:4], None, ALU.mult).then_inc(S["fs"], 1)

            def finish(e):
                e.wait_ge(S["fs"], b + 1)
                e.wait_ge(S["dn"], b + 1)
                for t in range(2):
                    e.scalar_tensor_tensor(out=x1[:, t, :], in0=pa[:, t * D:(t + 1) * D],
                                           scalar=st(12)[:, t:t + 1], in1=x1[:, t, :],
                                           op0=ALU.mult, op1=ALU.add).then_inc(S["fin"], 1)
            at("tensor", "turn2", b, turn2)
            at("scalar", "turn2_out", b, turn2_out)
            at("tensor", "narrow", b, narrow)
            at("vector", "finish_scale", b, finish_scale)
            at("vector", "finish", b, finish)

            def store(e):
                e.wait_ge(S["fin"], 2 * b + 2)
                e.dma_start(out[b * 256:(b + 1) * 256, :].rearrange("(t p) d -> p t d", p=P), x1).then_inc(s_o[b], 16)
            at("sync", "store", b, store)

        def uses():
            table = []

            def use(bank, row, name, i, reader, count):
                table.append((bank, when[(name, row, i)], (name, row, i), reader, count))

            table.append(("AUX0", when[("weight_total", 0, 0)], ("weight_total", 0, 0), "sw", 1))
            for p in range(NSB):
                use("LB", p, "rank", 0, "pl", 18 * p + 7)
                use("LB", p, "sum", 0, "slt", 2 * p + 2)
            for r in range(NSB * SPAIRS):
                use("TR", r + 0, "xt", 0, "xtl", r + 1)
                use("HT2", r + 1, "ht", 0, "hl", PLACE[False, r] + 1)
            for b in range(NBLK):
                use("TR", b, "xa", 0, "xam", b + 1)
                for k in range(2):
                    use("HT2", b, "tok", k, "tko", 2 * b + k + 1)
                use("AUX0", b, "gate", 0, "glf", b + 1)
                for k in range(2):
                    use(f"AUX{k}", b, "h0w", k, "h0l", 2 * b + k + 1)
            for b in range(2 * NBLK):
                banks = [n for _, n in BANKS[SET[b]]]
                split = len([c for c in range(b) if c not in NATIVE])
                use(banks[0], b, "mix", 0, *(("yh", b + 1) if b in NATIVE else ("yl", split + 1)))
                use(banks[0], b, "had1", 0, "qf", 2 * b + 2)
                use(banks[0], b, "turn1", 0, "q1c", b + 1)
                use(banks[0], b, "turn2", 0, "q2c", b + 1)
                use(banks[0], b, "narrow", 0, "fin", 2 * b + 2)
                for k in range(2):
                    use(banks[k], b, "wide", k, "rl", 2 * b + k + 1)
                    use(banks[k], b, "had2", k, "q2f", 2 * b + k + 1)
            return table

        BANKS = [((AUX[0], "AUX0"), (LB, "LB")), ((AUX[1], "AUX1"), (LB, "LB")),
                 ((UP[0], "UP0"), (TR, "TR")), ((UP[1], "UP1"), (HT2, "HT2"))]
        FROM_STEPS = {"UP0": ("t3", NST), "UP1": ("t3", NST), "TR": ("xtl", NSB * SPAIRS), "HT2": ("hl", NST)}
        done = 0
        for b in range(NBLK):
            plan_adapter(b)
            if b % BPS == BPS - 1:
                plan_route(b // BPS)
            more = PAIRS_AFTER[b] if b < NBLK - 1 else NSB * SPAIRS - done
            for r in range(done, done + more):
                plan_pair(r)
            done += more
        for p in range(NSB):
            plan_collect(p)
        for b in range(2 * NBLK):
            plan_layer2(b)

        last_reader = {}
        lists = {}
        for bank, t, key, reader, count in uses():
            lists.setdefault(bank, []).append((t, key, reader, count))
        for bank, lst in lists.items():
            lst.sort()
            for prev, this in zip(lst, lst[1:]):
                last_reader[(bank, this[1])] = prev[2:]
            later = [v[1] for v in lst if v[1][0] not in ("xa", "xt", "tok", "ht")]
            if bank in FROM_STEPS:
                last_reader[(bank, later[0])] = FROM_STEPS[bank]

        def bank_free(e, bank, key):
            got = last_reader.get((bank, key))
            if got:
                e.wait_ge(S[got[0]], got[1])

        def last(e):
            for b in range(2 * NBLK):
                e.wait_ge(s_o[b], 16)
            e.wait_ge(S["gw"], 16)
            for b in range(NBLK):
                e.wait_ge(s_hd[b], 16)
            for j in range(2):
                e.wait_ge(s_y[j], 16 * ((NSB * SPAIRS + 1 - j) // 2))
        put("sync", 10000, last)

        block = ctx.enter_context(nc.Block())

        def run(engine, e):
            for _, _, fn in sorted(plan[engine], key=lambda v: v[:2]):
                fn(e)

        @block.sync
        def _(e):
            run("sync", e)

        @block.gpsimd
        def _(e):
            run("gpsimd", e)

        @block.scalar
        def _(e):
            run("scalar", e)

        @block.vector
        def _(e):
            run("vector", e)

        @block.tensor
        def _(e):
            run("tensor", e)


def kernel(x, itok_B_0_6, itok_B_1_198, L0_cond_W, L0_cond_A, L0_cond_Bm, L0_cond_scalings, L0_ffn_gate_w,
           L0_ffn_w1, L0_ffn_w2, L0_ffn_w3, L0_ffn_ws1, L0_ffn_ws2, L0_ffn_ws3, L1_cond_weights,
           L1_ffn_w_up, L1_ffn_w_down):
    import numpy as np
    import concourse.bacc as bacc
    from concourse import mybir as mb
    from concourse.bass_utils import run_bass_kernel_spmd

    consts = np.zeros((128, 728), np.float32)
    consts[:, 0:128] = np.eye(128)
    had = np.ones((1, 1), np.float32)
    while had.shape[0] < 128:
        had = np.block([[had, had], [had, -had]])
    consts[:, 128:256] = had
    consts[:, 256:264] = 8 - np.arange(8)
    consts[:, 264] = np.arange(128) // 16
    consts[:, 265:265 + STILES] = 128 * np.arange(STILES)
    consts[:, 568:696] = np.arange(128)
    for k in range(2):
        consts[:, 696 + k * TPS:696 + (k + 1) * TPS] = np.arange(128)[:, None] + 128 * np.arange(TPS)
    consts[:, 312:440], consts[:, 440:568] = had, -had
    consts16 = np.zeros((128, 3, 128), mb.dt.np(mb.dt.bfloat16))
    consts16[:, 0, :] = np.triu(np.ones((128, 128)), 1)
    consts16[:, 1, :] = 1
    consts16[:, 2, :] = np.eye(128)

    def wide(a, k):
        return np.asarray(a).T.reshape(k, 128, -1).transpose(1, 0, 2)

    def pair(a, b):
        return np.concatenate([wide(a, 2), wide(b, 2)], axis=2).reshape(128, 512)

    w1, w2, w3 = np.asarray(L0_ffn_w1), np.asarray(L0_ffn_w2), np.asarray(L0_ffn_w3)
    x2 = np.asarray(x).reshape(4096, 256)
    ins = [
        ("xT", x2.T), ("x", x2),
        ("adapter", np.asarray(itok_B_0_6)), ("cond", np.asarray(itok_B_1_198)),
        ("WA", np.concatenate([
            wide(L0_cond_W, 2).reshape(128, 512), wide(np.asarray(L0_cond_A).reshape(128, 256), 2).reshape(128, 256),
            np.asarray(L0_cond_Bm).transpose(0, 2, 1).reshape(128, 256), wide(L0_ffn_gate_w, 2).reshape(128, 16),
            pair(L0_ffn_ws1, L0_ffn_ws3), np.asarray(L0_ffn_ws2).T], axis=1)),
        ("WE", np.stack([np.concatenate([pair(w1[i], w3[i]), w2[i].T], axis=1) for i in range(8)])),
        ("scal", np.repeat(np.asarray(L0_cond_scalings), 16).reshape(128, 1)),
        ("cw", np.asarray(L1_cond_weights).reshape(200, 1024)),
        ("wuT", np.asarray(L1_ffn_w_up).T), ("wdT", np.asarray(L1_ffn_w_down).T),
        ("consts", consts), ("consts16", consts16),
    ]
    nc = bacc.Bacc("TRN2", target_bir_lowering=False, num_devices=1)
    arrays, args = {}, []
    for name, a in ins:
        a = np.ascontiguousarray(a)
        arrays["in_" + name] = a
        args.append(nc.dram_tensor("in_" + name, a.shape, mb.dt.from_np(a.dtype), kind="ExternalInput").ap())
    out = nc.dram_tensor("out_0", (4096, 256), mb.dt.float32, kind="ExternalOutput").ap()
    adapter_moe_quant_ffn(nc, *args, out)
    r = run_bass_kernel_spmd(nc, [arrays], core_ids=[0])
    return r.results[0]["out_0"].reshape(128, 32, 256)
```

```python
from contextlib import ExitStack

import concourse.bass as bass
from concourse import mybir

F32 = mybir.dt.float32
F32R = mybir.dt.float32r
BF16 = mybir.dt.bfloat16
I32 = mybir.dt.int32
ALU = mybir.AluOpType
ACT = mybir.ActivationFunctionType
AX = mybir.AxisListType

P = 128
NT = 4096
TB = 512
NBLK = NT // TB
NSB = 2
BPS = NBLK // NSB
TPS = 4 * BPS
NE = 8
STILES = 2 * TPS + NE - 1
SPAIRS = (STILES + 1) // 2
NSH = 2 * NBLK
NST = NSH + NSB * SPAIRS
D = 256
HID = 512
MAGIC = 12582912.0
EPS = 1e-5
SAT = 17.4
QB = 127.0

C_W, C_A, C_B, C_G, C_S, C_E = 0, 512, 768, 1024, 1040, 1808
EW = 768
C_END = C_E + NE * EW

TIME = {
    "load_expert": [6.40, 6.46, 23.51, 23.57, 31.40, 31.46, 31.52, 33.64],
    "load_wq": [37.87],
    "stash": [12.10],
    "split_hi": [5.74, 8.53, 22.35, 23.54, 30.90, 31.63, 37.42, 38.16, 39.26, 40.96],
    "split_lo": [6.85, 9.45, 23.24, 25.00, 31.78, 35.84, 38.31, 42.37, 44.13, 45.89],
    "gate_weights": [10.51],
    "make_mask": [8.53],
    "make_identity": [7.99],
    "weight_sums": [44.06],
    "weight_total": [51.39],
    "ternary": [51.75],
    "clear_bd": [103.80],
    "load_x": [0.30, 0.36, 0.42, 0.48, 47.76, 47.82, 47.88, 48.23],
    "x_hi": [3.99, 21.10, 28.99, 35.52, 45.82, 62.34, 81.21, 88.69],
    "x_lo": [5.11, 22.22, 30.11, 36.63, 46.93, 68.55, 82.38, 91.68],
    "xa": [8.19, 23.73, 31.44, 38.05, 50.09, 70.81, 83.97, 93.01],
    "xam": [10.95, 25.20, 32.91, 39.66, 56.96, 79.61, 87.39, 94.48],
    "xa_hi": [11.73, 25.98, 33.69, 40.44, 57.74, 80.39, 88.17, 96.80],
    "xa_lo": [12.43, 26.67, 34.38, 41.13, 58.55, 81.18, 93.03, 97.64],
    "h0w": [
        10.78, 13.38, 26.22, 27.51, 32.74, 34.04, 42.65, 43.95, 59.56, 60.86, 77.62, 78.92, 85.79, 87.09, 99.67,
        103.34],
    "h0": [
        14.89, 15.54, 28.81, 29.46, 35.34, 35.99, 48.08, 48.73, 63.35, 64.68, 82.67, 83.32, 94.31, 94.96, 121.72,
        122.37],
    "h0_hi": [
        15.72, 16.37, 29.94, 30.42, 36.46, 36.94, 48.91, 49.56, 64.17, 65.51, 83.50, 84.15, 95.14, 95.79, 122.65,
        123.20],
    "h0_lo": [
        16.37, 17.02, 31.24, 31.84, 37.77, 38.37, 49.56, 50.21, 67.35, 67.95, 84.88, 85.49, 95.79, 96.44, 123.34,
        123.95],
    "h0_sum": [17.77, 33.54, 40.07, 64.83, 68.70, 87.10, 97.34, 125.76],
    "gate": [20.65, 39.35, 52.93, 56.94, 68.92, 96.59, 125.20, 132.76],
    "logits_lo": [25.28, 41.70, 55.00, 59.01, 74.31, 98.66, 127.27, 134.83],
    "logits": [25.80, 41.94, 56.53, 59.26, 77.17, 98.91, 127.52, 135.25],
    "tok": [
        23.25, 25.74, 62.87, 64.20, 65.54, 66.88, 68.44, 73.53, 75.07, 76.41, 89.74, 91.28, 102.86, 105.12, 152.27,
        153.61],
    "tok_out": [
        24.27, 26.50, 63.53, 64.86, 66.20, 67.54, 69.43, 74.39, 75.73, 77.07, 90.40, 91.94, 103.54, 105.78, 152.93,
        154.27],
    "hd_put": [27.08, 65.44, 68.12, 74.97, 77.64, 92.52, 106.36, 154.85],
    "s_up": [
        17.82, 19.24, 36.64, 41.24, 45.25, 46.67, 51.52, 54.82, 72.11, 81.26, 111.75, 113.91, 148.96, 150.38,
        181.86, 184.47],
    "s_silu": [
        19.42, 20.83, 38.89, 42.83, 46.85, 48.26, 53.11, 56.42, 73.71, 82.85, 114.55, 117.56, 150.56, 158.25,
        183.46, 187.73],
    "s_times3": [
        19.85, 21.27, 39.33, 43.27, 48.07, 48.70, 56.63, 80.21, 80.54, 95.08, 115.32, 118.00, 155.16, 159.63,
        183.89, 188.30],
    "s_h_hi": [
        20.37, 22.05, 40.00, 43.78, 48.58, 50.27, 57.14, 80.91, 82.16, 96.50, 124.16, 127.98, 159.83, 160.15,
        190.72, 191.03],
    "s_h_lo": [
        20.84, 24.02, 40.47, 46.33, 49.06, 50.81, 57.62, 82.05, 83.52, 98.24, 124.64, 128.45, 160.34, 160.67,
        191.44, 191.78],
    "s_down": [
        22.54, 25.03, 49.38, 56.24, 58.83, 62.16, 95.61, 98.96, 107.49, 115.57, 132.06, 134.89, 164.09, 166.94,
        193.38, 198.39],
    "s_out": [
        23.42, 25.91, 51.14, 57.95, 60.21, 93.63, 97.04, 100.39, 109.00, 116.44, 132.93, 135.77, 164.97, 168.59,
        194.85, 200.16],
    "load_xT": [6.34, 23.45, 31.34, 37.99, 48.17, 69.78, 83.62],
    "nonzero": [59.53, 137.51],
    "gate_silu": [60.22, 139.61],
    "top2": [60.81, 140.38],
    "rank": [67.38, 146.95],
    "place": [69.68, 149.24],
    "hot_lane": [
        75.60, 76.90, 78.30, 80.91, 81.78, 86.09, 89.08, 91.41, 157.13, 157.40, 161.72, 161.99, 170.94, 173.60,
        173.87, 176.21],
    "hot_lane2": [
        74.28, 75.44, 77.77, 80.89, 82.05, 85.94, 89.40, 90.56, 154.50, 155.66, 159.82, 163.06, 170.92, 172.08,
        173.23, 175.04],
    "hot": [
        75.87, 77.27, 78.57, 83.85, 86.36, 87.99, 89.35, 90.38, 156.09, 158.00, 162.25, 167.03, 171.21, 172.24,
        174.14, 175.18],
    "sum": [
        77.10, 80.22, 80.74, 85.27, 88.39, 89.22, 90.76, 91.91, 157.59, 159.23, 170.25, 170.77, 172.44, 174.37,
        175.60, 176.84],
    "slot_out": [92.81, 177.53],
    "load_slots": [
        93.18, 95.26, 99.64, 101.72, 105.27, 107.64, 111.90, 114.04, 118.32, 120.92, 123.68, 130.55, 136.23, 139.07,
        144.24, 152.42, 157.74, 160.98, 165.67, 168.27, 177.90, 179.98, 183.91, 186.51, 189.36, 191.87, 194.72,
        203.04, 209.28, 211.36, 216.56, 219.86, 231.52, 233.60, 237.76, 241.92, 245.22, 249.90, 258.40, 260.48],
    "xt": [
        98.48, 100.96, 104.64, 107.01, 111.27, 113.41, 117.69, 120.29, 123.05, 129.92, 135.60, 138.44, 143.61,
        151.79, 157.11, 159.83, 165.04, 167.64, 176.36, 178.55, 183.28, 185.88, 188.73, 191.24, 194.09, 197.91,
        200.02, 207.77, 215.36, 217.51, 221.29, 225.72, 236.36, 239.55, 243.76, 247.40, 252.16, 255.46, 265.91,
        274.89],
    "xt_hi": [
        99.14, 101.62, 105.30, 107.70, 111.93, 114.07, 118.35, 121.46, 125.65, 131.55, 136.26, 139.13, 144.27,
        152.45, 157.77, 163.36, 165.70, 168.30, 177.02, 178.97, 183.94, 187.05, 189.67, 191.90, 194.75, 198.57,
        200.68, 208.43, 216.06, 218.19, 221.95, 226.83, 237.35, 240.21, 245.17, 249.02, 252.82, 256.43, 268.46,
        275.78],
    "xt_lo": [
        99.79, 102.27, 105.95, 108.39, 112.58, 114.72, 119.00, 122.11, 126.35, 132.25, 136.91, 139.78, 147.25,
        155.49, 159.03, 164.15, 166.43, 169.19, 177.75, 179.41, 184.59, 187.70, 190.31, 192.55, 195.46, 199.22,
        201.33, 209.08, 216.71, 218.84, 222.60, 228.31, 238.12, 240.86, 246.60, 249.82, 254.66, 257.08, 269.78,
        276.28],
    "up": [
        101.44, 105.60, 108.20, 109.62, 116.27, 118.88, 123.78, 127.80, 130.40, 136.08, 140.07, 142.20, 155.69,
        160.31, 162.68, 165.52, 168.12, 172.96, 178.79, 180.21, 186.60, 189.33, 191.72, 194.57, 196.26, 201.67,
        204.03, 210.99, 218.43, 219.84, 226.91, 233.98, 240.03, 244.51, 248.85, 253.35, 260.57, 263.94, 270.58,
        276.82],
    "silu": [
        103.04, 107.19, 109.80, 112.41, 122.14, 125.15, 128.97, 131.05, 134.05, 137.68, 141.67, 147.43, 160.52,
        161.91, 164.27, 167.12, 169.72, 174.55, 180.39, 181.10, 190.22, 192.38, 193.32, 196.67, 197.85, 203.26,
        205.63, 212.59, 220.02, 223.65, 230.29, 238.74, 243.96, 248.25, 250.93, 257.45, 264.46, 266.18, 272.30,
        277.71],
    "times3": [
        103.71, 107.87, 110.47, 113.18, 122.82, 125.82, 129.64, 131.72, 134.72, 138.35, 147.85, 148.38, 161.19,
        163.29, 165.57, 168.07, 170.39, 176.48, 181.06, 181.59, 190.92, 193.15, 193.99, 197.34, 198.53, 203.94,
        206.30, 213.26, 221.24, 224.32, 230.97, 241.46, 244.72, 250.75, 255.26, 258.88, 265.13, 267.58, 273.06,
        278.13],
    "ht": [
        111.03, 113.17, 115.33, 120.77, 123.54, 131.82, 134.65, 138.20, 139.83, 148.01, 154.95, 158.91, 162.44,
        164.80, 172.00, 176.12, 178.25, 180.92, 186.36, 189.21, 193.14, 195.98, 197.67, 200.50, 203.79, 207.25,
        210.75, 215.84, 222.64, 225.48, 232.09, 246.81, 254.76, 258.68, 261.99, 266.39, 268.56, 272.55, 274.65,
        278.59],
    "h_hi": [
        111.45, 113.59, 116.45, 121.19, 130.10, 132.94, 135.78, 138.86, 140.43, 148.43, 155.37, 159.57, 163.09,
        165.22, 172.42, 176.54, 179.24, 181.35, 186.78, 189.51, 193.82, 196.40, 199.28, 202.33, 204.45, 207.91,
        213.09, 217.92, 223.38, 227.31, 232.51, 248.76, 256.17, 259.10, 264.96, 266.81, 269.42, 272.97, 275.51,
        279.00],
    "h_lo": [
        111.89, 114.03, 117.05, 121.63, 130.54, 133.54, 136.37, 139.30, 146.92, 148.90, 157.66, 160.00, 163.81,
        166.10, 173.27, 177.00, 179.74, 181.85, 187.22, 189.84, 194.52, 196.84, 199.82, 202.76, 204.88, 208.34,
        215.12, 218.36, 223.82, 228.91, 235.84, 250.42, 256.60, 259.53, 265.66, 267.24, 270.38, 273.58, 275.95,
        279.33],
    "down": [
        118.17, 121.01, 127.09, 129.21, 137.50, 139.06, 141.49, 144.09, 148.25, 152.75, 158.20, 161.73, 169.54,
        171.29, 174.89, 177.54, 181.16, 183.76, 188.02, 190.74, 200.96, 203.08, 206.54, 208.25, 213.63, 216.08,
        222.88, 226.20, 228.32, 233.28, 237.63, 252.64, 258.92, 262.23, 266.63, 268.80, 273.67, 275.24, 278.71,
        280.28],
    "y_out": [
        119.06, 123.68, 128.28, 130.37, 138.38, 139.95, 142.38, 144.98, 149.14, 153.64, 159.09, 162.62, 170.43,
        172.68, 175.78, 178.43, 182.04, 184.65, 188.91, 191.34, 201.85, 203.97, 207.43, 209.14, 214.52, 217.44,
        224.15, 227.58, 229.81, 234.16, 239.24, 253.53, 259.81, 265.23, 267.98, 271.82, 274.56, 276.12, 279.60,
        280.83],
    "y_put": [
        119.64, 124.26, 128.86, 130.94, 138.96, 140.53, 142.96, 145.56, 149.72, 154.22, 159.67, 163.19, 171.01,
        173.26, 176.36, 179.00, 182.62, 185.23, 189.49, 191.70, 202.43, 204.55, 208.01, 209.71, 215.10, 218.02,
        224.73, 228.15, 230.39, 234.74, 239.82, 254.10, 260.39, 265.80, 268.56, 272.40, 275.14, 276.70, 280.18,
        281.20],
    "collect": [
        196.80, 197.84, 198.88, 199.92, 207.20, 208.24, 215.52, 225.80, 228.21, 230.48, 239.84, 240.88, 254.06,
        256.32, 257.36, 261.52, 283.85, 284.89, 285.93, 286.97, 292.17, 294.44, 295.48, 296.52, 304.54, 305.58,
        307.84, 309.92, 310.96, 312.00, 313.04, 322.46],
    "collect2": [
        200.96, 202.00, 205.12, 206.16, 213.44, 214.48, 224.76, 229.44, 235.68, 236.72, 251.98, 253.02, 262.56,
        263.60, 264.64, 265.68, 288.01, 289.05, 290.09, 291.13, 297.56, 301.05, 302.09, 308.88, 315.44, 317.86,
        318.90, 323.50, 324.54, 325.58, 326.62, 327.66],
    "load_bd": [104.79, 105.03, 210.85, 236.46, 264.04, 283.48, 301.53, 313.60],
    "mix": [
        205.69, 209.90, 229.35, 235.51, 255.94, 263.09, 279.42, 282.52, 292.74, 300.58, 307.30, 312.64, 324.92,
        331.29, 338.97, 342.63],
    "y_hi": [
        206.72, 210.93, 230.80, 236.87, 256.97, 265.70, 281.10, 283.56, 294.05, 301.61, 308.85, 314.07, 325.96,
        332.89, 340.00, 343.78],
    "y_lo": [207.37, 211.58, 231.49, 237.52, 258.28, 266.41, 282.13, 284.91, 294.70, 302.46],
    "had1": [
        208.96, 212.41, 232.33, 238.33, 259.63, 267.34, 283.38, 285.71, 295.50, 303.59, 309.90, 314.74, 326.72,
        333.85, 340.92, 344.46],
    "stats1": [
        210.07, 213.79, 234.44, 239.45, 262.04, 268.45, 285.51, 291.63, 297.05, 306.44, 311.78, 318.44, 330.14,
        336.91, 342.80, 346.33],
    "stats1_value": [
        212.18, 215.46, 236.77, 241.99, 263.54, 270.72, 287.51, 295.30, 300.71, 307.94, 313.88, 319.94, 332.68,
        342.03, 344.73, 353.63],
    "round1": [
        211.58, 212.03, 216.54, 216.99, 235.97, 236.42, 240.96, 241.41, 263.55, 264.01, 269.96, 270.41, 287.02,
        287.47, 293.14, 293.60, 298.78, 299.23, 307.95, 308.40, 314.54, 315.00, 321.08, 321.54, 331.99, 332.44,
        338.42, 338.87, 345.21, 345.66, 347.84, 348.30],
    "quant1": [
        212.73, 217.61, 238.73, 243.32, 266.08, 272.72, 288.09, 294.22, 300.38, 309.09, 317.44, 323.87, 341.36,
        341.70, 347.76, 350.09],
    "turn1": [
        213.35, 218.15, 239.28, 244.24, 268.28, 274.38, 288.63, 294.92, 303.32, 309.63, 318.29, 328.43, 343.48,
        343.98, 349.90, 352.93],
    "turn1_out": [
        213.81, 218.67, 239.73, 244.69, 268.94, 275.04, 289.35, 296.00, 303.77, 310.08, 318.74, 328.88, 344.26,
        344.73, 351.51, 353.39],
    "wide": [
        214.49, 214.93, 221.77, 222.21, 241.45, 241.89, 245.93, 246.37, 269.62, 270.05, 275.94, 276.38, 290.42,
        290.86, 296.68, 297.12, 304.54, 304.98, 311.61, 312.05, 319.51, 319.95, 330.41, 330.85, 346.16, 346.60,
        348.47, 348.91, 354.92, 355.36, 355.79, 356.23],
    "relu": [
        215.11, 215.58, 222.43, 222.90, 242.07, 242.55, 247.30, 247.78, 270.87, 271.34, 276.60, 277.08, 292.11,
        292.59, 297.30, 297.78, 305.16, 305.63, 313.11, 313.59, 320.13, 320.61, 331.03, 331.51, 346.78, 347.26,
        349.65, 350.13, 355.54, 356.01, 356.49, 356.97],
    "square": [
        216.00, 223.20, 242.72, 247.95, 271.51, 277.25, 292.96, 298.38, 305.84, 315.63, 321.09, 332.08, 348.10,
        351.03, 357.26, 358.66],
    "square2": [
        218.64, 223.53, 244.00, 248.67, 271.97, 277.71, 293.22, 298.60, 306.62, 314.22, 321.23, 332.13, 347.89,
        350.76, 356.64, 357.87],
    "stage": [
        220.03, 220.63, 224.93, 225.53, 245.39, 246.00, 251.28, 251.88, 274.71, 275.31, 279.53, 280.13, 295.85,
        296.45, 301.26, 301.86, 314.43, 315.03, 316.83, 317.77, 324.99, 325.60, 333.53, 334.13, 349.49, 350.43,
        352.42, 353.02, 360.65, 361.25, 364.18, 364.79],
    "v_hi": [
        220.81, 221.42, 225.71, 226.31, 246.18, 246.78, 252.06, 254.00, 277.96, 278.48, 280.31, 281.58, 296.63,
        298.26, 302.09, 302.64, 315.45, 315.97, 318.09, 319.22],
    "v_lo": [221.76, 229.24, 247.20, 255.78, 278.65, 281.53, 298.98, 303.06, 316.23, 320.49],
    "v_lo2": [222.09, 226.98, 247.45, 255.10, 279.15, 282.25, 299.83, 303.31, 316.64, 319.94],
    "had2": [
        223.59, 224.54, 230.20, 231.15, 250.27, 251.21, 256.79, 257.73, 280.64, 281.58, 284.32, 286.65, 301.43,
        302.37, 305.41, 306.36, 318.56, 320.39, 322.76, 325.78, 328.70, 332.14, 335.55, 337.26, 351.23, 353.21,
        358.43, 360.13, 362.06, 363.76, 365.59, 367.29],
    "round2": [
        228.49, 229.15, 234.64, 235.31, 254.84, 255.50, 262.22, 262.89, 285.09, 285.75, 290.78, 291.44, 306.11,
        306.78, 311.78, 312.44, 324.05, 324.71, 329.58, 330.25, 337.09, 337.75, 341.54, 342.21, 357.45, 358.12,
        364.36, 365.03, 367.99, 368.66, 371.54, 372.21],
    "stats2": [
        226.13, 232.26, 252.48, 259.87, 282.73, 288.43, 303.66, 309.43, 321.69, 327.23, 334.73, 339.19, 355.09,
        362.01, 365.64, 369.17],
    "quant2": [
        229.98, 236.17, 257.68, 264.09, 286.91, 293.57, 308.49, 313.28, 329.40, 331.48, 338.59, 344.13, 359.26,
        367.81, 371.58, 373.04],
    "turn2": [
        237.07, 242.33, 265.36, 272.00, 287.71, 294.37, 316.45, 322.21, 339.82, 340.37, 347.04, 349.35, 369.00,
        369.55, 372.62, 373.84],
    "turn2_out": [
        237.83, 243.06, 267.07, 273.24, 288.44, 295.10, 317.18, 322.94, 340.55, 342.87, 348.75, 350.61, 369.73,
        370.64, 373.35, 374.58],
    "narrow": [
        242.88, 247.98, 272.79, 277.53, 289.55, 297.56, 321.33, 324.04, 347.59, 350.33, 356.67, 357.55, 370.84,
        371.74, 374.46, 375.68],
    "finish_scale": [
        230.59, 235.77, 264.69, 264.76, 286.84, 290.77, 318.37, 326.20, 330.01, 330.07, 338.24, 345.28, 365.39,
        368.41, 368.48, 371.51],
    "finish": [
        243.93, 249.02, 273.92, 280.74, 290.84, 299.58, 324.20, 326.44, 348.70, 351.63, 357.86, 359.86, 372.19,
        373.64, 375.51, 376.73],
    "store": [
        244.82, 249.92, 274.81, 281.63, 291.73, 300.48, 325.09, 327.33, 349.59, 352.52, 358.76, 360.75, 373.08,
        374.54, 376.40, 377.62],
}
SET = [0, 1, 0, 1, 0, 1, 2, 3, 0, 1, 2, 3, 0, 1, 2, 3]
PAIRS_AFTER = (0, 0, 0, 0, 4, 8, 8, 0)
STEPS = []
for _b in range(NBLK):
    STEPS += [(True, 2 * _b), (True, 2 * _b + 1)]
    _n = sum(PAIRS_AFTER[:_b])
    STEPS += [(False, _n + _j) for _j in range(PAIRS_AFTER[_b] if _b < NBLK - 1 else NSB * SPAIRS - _n)]
PLACE = {v: _i for _i, v in enumerate(STEPS)}
LD = 8
NATIVE = range(10, 16)


def adapter_moe_quant_ffn(nc, xT, x, adapter, cond, WA, WE, scal, cw, wuT, wdT, consts, consts16, out):
    with ExitStack() as ctx:
        def sb(name, shape, dt=F32):
            return ctx.enter_context(nc.sbuf_tensor(name, shape, dt))

        def pb(name):
            return ctx.enter_context(nc.psum_tensor(name, [P, 512], F32))

        def sem(name):
            return ctx.enter_context(nc.semaphore(name))

        gd = nc.dram_tensor("gd", (P, 1024), F32, kind="Internal").ap()
        hd = [nc.dram_tensor(f"hd{i}", (TPS * P, D), F32, kind="Internal").ap() for i in range(NSB)]
        ys = [nc.dram_tensor(f"ys{i}", (STILES * P, D), F32, kind="Internal").ap() for i in range(NSB)]

        WH = sb("WH", [P, C_END], F32R)
        WL = sb("WL", [P, C_END], F32R)
        X1 = sb("X1", [P, 4 * NBLK, D])
        CON = sb("CON", [P, 728])
        IDENT, HADF = CON[:, 0:128], CON[:, 128:256]
        W8, EIDX, SLOT0 = CON[:, 256:264], CON[:, 264:265], CON[:, 265:265 + STILES]
        LANE = CON[:, 568:696]
        TOKEN = CON[:, 696:728].rearrange("p (k t) -> p k t", k=2)
        HADP = [HADF.unsqueeze(1).broadcast_to([P, 2, P]), CON[:, 312:568].rearrange("p (a n) -> p a n", a=2)]
        C16 = sb("C16", [P, 3, P], BF16)
        LOWER, ONES16, IDB = C16[:, 0, :], C16[:, 1, :], C16[:, 2, :]
        HAD2 = sb("HAD2", [P, 2, 2, P], F32R)
        MAG = sb("MAG", [P, 1])
        ONES = sb("ONES", [P, P])
        IDXC = sb("IDXC", [P, 1], I32)
        SCAL = sb("SCAL", [P, 1])
        MASK = sb("MASK", [P, P])
        GS = sb("GS", [P, 12, P])
        GATH = GS[:, 0:8, :].rearrange("p a b -> p (a b)")
        GS_HOT = GS[:, 3:10, :].rearrange("p a b -> p (a b)")[:, 0:16 * STILES]\
            .rearrange("p (r j a n) -> p r j a n", r=2, j=4, a=2)
        G4 = sb("G4", [P, NSB, 4, TPS])
        MCB = sb("MCB", [P, P], BF16)
        SM = sb("SM", [P, 16])
        PB = sb("PB", [P, 4, 12])
        POSF = sb("POSF", [P, 2, TPS])
        POS = sb("POS", [P, NSB, 2, TPS], I32)
        ROW = sb("ROW", [P, 3, 2, TPS])
        SLOT = sb("SLOT", [P, NSB, STILES], I32)
        SLOTS = sb("SLOTS", [P, NSB, STILES])
        EXF = sb("EXF", [P, 2, STILES])
        EX = sb("EX", [P, NSB, STILES], I32)
        WU = sb("WU", [P, 2, HID], BF16)
        WD = sb("WD", [P, 4, D], BF16)
        SW = sb("SW", [P, 8])

        XIN = sb("XIN", [P, 2, 2, D])
        YS = sb("YS", [P, 2, 2, D])
        XSH = sb("XSH", [P, 2, 2, 2 * P], F32R)
        XSL = sb("XSL", [P, 2, 2, 2 * P], F32R)
        T = sb("T", [P, 3, 2 * P])
        HH = sb("HH", [P, 3, 2 * P], F32R)
        HL = sb("HL", [P, 3, 2 * P], F32R)
        WUR = XIN[:, :, :, :].rearrange("p a b d -> p (a b d)").rearrange("p (k n) -> p k n", k=2)
        WDR = YS[:, :, :, :].rearrange("p a b d -> p (a b) d")
        RAWE = X1[:, 4 * BPS:, :].rearrange("p t d -> p (t d)")[:, 0:5 * EW].rearrange("p (e n) -> p e n", e=5)

        ZR = sb("ZR", [P, 7168], F32R)
        ZF = sb("ZF", [P, 6656])

        def zr(a, n):
            return ZR[:, a:a + n]

        def zf(a, n):
            return ZF[:, a:a + n]

        H0H = zr(0, 2048).rearrange("p (a k t) -> p a k t", a=2, k=2)
        H0L = zr(2048, 2048).rearrange("p (a k t) -> p a k t", a=2, k=2)
        XH = zr(4096, 1024).rearrange("p (k t) -> p k t", k=2)
        XL = zr(5120, 1024).rearrange("p (k t) -> p k t", k=2)
        XAH, XAL = zr(6144, 512), zr(6656, 512)
        HT = zf(0, 2048).rearrange("p (t d) -> p t d", d=D)
        H0F = zf(2048, 2048).rearrange("p (a k t) -> p a k t", a=2, k=2)
        RAWA, RAWB = zf(0, C_G), zf(C_G, C_E - C_G)
        HOTL = zf(4096, 1024).rearrange("p (r j n) -> p r j n", r=2, j=4)
        XR = zf(5120, 1024).rearrange("p (k t) -> p k t", k=2)
        XA = zf(6144, 512)
        IDXI = XA[:, 0:P].bitcast(I32)

        def cut(v, c):
            return v.rearrange("p (c t) -> p c t", c=c)

        BD = zf(5120, 1024).rearrange("p (a t d) -> p a t d", a=2, t=4)
        SETS = [(cut(zr(1024 * i, 1024), 4), cut(zr(2048 + 1024 * i, 1024), 4),
                 cut(zf(1024 * i, 1024), 4), cut(zf(2048 + 1024 * i, 1024), 4),
                 cut(zf(6144 + 256 * i, 256).bitcast(BF16), 2), cut(zf(4096 + 512 * i, 512).bitcast(BF16), 2),
                 sb(f"ST{i}", [P, 13, 2])) for i in range(2)]
        first2 = X1[:, 0:8, :].rearrange("p t d -> p (t d)")
        spare = [(first2[:, 0:1024], first2[:, 1024:2048]),
                 (YS[:, :, :, :].rearrange("p a b d -> p (a b d)"), GS[:, 0:8, :].rearrange("p a b -> p (a b)"))]
        tiles = T[:, :, :].rearrange("p a n -> p (a n)")
        slots = XIN[:, :, :, :].rearrange("p a b d -> p (a b d)")
        SETS += [(cut(WH[:, C_E + 2048 * i:C_E + 2048 * i + 1024], 4),
                  cut(WH[:, C_E + 2048 * i + 1024:C_E + 2048 * i + 2048], 4),
                  cut(spare[i][0], 4), cut(spare[i][1], 4),
                  cut(tiles[:, 256 * i:256 * i + 256].bitcast(BF16), 2),
                  cut(slots[:, 512 * i:512 * i + 512].bitcast(BF16), 2), sb(f"ST{2 + i}", [P, 13, 2])) for i in range(2)]

        UP = [pb(f"UP{i}") for i in range(2)]
        DN, LB, TR, HT2 = pb("DN"), pb("LB"), pb("TR"), pb("HT2")
        AUX = [pb(f"AUX{i}") for i in range(2)]

        names = ("con c16 idc idi scl cg gw xr mag out wq "
                 "wh wl gwc had2 mask "
                 "xh xl xa xam xah xal h0w h0 h0h h0f h0l gate glc glf tk tko gsil gch rank pl pos ext hot hotl hotm slt tab xt xth xtl "
                 "a sil t3 ht hh hl acc x1s ye bdz "
                 "y yh yl f st1 qf q1 q1t q1c up rl sq sq2 bf vh vl vl2 g st2 q2f q2 q2t q2c dn fs fin "
                 "wsum wtot sw wt").split()
        S = {n: sem("s_" + n) for n in names}
        s_wa = [sem(f"s_wa{i}") for i in range(2)]
        s_we = [sem(f"s_we{i}") for i in range(NE)]
        s_x = [sem(f"p_x{i}") for i in range(NBLK)]
        s_bd = [sem(f"p_bd{i}") for i in range(2)]
        s_hd = [sem(f"p_hd{i}") for i in range(NBLK)]
        s_xi = [sem(f"p_xi{i}") for i in range(2)]
        s_y = [sem(f"p_y{i}") for i in range(2)]
        s_g = [[sem(f"p_g{k}{i}") for i in range(4)] for k in range(2)]
        s_o = [sem(f"p_o{i}") for i in range(2 * NBLK)]

        plan = {e: [] for e in ("sync", "gpsimd", "scalar", "vector", "tensor")}

        def put(engine, t, fn):
            plan[engine].append((t, len(plan[engine]), fn))

        used, when = {}, {}

        def at(engine, name, key, fn, i=0):
            k = used.get(name, 0)
            used[name] = k + 1
            t = when[(name, key, i)] = TIME[name][k]
            put(engine, t, fn)

        EARLY = -1000

        def load_first(e):
            e.dma_start(XR, xT.rearrange("(k p) t -> p k t", p=P)[:, :, 0:TB]).then_inc(S["xr"], 16)
            e.dma_start(RAWA, WA[:, 0:C_G]).then_inc(s_wa[0], 16)
            e.dma_start(IDXI, adapter.partition_broadcast(P)).then_inc(S["idi"], 16)
            e.dma_start(CON[:, :], consts).then_inc(S["con"], 16)
            e.dma_start(RAWB[:, 0:C_E - C_G], WA[:, C_G:C_E]).then_inc(s_wa[1], 16)
        put("sync", EARLY, load_first)

        def load_small(e):
            e.dma_start(IDXC[:, :], cond.rearrange("(p a) -> p a", a=1)).then_inc(S["idc"], 16)
            e.dma_start(SCAL[:, :], scal).then_inc(S["scl"], 16)
            e.dma_start(C16[:, :, :], consts16).then_inc(S["c16"], 16)
        put("scalar", EARLY, load_small)

        def load_expert(e, i):
            if i >= 5:
                e.wait_ge(S["wl"], 2 + i - 5 + 1)
            elif i % 2 == 0:
                e.wait_ge(S["xl"], 1 + i // 2)
            e.dma_start(RAWE[:, i % 5, :], WE[i]).then_inc(s_we[i], 16)
        for i in range(NE):
            at("sync", "load_expert", 0, lambda e, i=i: load_expert(e, i))

        def load_wq(e):
            e.wait_ge(S["xl"], 4)
            e.dma_start(WUR, wuT.rearrange("(k p) n -> p k n", p=P)).then_inc(S["wq"], 16)
            e.dma_start(WDR, wdT.rearrange("(k p) n -> p k n", p=P)).then_inc(S["wq"], 16)
        at("sync", "load_wq", 0, load_wq)

        def gather(e):
            e.memset(ONES[:, :], 1.0).then_inc(S["mag"], 1)
            e.memset(MAG[:, :], MAGIC).then_inc(S["mag"], 1)
            e.memset(PB[:, :, :], 0.0).then_inc(S["mag"], 1)
            e.wait_ge(S["idc"], 16)
            e.indirect_dma_start(GATH, None, cw, bass.IndirectOffsetOnAxis(ap=IDXC[:, 0:1], axis=0))\
             .then_inc(S["cg"], 16)
        put("gpsimd", EARLY, gather)

        def stash(e):
            e.wait_ge(S["cg"], 16)
            e.dma_start(gd, GATH).then_inc(S["gw"], 16)
        at("sync", "stash", 0, stash)

        def split_hi(e, i):
            if i < 2:
                e.wait_ge(s_wa[i], 16)
                a, b, raw = ((0, C_G, RAWA), (C_G, C_E, RAWB[:, 0:C_E - C_G]))[i]
            else:
                e.wait_ge(s_we[i - 2], 16)
                a = C_E + (i - 2) * EW
                b, raw = a + EW, RAWE[:, (i - 2) % 5, :]
            e.activation(WH[:, a:b], raw, ACT.Copy).then_inc(S["wh"], 1)

        def split_lo(e, i):
            if i < 2:
                a, b, raw = ((0, C_G, RAWA), (C_G, C_E, RAWB[:, 0:C_E - C_G]))[i]
            else:
                a = C_E + (i - 2) * EW
                b, raw = a + EW, RAWE[:, (i - 2) % 5, :]
            e.wait_ge(S["wh"], i + 1)
            if i == 2:
                e.wait_ge(S["wl"], 2)
            e.tensor_tensor(WL[:, a:b], raw, WH[:, a:b].bitcast(F32), ALU.subtract).then_inc(S["wl"], 1)

        for i in range(NE + 2):
            at("scalar", "split_hi", 0, lambda e, i=i: split_hi(e, i))
            at("gpsimd" if i >= 2 else "vector", "split_lo", 0, lambda e, i=i: split_lo(e, i))

        GW = sb("GW", [P, 2, 2, NE], F32R)

        def gate_weights(e):
            e.wait_ge(S["wl"], 2)
            for i, w in enumerate((WH, WL)):
                e.tensor_copy(GW[:, :, i, :], w[:, C_G:C_S].bitcast(F32).rearrange("p (k e) -> p k e", k=2))\
                 .then_inc(S["gwc"], 1)
        at("vector", "gate_weights", 0, gate_weights)

        def make_mask(e):
            e.wait_ge(S["idi"], 16)
            e.wait_ge(S["con"], 16)
            e.wait_ge(S["scl"], 16)
            e.tensor_copy(MASK[:, :], IDXI).then_inc(S["mask"], 1)
            e.wait_ge(S["mask"], 1)
            e.tensor_scalar(MASK[:, :], MASK[:, :], EIDX, SCAL[:, 0:1], ALU.is_equal, ALU.mult).then_inc(S["mask"], 1)
        at("vector", "make_mask", 0, make_mask)

        def make_identity(e):
            e.wait_ge(S["con"], 16)
            for k in range(2):
                e.tensor_copy(HAD2[:, k, 0, :], HADF).then_inc(S["had2"], 1)
                e.tensor_scalar(HAD2[:, k, 1, :], HADF, 1.0 - 2 * k, None, ALU.mult).then_inc(S["had2"], 1)
        at("vector", "make_identity", 0, make_identity)

        def weight_sums(e):
            e.wait_ge(S["wq"], 32)
            e.tensor_reduce(SW[:, 0:1], WUR, AX.XY, ALU.add, apply_absolute_value=True).then_inc(S["wsum"], 1)
            e.tensor_reduce(SW[:, 1:2], WDR, AX.XY, ALU.add, apply_absolute_value=True).then_inc(S["wsum"], 1)
        at("vector", "weight_sums", 0, weight_sums)

        def weight_total(e):
            e.wait_ge(S["wsum"], 2)
            e.wait_ge(S["mag"], 1)
            bank_free(e, "AUX0", ("weight_total", 0, 0))
            e.matmul(AUX[0][:, 0:2], ONES[:, :], SW[:, 0:2], start=True, stop=True).then_inc(S["wtot"], 1)
        at("tensor", "weight_total", 0, weight_total)

        def ternary(e):
            e.wait_ge(S["wtot"], 1)
            e.tensor_scalar(SW[:, 2:4], AUX[0][:, 0:2], 1.0 / (D * HID), EPS, ALU.mult, ALU.max).then_inc(S["sw"], 1)
            e.wait_ge(S["sw"], 1)
            e.reciprocal(SW[:, 4:6], SW[:, 2:4]).then_inc(S["sw"], 1)
            e.wait_ge(S["sw"], 2)
            n = 0
            for raw, q, c in ((WUR, WU, 4), (WDR, WD, 5)):
                e.tensor_scalar(raw, raw, SW[:, c:c + 1], MAGIC, ALU.mult, ALU.add).then_inc(S["wt"], 1)
                e.wait_ge(S["wt"], n + 1)
                e.tensor_scalar(raw, raw, MAGIC, 1.0, ALU.subtract, ALU.min).then_inc(S["wt"], 1)
                e.wait_ge(S["wt"], n + 2)
                e.tensor_scalar(q[:, :, :], raw, -1.0, None, ALU.max).then_inc(S["wt"], 1)
                n += 3
        at("vector", "ternary", 0, ternary)

        def down_free(e, s):
            if s > 0:
                shared, i = STEPS[s - 1]
                e.wait_ge(S["x1s" if shared else "ye"], i + 1)

        def plan_adapter(b):
            pr = b % 2
            h0h, h0l = H0H[:, pr, :, :], H0L[:, pr, :, :]

            def load_x(e):
                if b >= BPS:
                    e.wait_ge(S["wl"], NE + 2)
                e.dma_start(X1[:, 4 * b:4 * b + 4, :], x[b * TB:(b + 1) * TB, :].rearrange("(t p) d -> p t d", p=P))\
                 .then_inc(s_x[b], 16)
            at("sync", "load_x", b, load_x)

            if b > 0:
                def load(e):
                    e.wait_ge(S["xl"], b)
                    e.dma_start(XR, xT.rearrange("(k p) t -> p k t", p=P)[:, :, b * TB:(b + 1) * TB])\
                     .then_inc(S["xr"], 16)
                at("sync", "load_xT", b, load)

            def x_hi(e):
                e.wait_ge(S["xr"], 16 * (b + 1))
                if b > 0:
                    e.wait_ge(S["xa"], b)
                    e.wait_ge(S["h0w"], 2 * b)
                e.activation(XH, XR, ACT.Copy).then_inc(S["xh"], 1)
            at("scalar", "x_hi", b, x_hi)

            def x_lo(e):
                e.wait_ge(S["xh"], b + 1)
                e.tensor_tensor(XL, XR, XH.bitcast(F32), ALU.subtract).then_inc(S["xl"], 1)
            at("vector", "x_lo", b, x_lo)

            def xa(e):
                e.wait_ge(S["xl"], b + 1)
                e.wait_ge(S["wl"], 1)
                bank_free(e, "TR", ("xa", b, 0))
                n = 0
                for k in range(2):
                    for w, xx in ((WH, XH), (WH, XL), (WL, XH)):
                        mm = e.matmul(TR[:, :], w[:, C_A + k * P:C_A + (k + 1) * P], xx[:, k, :],
                                      start=(n == 0), stop=(n == 5))
                        n += 1
                mm.then_inc(S["xa"], 1)
            at("tensor", "xa", b, xa)

            def xam(e):
                e.wait_ge(S["xa"], b + 1)
                if b == 0:
                    e.wait_ge(S["mask"], 2)
                if b > 0:
                    e.wait_ge(S["xal"], b)
                m = MASK[:, 16 * b:16 * b + 16].unsqueeze(2).broadcast_to([P, 16, 32])
                e.tensor_tensor(XA.rearrange("p (n t) -> p n t", t=32),
                                TR[:, :].rearrange("p (n t) -> p n t", t=32), m, ALU.mult).then_inc(S["xam"], 1)
            at("vector", "xam", b, xam)

            def xa_hi(e):
                e.wait_ge(S["xam"], b + 1)
                if b > 0:
                    e.wait_ge(S["h0"], 2 * b)
                e.activation(XAH, XA, ACT.Copy).then_inc(S["xah"], 1)
            at("scalar", "xa_hi", b, xa_hi)

            def xa_lo(e):
                e.wait_ge(S["xah"], b + 1)
                e.tensor_tensor(XAL, XA, XAH.bitcast(F32), ALU.subtract).then_inc(S["xal"], 1)
            at("vector", "xa_lo", b, xa_lo)

            def h0w(e, o):
                e.wait_ge(S["xl"], b + 1)
                if b == 0:
                    e.wait_ge(S["wl"], 1)
                bank_free(e, f"AUX{o}", ("h0w", b, o))
                n = 0
                for k in range(2):
                    c = C_W + k * D + o * P
                    for w, xx in ((WH, XH), (WH, XL), (WL, XH)):
                        mm = e.matmul(AUX[o][:, :], w[:, c:c + P], xx[:, k, :], start=(n == 0), stop=False,
                                      skip_group_check=True)
                        n += 1
                mm.then_inc(S["h0w"], 1)

            def h0(e, o):
                e.wait_ge(S["xal"], b + 1)
                e.wait_ge(S["h0w"], 2 * b + o + 1)
                c = C_B + o * P
                e.matmul(AUX[o][:, :], WH[:, c:c + P], XAH, start=False, stop=False, skip_group_check=True)
                e.matmul(AUX[o][:, :], WH[:, c:c + P], XAL, start=False, stop=False, skip_group_check=True)
                e.matmul(AUX[o][:, :], WL[:, c:c + P], XAH, start=False, stop=True, skip_group_check=True)\
                 .then_inc(S["h0"], 1)

            def h0_hi(e, o):
                e.wait_ge(S["h0"], 2 * b + o + 1)
                if b >= 2 and o == 0:
                    e.wait_ge(S["a"], PLACE[True, 2 * b - 3] + 1)
                    e.wait_ge(S["gate"], b - 1)
                    e.wait_ge(S["h0f"], b - 1)
                e.activation(h0h[:, o, :], AUX[o][:, :], ACT.Copy).then_inc(S["h0h"], 1)

            def h0_lo(e, o):
                e.wait_ge(S["h0h"], 2 * b + o + 1)
                e.tensor_tensor(h0l[:, o, :], AUX[o][:, :], h0h[:, o, :].bitcast(F32), ALU.subtract)\
                 .then_inc(S["h0l"], 1)
            for o in range(2):
                at("tensor", "h0w", b, lambda e, o=o: h0w(e, o), o)
                at("tensor", "h0", b, lambda e, o=o: h0(e, o), o)
                at("scalar", "h0_hi", b, lambda e, o=o: h0_hi(e, o), o)
                at("vector", "h0_lo", b, lambda e, o=o: h0_lo(e, o), o)

            def h0_sum(e):
                e.wait_ge(S["h0l"], 2 * b + 2)
                if b == 0:
                    e.wait_ge(S["wl"], 2)
                if b >= 2:
                    e.wait_ge(S["tk"], 2 * (b - 1))
                e.tensor_tensor(H0F[:, pr, :, :], h0h.bitcast(F32), h0l.bitcast(F32), ALU.add).then_inc(S["h0f"], 1)
            at("gpsimd", "h0_sum", b, h0_sum)

            def gate(e):
                e.wait_ge(S["h0l"], 2 * b + 2)
                if b == 0:
                    e.wait_ge(S["gwc"], 2)
                bank_free(e, "AUX0", ("gate", b, 0))
                for t in range(4):
                    tok = slice(t * P, (t + 1) * P)
                    for k in range(2):
                        e.matmul(AUX[0][:, 16 * t:16 * t + 16], h0h[:, k, tok],
                                 GW[:, k, :, :].rearrange("p a e -> p (a e)"),
                                 start=(k == 0), stop=False, skip_group_check=True)
                    for k in range(2):
                        mm = e.matmul(AUX[0][:, 16 * t:16 * t + 8], h0l[:, k, tok], GW[:, k, 0, :],
                                      start=False, stop=(k == 1), skip_group_check=True)
                mm.then_inc(S["gate"], 1)
            at("tensor", "gate", b, gate)

            c4 = slice(32 * (b % BPS), 32 * (b % BPS) + 32)

            def logits_lo(e):
                e.wait_ge(S["gate"], b + 1)
                if b == 0:
                    e.wait_ge(S["gw"], 16)
                if b % BPS == 0 and b > 0:
                    e.wait_ge(S["pos"], b // BPS)
                e.activation(GS[:, 0, c4].rearrange("p (t e) -> p t e", e=NE),
                             AUX[0][:, 0:64].rearrange("p (t a e) -> p t a e", a=2, e=NE)[:, :, 1, :],
                             ACT.Copy).then_inc(S["glc"], 1)
            at("scalar", "logits_lo", b, logits_lo)

            def logits(e):
                e.wait_ge(S["glc"], b + 1)
                e.tensor_tensor(GS[:, 2, c4].rearrange("p (t e) -> p t e", e=NE),
                                AUX[0][:, 0:64].rearrange("p (t a e) -> p t a e", a=2, e=NE)[:, :, 0, :],
                                GS[:, 0, c4].rearrange("p (t e) -> p t e", e=NE), ALU.add).then_inc(S["glf"], 1)
            at("vector", "logits", b, logits)

            def tok(e, j):
                if j == 0:
                    e.wait_ge(S["h0f"], b + 1)
                    if b == 0:
                        e.wait_ge(S["con"], 16)
                bank_free(e, "HT2", ("tok", b, j))
                for t in range(2):
                    tok = slice((2 * j + t) * P, (2 * j + t + 1) * P)
                    for k in range(2):
                        dst = HT2[:, t * D + k * P:t * D + (k + 1) * P]
                        mm = e.transpose(dst, H0F[:, pr, k, tok], IDENT)
                mm.then_inc(S["tk"], 1)

            def tok_out(e, j):
                e.wait_ge(S["tk"], 2 * b + j + 1)
                t = 4 * pr + 2 * j
                if b == 0:
                    e.wait_ge(S["wl"], 2)
                if b >= 2:
                    e.wait_ge(s_hd[b - 2], 16)
                e.activation(HT[:, t:t + 2, :], HT2[:, :].rearrange("p (t d) -> p t d", t=2), ACT.Copy)\
                 .then_inc(S["tko"], 1)
            for j in range(2):
                at("tensor", "tok", b, lambda e, j=j: tok(e, j), j)
                at("scalar", "tok_out", b, lambda e, j=j: tok_out(e, j), j)

            def hd_put(e):
                p, t = b // BPS, 4 * (b % BPS)
                e.wait_ge(S["tko"], 2 * b + 2)
                e.dma_start(hd[p][t * P:(t + 4) * P, :].rearrange("(t p) d -> p t d", p=P), HT[:, 4 * pr:4 * pr + 4, :])\
                 .then_inc(s_hd[b], 16)
            at("sync", "hd_put", b, hd_put)

            for h in range(2):
                m = 2 * b + h
                s = PLACE[True, m]
                tk = slice(h * 256, h * 256 + 256)

                def s_up(e, s=s, tk=tk):
                    e.wait_ge(S["h0l"], 2 * b + 2)
                    if b == 0:
                        e.wait_ge(S["wl"], 2)
                    if s >= 2:
                        e.wait_ge(S["t3"], s - 1)
                    for i in range(2):
                        n = 0
                        for k in range(2):
                            c = C_S + 2 * k * P + i * P
                            for w, hh in ((WH, h0h), (WH, h0l), (WL, h0h)):
                                mm = e.matmul(UP[s % 2][:, i * 256:i * 256 + 256], w[:, c:c + P], hh[:, k, tk],
                                              start=(n == 0), stop=(n == 5))
                                n += 1
                    mm.then_inc(S["a"], 1)

                def s_silu(e, s=s):
                    e.wait_ge(S["a"], s + 1)
                    if s >= 3:
                        e.wait_ge(S["hl"], s - 2)
                    e.activation(T[:, s % 3, :], UP[s % 2][:, 0:256], ACT.Silu).then_inc(S["sil"], 1)

                def s_times3(e, s=s):
                    e.wait_ge(S["sil"], s + 1)
                    e.tensor_tensor(T[:, s % 3, :], UP[s % 2][:, 256:512], T[:, s % 3, :], ALU.mult).then_inc(S["t3"], 1)

                def s_h_hi(e, s=s):
                    e.wait_ge(S["t3"], s + 1)
                    if s >= 3:
                        e.wait_ge(S["acc"], s - 2)
                    e.activation(HH[:, s % 3, :], T[:, s % 3, :], ACT.Copy).then_inc(S["hh"], 1)

                def s_h_lo(e, s=s):
                    e.wait_ge(S["hh"], s + 1)
                    e.tensor_tensor(HL[:, s % 3, :], T[:, s % 3, :], HH[:, s % 3, :].bitcast(F32), ALU.subtract)\
                     .then_inc(S["hl"], 1)

                def s_down(e, s=s):
                    e.wait_ge(S["hl"], s + 1)
                    down_free(e, s)
                    for c in range(2):
                        for n, (hh, w) in enumerate(((HH, WH), (HL, WH), (HH, WL))):
                            mm = e.matmul(DN[:, c * D:(c + 1) * D], hh[:, s % 3, c * P:(c + 1) * P],
                                          w[:, C_S + 512:C_E], start=(n == 0), stop=(n == 2))
                    mm.then_inc(S["acc"], 1)

                def s_out(e, s=s, m=m, h=h):
                    e.wait_ge(S["acc"], s + 1)
                    if h == 0:
                        e.wait_ge(s_x[b], 16)
                    v = X1[:, 2 * m:2 * m + 2, :].rearrange("p t d -> p (t d)")
                    e.tensor_tensor(v, DN[:, :], v, ALU.add).then_inc(S["x1s"], 1)
                at("tensor", "s_up", b, s_up, h)
                at("scalar", "s_silu", b, s_silu, h)
                at("vector", "s_times3", b, s_times3, h)
                at("scalar", "s_h_hi", b, s_h_hi, h)
                at("vector", "s_h_lo", b, s_h_lo, h)
                at("tensor", "s_down", b, s_down, h)
                at("vector", "s_out", b, s_out, h)

        def plan_route(p):
            n = [18 * p]

            def link(e, ins):
                n[0] += 1
                ins.then_inc(S["gch"], 1)
                e.wait_ge(S["gch"], n[0])

            def r(i):
                return GS[:, i, :].rearrange("p (t e) -> p t e", e=NE)

            def g4(i):
                return G4[:, p, i, :]

            def c(i):
                return g4(i).unsqueeze(2).broadcast_to([P, TPS, NE])

            def nonzero(e):
                e.wait_ge(S["glf"], BPS * (p + 1))
                if p > 0:
                    e.wait_ge(S["ext"], p)
                    e.wait_ge(S["tab"], 8 * p)
                link(e, e.tensor_scalar(GS[:, 0, :], GS[:, 2, :], 0.0, 1e-30, ALU.is_equal, ALU.mult))
                link(e, e.tensor_tensor(GS[:, 1, :], GS[:, 2, :], GS[:, 0, :], ALU.add))
            at("vector", "nonzero", p, nonzero)

            def gate_silu(e):
                e.wait_ge(S["gch"], 18 * p + 2)
                e.activation(GS[:, 2, :], GS[:, 1, :], ACT.Silu).then_inc(S["gsil"], 1)
            at("scalar", "gate_silu", p, gate_silu)

            def top2(e):
                w8 = W8.unsqueeze(1).broadcast_to([P, TPS, NE])
                link(e, e.reciprocal(GS[:, 4, :], GS[:, 1, :]))
                e.wait_ge(S["gsil"], p + 1)
                link(e, e.tensor_tensor(GS[:, 5, :], GS[:, 2, :], GS[:, 4, :], ALU.mult))
                link(e, e.tensor_scalar(GS[:, 6, :], GS[:, 1, :], SAT, None, ALU.is_ge))
                link(e, e.scalar_tensor_tensor(out=GS[:, 3, :], in0=GS[:, 5, :], scalar=1.0, in1=GS[:, 6, :],
                                               op0=ALU.min, op1=ALU.max))
                for j, sc, base in ((0, 3, 4), (1, 7, 8)):
                    link(e, e.tensor_reduce(g4(2 * j), r(sc), AX.X, ALU.max))
                    link(e, e.tensor_tensor(r(base), r(sc), c(2 * j), ALU.is_equal))
                    link(e, e.tensor_tensor(r(base + 1), r(base), w8, ALU.mult))
                    link(e, e.tensor_reduce(g4(2 * j + 1), r(base + 1), AX.X, ALU.max))
                    link(e, e.tensor_tensor(r(base + 2), r(base + 1), c(2 * j + 1), ALU.is_equal))
                    if j == 0:
                        link(e, e.scalar_tensor_tensor(out=GS[:, 7, :], in0=GS[:, 6, :], scalar=-4.0, in1=GS[:, 3, :],
                                                       op0=ALU.mult, op1=ALU.add))
                link(e, e.tensor_tensor(MCB[:, :], GS[:, 6, :], GS[:, 10, :], ALU.add))
            at("vector", "top2", p, top2)

            def rank(e):
                e.wait_ge(S["gch"], 18 * p + 18)
                if p == 0:
                    e.wait_ge(S["c16"], 16)
                bank_free(e, "LB", ("rank", p, 0))
                e.matmul(LB[:, 0:P], LOWER, MCB[:, :], start=True, stop=False, skip_group_check=True)
                for t in range(TPS):
                    m = MCB[:, t * NE:(t + 1) * NE]
                    mm = e.matmul(LB[:, P:P + NE], ONES16, m, start=False, stop=(t == TPS - 1),
                                  skip_group_check=True)
                    if t < TPS - 1:
                        k = TPS - 1 - t
                        e.matmul(LB[:, (t + 1) * NE:P].rearrange("p (t e) -> p t e", e=NE), ONES16,
                                 m.unsqueeze(1).broadcast_to([P, k, NE]), start=False, stop=(t == TPS - 2),
                                 skip_group_check=True)
                mm.then_inc(S["rank"], 1)
            at("tensor", "rank", p, rank)

            def place(e):
                k = [18 * p]

                def link(ins):
                    k[0] += 1
                    ins.then_inc(S["pl"], 1)
                    e.wait_ge(S["pl"], k[0])
                e.wait_ge(S["rank"], p + 1)
                if p == 0:
                    e.wait_ge(S["mag"], 3)
                chosen = LB[:, P:P + NE]
                link(e.tensor_scalar(SM[:, 0:8], chosen, 63.5, 1.0 / P, ALU.add, ALU.mult))
                link(e.tensor_scalar(SM[:, 8:16], SM[:, 0:8], MAGIC, None, ALU.add))
                link(e.tensor_scalar(PB[:, 0, 4:12], SM[:, 8:16], MAGIC, float(P), ALU.subtract, ALU.mult))
                for i, d in enumerate((1, 2, 4)):
                    link(e.tensor_tensor(PB[:, i + 1, 4:12], PB[:, i, 4:12], PB[:, i, 4 - d:12 - d], ALU.add))
                start = PB[:, 3, 3:11].unsqueeze(1).broadcast_to([P, TPS, NE])
                link(e.tensor_tensor(r(0), LB[:, 0:P].rearrange("p (t e) -> p t e", e=NE), start, ALU.add))
                for j, m in ((0, 6), (1, 10)):
                    link(e.tensor_tensor(r(4 + j), r(0), r(m), ALU.mult))
                    link(e.tensor_reduce(POSF[:, j, :], r(4 + j), AX.X, ALU.add))
                link(e.tensor_scalar(ROW[:, 0, :, :], POSF[:, :, :], -63.5, 1.0 / P, ALU.add, ALU.mult))
                link(e.tensor_scalar(ROW[:, 2, :, :], ROW[:, 0, :, :], MAGIC, None, ALU.add))
                link(e.tensor_scalar(ROW[:, 0, :, :], ROW[:, 2, :, :], MAGIC, float(P), ALU.subtract, ALU.mult))
                link(e.tensor_tensor(ROW[:, 1, :, :], POSF[:, :, :], ROW[:, 0, :, :], ALU.subtract))
                e.tensor_copy(POS[:, p, :, :], POSF[:, :, :]).then_inc(S["pos"], 1)
                v = GS[:, 7:10, :].rearrange("p a b -> p (a b)")[:, 0:STILES * NE].rearrange("p (i e) -> p i e", e=NE)
                link(e.tensor_tensor(v, PB[:, 3, 4:12].unsqueeze(1).broadcast_to([P, STILES, NE]),
                                     SLOT0.unsqueeze(2).broadcast_to([P, STILES, NE]), ALU.is_le))
                link(e.tensor_reduce(EXF[:, 0, :], v, AX.X, ALU.add))
                link(e.tensor_scalar(EXF[:, 1, :], EXF[:, 0, :], float(NE - 1), float(EW), ALU.min, ALU.mult))
                e.tensor_copy(EX[:, p, :], EXF[:, 1, :]).then_inc(S["ext"], 1)
                assert k[0] == 18 * (p + 1)
            at("vector", "place", p, place)

            def hot_lane(e, i, half):
                n = 8 * p + i
                k, t = divmod(4 * i, TPS)
                if i == 0:
                    e.wait_ge(S["pos"], p + 1)
                if n >= 2:
                    e.wait_ge(S["tab"], n - 1)
                for j in half:
                    ins = e.tensor_scalar(HOTL[:, n % 2, j, :], LANE, ROW[:, 1, k, t + j:t + j + 1], None, ALU.is_equal)
                ins.then_inc(S["hotl" if half[0] else "hotm"], 1)

            def hot(e, i):
                n = 8 * p + i
                k, t = divmod(4 * i, TPS)
                if i == 0:
                    e.wait_ge(S["ext"], p + 1)
                if n >= 2:
                    e.wait_ge(S["tab"], n - 1)
                ht = GS_HOT[:, n % 2, :, :, :]
                e.tensor_tensor(ht[:, :, 1, :], ROW[:, 0, k, t:t + 4].unsqueeze(2).broadcast_to([P, 4, STILES]),
                                SLOT0.unsqueeze(1).broadcast_to([P, 4, STILES]), ALU.is_equal).then_inc(S["hot"], 1)
                e.wait_ge(S["hot"], 3 * n + 1)
                e.tensor_tensor(ht[:, :, 0, :], ht[:, :, 1, :],
                                TOKEN[:, k, t:t + 4].unsqueeze(2).broadcast_to([P, 4, STILES]), ALU.mult)\
                 .then_inc(S["hot"], 1)
                e.wait_ge(S["hot"], 3 * n + 2)
                e.tensor_tensor(ht[:, :, 1, :], ht[:, :, 1, :],
                                G4[:, p, 2 * k, t:t + 4].unsqueeze(2).broadcast_to([P, 4, STILES]), ALU.mult)\
                 .then_inc(S["hot"], 1)

            tv = LB[:, 0:2 * STILES]

            def sum_up(e, i):
                n = 8 * p + i
                e.wait_ge(S["hot"], 3 * n + 3)
                e.wait_ge(S["hotl"], n + 1)
                e.wait_ge(S["hotm"], n + 1)
                if i == 0:
                    bank_free(e, "LB", ("sum", p, 0))
                for j in range(4):
                    mm = e.matmul(tv, HOTL[:, n % 2, j, :], GS_HOT[:, n % 2, j, :, :].rearrange("p a n -> p (a n)"),
                                  start=(4 * i + j == 0), stop=(4 * i + j == 2 * TPS - 1))
                mm.then_inc(S["tab"], 1)

            def slot_out(e):
                e.wait_ge(S["tab"], 8 * p + 8)
                e.tensor_copy(SLOT[:, p, :], LB[:, 0:STILES]).then_inc(S["slt"], 1)
                e.tensor_copy(SLOTS[:, p, :], LB[:, STILES:2 * STILES]).then_inc(S["slt"], 1)
            for i in range(8):
                at("vector", "hot_lane", p, lambda e, i=i: hot_lane(e, i, range(0, 2)), i)
                at("gpsimd", "hot_lane2", p, lambda e, i=i: hot_lane(e, i, range(2, 4)), i)
                at("vector", "hot", p, lambda e, i=i: hot(e, i), i)
                at("tensor", "sum", p, lambda e, i=i: sum_up(e, i), i)
            at("vector", "slot_out", p, slot_out)

        first = {}

        def plan_pair(r):
            p, i = divmod(r, SPAIRS)
            s = PLACE[False, r]
            tiles = min(2, STILES - 2 * i)
            rows = slice(2 * i * P, (2 * i + tiles) * P)
            n = tiles * P

            def load_slots(e):
                if i == 0:
                    for b in range(BPS):
                        e.wait_ge(s_hd[BPS * p + b], 16)
                    e.wait_ge(S["slt"], 2 * p + 2)
                if r == 0:
                    e.wait_ge(S["wt"], 6)
                if r >= 2:
                    e.wait_ge(S["xt"], r - 1)
                for c in range(tiles):
                    e.indirect_dma_start(XIN[:, r % 2, c, :], None, hd[p],
                                         bass.IndirectOffsetOnAxis(ap=SLOT[:, p, 2 * i + c:2 * i + c + 1], axis=0))\
                     .then_inc(s_xi[r % 2], 16)
            at("gpsimd", "load_slots", r + 0, load_slots)

            arrived = 16 * sum(min(2, STILES - 2 * (q % SPAIRS)) for q in range(r % 2, r + 1, 2))

            def expert_numbers(e):
                if i == 0:
                    e.wait_ge(S["ext"], p + 1)
                a, b = 2 * i, min(2 * i + LD, STILES)
                _, got = nc.values_load_multi_w_load_instructions(
                    EX[0:1, p, a:b], engines=[mybir.EngineType.PE], min_val=0, max_val=(NE - 1) * EW,
                    skip_runtime_bounds_check_because="place() takes the minimum with the last expert's column")
                first.update({(p, a + j): v for j, v in enumerate(got)})

            def xt(e):
                e.wait_ge(s_xi[r % 2], arrived)
                bank_free(e, "TR", ("xt", r, 0))
                for k in range(2):
                    for c in range(tiles):
                        mm = e.transpose(TR[:, k * 256 + c * P:k * 256 + (c + 1) * P],
                                         XIN[:, r % 2, c, k * P:(k + 1) * P], IDENT)
                mm.then_inc(S["xt"], 1)
                if 2 * i % LD == 0:
                    expert_numbers(e)
            at("tensor", "xt", r + 0, xt)

            trv = TR[:, :].rearrange("p (k n) -> p k n", k=2)[:, :, 0:n]

            def xt_hi(e):
                e.wait_ge(S["xt"], r + 1)
                if r >= 2:
                    e.wait_ge(S["a"], PLACE[False, r - 2] + 1)
                e.activation(XSH[:, r % 2, :, 0:n], trv, ACT.Copy).then_inc(S["xth"], 1)
            at("scalar", "xt_hi", r + 0, xt_hi)

            def xt_lo(e):
                e.wait_ge(S["xth"], r + 1)
                e.tensor_tensor(XSL[:, r % 2, :, 0:n], trv, XSH[:, r % 2, :, 0:n].bitcast(F32), ALU.subtract)\
                 .then_inc(S["xtl"], 1)
            at("vector", "xt_lo", r + 0, xt_lo)

            def up(e):
                if r == 0:
                    e.wait_ge(S["wl"], NE + 2)
                e.wait_ge(S["xtl"], r + 1)
                e.wait_ge(S["t3"], s - 1)
                for c in range(tiles):
                    n = 0
                    for k in range(2):
                        cols = bass.ds(first[p, 2 * i + c] + (C_E + k * 256), 256)
                        for w, v in ((WH, XSH), (WH, XSL), (WL, XSH)):
                            mm = e.matmul(UP[s % 2][:, c * 256:c * 256 + 256], v[:, r % 2, k, c * P:(c + 1) * P],
                                          w[:, cols], start=(n == 0), stop=(n == 5))
                            n += 1
                mm.then_inc(S["a"], 1)
            at("tensor", "up", r + 1, up)

            score = [SLOTS[:, p, 2 * i + c:2 * i + c + 1] for c in range(tiles)]
            upv = UP[s % 2][:, :].rearrange("p (c a n) -> p c a n", c=2, a=2)[:, 0:tiles, :, :]
            tv = T[:, s % 3, 0:n].rearrange("p (c n) -> p c n", c=tiles)

            def silu(e):
                e.wait_ge(S["a"], s + 1)
                e.wait_ge(S["hl"], s - 2)
                for c in range(tiles):
                    ins = e.activation(tv[:, c, :], upv[:, c, 0, :], ACT.Silu, scale=score[c])
                ins.then_inc(S["sil"], 1)
            at("scalar", "silu", r + 1, silu)

            def times3(e):
                e.wait_ge(S["sil"], s + 1)
                for c in range(tiles):
                    ins = e.scalar_tensor_tensor(out=tv[:, c, :], in0=upv[:, c, 1, :], scalar=score[c], in1=tv[:, c, :],
                                                 op0=ALU.mult, op1=ALU.mult)
                ins.then_inc(S["t3"], 1)
            at("vector", "times3", r + 1, times3)

            hb = HT2[:, 0:n]

            def ht(e):
                e.wait_ge(S["t3"], s + 1)
                bank_free(e, "HT2", ("ht", r + 1, 0))
                for c in range(tiles):
                    mm = e.transpose(hb[:, c * P:(c + 1) * P], T[:, s % 3, c * P:(c + 1) * P], IDENT)
                mm.then_inc(S["ht"], 1)
            at("tensor", "ht", r + 1, ht)

            def h_hi(e):
                e.wait_ge(S["ht"], r + 1)
                e.wait_ge(S["acc"], s - 2)
                e.activation(HH[:, s % 3, 0:n], hb, ACT.Copy).then_inc(S["hh"], 1)
            at("scalar", "h_hi", r + 2, h_hi)

            def h_lo(e):
                e.wait_ge(S["hh"], s + 1)
                e.tensor_tensor(HL[:, s % 3, 0:n], hb, HH[:, s % 3, 0:n].bitcast(F32), ALU.subtract)\
                 .then_inc(S["hl"], 1)
            at("vector", "h_lo", r + 2, h_lo)

            def down(e):
                e.wait_ge(S["hl"], s + 1)
                down_free(e, s)
                for c in range(tiles):
                    cols = bass.ds(first[p, 2 * i + c] + (C_E + 512), 256)
                    for j, (hh, w) in enumerate(((HH, WH), (HL, WH), (HH, WL))):
                        mm = e.matmul(DN[:, c * D:(c + 1) * D], hh[:, s % 3, c * P:(c + 1) * P],
                                      w[:, cols], start=(j == 0), stop=(j == 2))
                mm.then_inc(S["acc"], 1)
            at("tensor", "down", r + 2, down)

            def y_out(e):
                e.wait_ge(S["acc"], s + 1)
                if r == 0:
                    e.wait_ge(S["wt"], 6)
                if r >= 2:
                    e.wait_ge(s_y[r % 2], 16 * (r // 2))
                e.activation(YS[:, r % 2, 0:tiles, :], DN[:, 0:tiles * D].rearrange("p (c d) -> p c d", c=tiles),
                             ACT.Copy).then_inc(S["ye"], 1)
            at("scalar", "y_out", r + 2, y_out)

            def y_put(e):
                e.wait_ge(S["ye"], r + 1)
                e.dma_start(ys[p][rows, :].rearrange("(c q) d -> q c d", q=P), YS[:, r % 2, 0:tiles, :])\
                 .then_inc(s_y[r % 2], 16)
            at("sync", "y_put", r + 2, y_put)

        def plan_collect(p):
            for t in range(TPS):
                tt = TPS * p + t
                q, n = tt % 4, tt // 4

                def collect(e, k, t=t, tt=tt, q=q, n=n):
                    if k == 0:
                        if t == 0:
                            for j in range(2):
                                e.wait_ge(s_y[j], 16 * ((SPAIRS * (p + 1) + 1 - j) // 2))
                        e.wait_ge(S["x1s"], tt // 2 + 1)
                        if n > 0:
                            e.wait_ge(s_g[0][q], 16 * n)
                    else:
                        e.wait_ge(s_g[0][q], 16 * (n + 1))
                        if n > 0:
                            e.wait_ge(s_g[1][q], 16 * n)
                    e.indirect_dma_start(X1[:, tt, :], None, ys[p],
                                         bass.IndirectOffsetOnAxis(ap=POS[:, p, k, t:t + 1], axis=0),
                                         compute_op=ALU.add).then_inc(s_g[k][q], 16)
                at("gpsimd", "collect", p, lambda e, f=collect: f(e, 0))
                at("gpsimd", "collect2", p, lambda e, f=collect: f(e, 1))

        def clear_bd(e):
            e.wait_ge(S["xl"], NBLK)
            e.memset(BD, 0.0).then_inc(S["bdz"], 1)
        at("gpsimd", "clear_bd", 1, clear_bd)

        def plan_layer2(b):
            x1 = X1[:, 2 * b:2 * b + 2, :]
            blk, pr, bt = b // 2, b // 2 % 2, 2 * (b % 2)
            ss = SET[b]
            P1H, P1L, R, U, Q1T, Q2, ST = SETS[ss]
            (pa, pa_name), (pc, pc_name) = BANKS[ss]
            QF = U[:, 0:2, :]
            UF = U[:, :, :].rearrange("p (t c) n -> p t (c n)", t=2)
            Q1 = Q2[:, :, 0:D]
            Q2T = U[:, 2:4, :].rearrange("p a b -> p (a b)").bitcast(BF16).rearrange("p (c t) -> p c t", c=4)
            before = [c for c in range(b) if SET[c] == ss]
            pv = before[-1] + 1 if before else 0

            split = len([c for c in range(b) if c not in NATIVE])

            def st(i):
                return ST[:, i, :]

            def steps_done(e):
                e.wait_ge(S["acc"], NST)
                if ss == 2:
                    for c in range(4):
                        e.wait_ge(s_o[c], 16)
                else:
                    for j in range(2):
                        e.wait_ge(s_y[j], 16 * ((NSB * SPAIRS + 1 - j) // 2))

            def load_bd(e):
                if blk == 0:
                    e.wait_ge(S["gw"], 16)
                    e.wait_ge(S["bdz"], 1)
                if blk >= 2:
                    e.wait_ge(S["y"], 2 * (blk - 1))
                src = gd[16 * blk:16 * blk + 16, :].rearrange("(t j) (c d) -> j c t d", j=4, c=32)
                for j in range(4):
                    s32 = slice(32 * j, 32 * j + 32)
                    e.dma_start(BD[s32, pr, :, s32], src[j]).then_inc(s_bd[pr], 16)
            if b % 2 == 0:
                at("sync", "load_bd", b, load_bd)

            def mix(e):
                for t in (2 * b, 2 * b + 1):
                    e.wait_ge(s_g[1][t % 4], 16 * (t // 4 + 1))
                e.wait_ge(s_bd[pr], 64 * (blk // 2 + 1))
                if pv:
                    e.wait_ge(S["g"], 2 * pv)
                bank_free(e, pa_name, ("mix", b, 0))
                for k in range(2):
                    for t in range(2):
                        mm = e.matmul(pa[:, k * 256 + t * P:k * 256 + (t + 1) * P], x1[:, t, k * P:(k + 1) * P],
                                      BD[:, pr, bt + t, :], start=True, stop=True)
                mm.then_inc(S["y"], 1)

            yv = pa[:, :].rearrange("p (k t) -> p k t", k=2)

            def y_hi(e):
                e.wait_ge(S["y"], b + 1)
                if pv:
                    e.wait_ge(S["g"], 2 * pv)
                elif ss < 2:
                    e.wait_ge(S["a"], PLACE[True, NSH - 1] + 1)
                    e.wait_ge(S["gate"], NBLK)
                    e.wait_ge(S["tk"], 2 * NBLK)
                else:
                    e.wait_ge(S["acc"], NST)
                e.activation(P1H[:, 0:2, :], yv, ACT.Copy).then_inc(S["yh"], 1)

            def y_out(e):
                e.wait_ge(S["y"], b + 1)
                if pv:
                    e.wait_ge(S["bf"], 2 * pv)
                elif ss < 2:
                    for c in range(BPS, NBLK):
                        e.wait_ge(s_hd[c], 16)
                else:
                    steps_done(e)
                e.activation(R[:, 0:2, :], yv, ACT.Copy).then_inc(S["yh"], 1)

            def y_lo(e):
                e.wait_ge(S["yh"], b + 1)
                e.tensor_tensor(P1L[:, 0:2, :], yv, P1H[:, 0:2, :].bitcast(F32), ALU.subtract).then_inc(S["yl"], 1)
            at("tensor", "mix", b, mix)
            native = b in NATIVE
            at("scalar", "y_hi", b, y_out if native else y_hi)
            if not native:
                at("vector", "y_lo", b, y_lo)

            def had1(e):
                if native:
                    e.wait_ge(S["yh"], b + 1)
                else:
                    e.wait_ge(S["yl"], split + 1)
                if b == 0:
                    e.wait_ge(S["had2"], 4)
                bank_free(e, pa_name, ("had1", b, 0))
                for t in range(2):
                    n = 0
                    if native:
                        for k in range(2):
                            mm = e.matmul(pa[:, t * D:(t + 1) * D], R[:, k, t * P:(t + 1) * P], HADP[k],
                                          start=(k == 0), stop=(k == 1))
                        continue
                    for k in range(2):
                        for src in (P1H, P1L):
                            mm = e.matmul(pa[:, t * D:(t + 1) * D], src[:, k, t * P:(t + 1) * P],
                                          HAD2[:, k, :, :].rearrange("p a n -> p (a n)"),
                                          start=(n == 0), stop=(n == 3))
                            n += 1
                mm.then_inc(S["f"], 1)

            def stats1(e):
                k = 7 * b
                e.wait_ge(S["f"], b + 1)
                if b > 0:
                    e.wait_ge(S["st1"], k)
                if pv:
                    e.wait_ge(S["st2"], 6 * pv)
                e.tensor_reduce(st(0), pa[:, :].rearrange("p (t d) -> p t d", t=2),
                                AX.X, ALU.max, apply_absolute_value=True).then_inc(S["st1"], 1)
                e.wait_ge(S["st1"], k + 1)
                e.tensor_scalar(st(1), st(0), 1.0 / 16, EPS, ALU.mult, ALU.max).then_inc(S["st1"], 1)
                e.wait_ge(S["st1"], k + 2)
                e.reciprocal(st(2), st(1)).then_inc(S["st1"], 1)
                e.wait_ge(S["st1"], k + 3)
                e.tensor_scalar(st(3), st(2), QB, 1.0 / 16, ALU.mult, ALU.mult).then_inc(S["st1"], 1)

            def stats1_value(e):
                k = 7 * b
                e.wait_ge(S["st1"], k + 4)
                if b == 0:
                    e.wait_ge(S["sw"], 1)
                e.tensor_scalar(st(4), st(1), 1.0 / QB, SW[:, 2:3], ALU.mult, ALU.mult).then_inc(S["st1"], 1)
                e.wait_ge(S["st1"], k + 5)
                e.tensor_tensor(st(5), st(4), st(4), ALU.mult).then_inc(S["st1"], 1)
                e.wait_ge(S["st1"], k + 6)
                e.tensor_scalar(st(6), st(5), float(HID) ** -0.5, None, ALU.mult).then_inc(S["st1"], 1)

            def round1(e, t):
                e.wait_ge(S["st1"], 7 * b + 4)
                if t == 0 and pv:
                    e.wait_ge(S["q2"], pv)
                elif t == 0 and ss < 2:
                    for c in range(BPS, NBLK):
                        e.wait_ge(s_hd[c], 16)
                elif t == 0:
                    steps_done(e)
                if t == 0 and b == 0:
                    e.wait_ge(S["mag"], 2)
                e.activation(QF[:, t, :], pa[:, t * D:(t + 1) * D], ACT.Identity,
                             bias=MAG[:, 0:1], scale=st(3)[:, t:t + 1]).then_inc(S["qf"], 1)

            def quant1(e):
                e.wait_ge(S["qf"], 2 * b + 2)
                if pv:
                    e.wait_ge(S["q2t"], pv)
                elif ss < 2:
                    e.wait_ge(S["tab"], 8 * NSB)
                else:
                    e.wait_ge(S["acc"], NST)
                e.tensor_scalar(Q1, QF, MAGIC, None, ALU.subtract).then_inc(S["q1"], 1)
            at("tensor", "had1", b, had1)
            at("vector", "stats1", b, stats1)
            at("vector", "stats1_value", b, stats1_value)
            for t in range(2):
                at("scalar", "round1", b, lambda e, t=t: round1(e, t), t)
            at("vector", "quant1", b, quant1)

            turned1 = pa[:, 0:256].bitcast(BF16).rearrange("p (k t) -> p k t", k=2)

            def turn1(e):
                e.wait_ge(S["q1"], b + 1)
                if b == 0:
                    e.wait_ge(S["c16"], 16)
                bank_free(e, pa_name, ("turn1", b, 0))
                for t in range(2):
                    for k in range(2):
                        mm = e.transpose(turned1[:, k, t * P:(t + 1) * P], Q1[:, t, k * P:(k + 1) * P], IDB)
                mm.then_inc(S["q1t"], 1)
            at("tensor", "turn1", b, turn1)

            def turn1_out(e):
                e.wait_ge(S["q1t"], b + 1)
                if pv:
                    e.wait_ge(S["up"], 2 * pv)
                elif ss < 2:
                    e.wait_ge(S["xal"], NBLK)
                else:
                    e.wait_ge(S["acc"], NST)
                e.activation(Q1T[:, :, :], turned1, ACT.Copy).then_inc(S["q1c"], 1)
            at("scalar", "turn1_out", b, turn1_out)

            both = ((pa, pa_name), (pc, pc_name))

            def wide(e, j):
                e.wait_ge(S["q1c"], b + 1)
                if b == 0:
                    e.wait_ge(S["wt"], 6)
                bank_free(e, both[j][1], ("wide", b, j))
                for c in (2 * j, 2 * j + 1):
                    for k in range(2):
                        mm = e.matmul(both[j][0][:, (c % 2) * 256:(c % 2 + 1) * 256], WU[:, k, c * P:(c + 1) * P],
                                      Q1T[:, k, :], start=(k == 0), stop=(k == 1))
                mm.then_inc(S["up"], 1)

            def relu(e, j):
                e.wait_ge(S["up"], 2 * b + j + 1)
                if j == 0 and native:
                    e.wait_ge(S["f"], b + 1)
                elif j == 0 and pv:
                    e.wait_ge(S["bf"], 2 * pv)
                elif j == 0 and ss < 2:
                    for c in range(BPS, NBLK):
                        e.wait_ge(s_hd[c], 16)
                elif j == 0:
                    steps_done(e)
                e.activation(R[:, 2 * j:2 * j + 2, :], both[j][0][:, :].rearrange("p (c t) -> p c t", c=2), ACT.Relu)\
                 .then_inc(S["rl"], 1)

            def square(e, j):
                e.wait_ge(S["rl"], 2 * b + j + 1)
                v = R[:, 2 * j:2 * j + 2, :]
                e.tensor_tensor(v, v, v, ALU.mult).then_inc(S["sq2"] if j else S["sq"], 1)
            for j in range(2):
                at("tensor", "wide", b, lambda e, j=j: wide(e, j), j)
                at("scalar", "relu", b, lambda e, j=j: relu(e, j), j)
            at("vector", "square", b, lambda e: square(e, 0))
            at("gpsimd", "square2", b, lambda e: square(e, 1))

            def stage(e, j):
                e.wait_ge(S["sq"], b + 1)
                e.wait_ge(S["sq2"], b + 1)
                e.wait_ge(S["q1"], b + 1)
                if pv:
                    e.wait_ge(S["dn"], pv)
                e.tensor_tensor(U[:, 2 * j:2 * j + 2, :], R[:, 0:2, :], R[:, 2:4, :],
                                ALU.subtract if j else ALU.add).then_inc(S["bf"], 1)
            for j in range(2):
                at("vector", "stage", b, lambda e, j=j: stage(e, j), j)

            def v_hi(e, j):
                e.wait_ge(S["bf"], 2 * b + 1 + j)
                e.wait_ge(S["f"], b + 1)
                e.activation(P1H[:, 2 * j:2 * j + 2, :], U[:, 2 * j:2 * j + 2, :], ACT.Copy).then_inc(S["vh"], 1)

            def v_lo(e, j):
                e.wait_ge(S["vh"], 2 * split + j + 1)
                e.tensor_tensor(P1L[:, 2 * j:2 * j + 2, :], U[:, 2 * j:2 * j + 2, :],
                                P1H[:, 2 * j:2 * j + 2, :].bitcast(F32), ALU.subtract).then_inc(S["vl2"] if j else S["vl"], 1)
            if not native:
                for j in range(2):
                    at("scalar", "v_hi", b, lambda e, j=j: v_hi(e, j), j)
                at("vector", "v_lo", b, lambda e: v_lo(e, 0))
                at("gpsimd", "v_lo2", b, lambda e: v_lo(e, 1))

            def had2(e, t):
                if native:
                    e.wait_ge(S["bf"], 2 * b + 2)
                else:
                    e.wait_ge(S["vl"], split + 1)
                    e.wait_ge(S["vl2"], split + 1)
                bank_free(e, both[t][1], ("had2", b, t))
                for half in range(2):
                    n = 0
                    if native:
                        for k in range(2):
                            mm = e.matmul(both[t][0][:, half * D:(half + 1) * D], U[:, 2 * half + k, t * P:(t + 1) * P],
                                          HADP[k], start=(k == 0), stop=(k == 1))
                        continue
                    for k in range(2):
                        for src in (P1H, P1L):
                            mm = e.matmul(both[t][0][:, half * D:(half + 1) * D], src[:, 2 * half + k, t * P:(t + 1) * P],
                                          HAD2[:, k, :, :].rearrange("p a n -> p (a n)"),
                                          start=(n == 0), stop=(n == 3))
                            n += 1
                mm.then_inc(S["g"], 1)

            def stats2(e):
                k = 6 * b
                if pv:
                    e.wait_ge(S["fin"], 2 * pv)
                for t in range(2):
                    e.wait_ge(S["g"], 2 * b + t + 1)
                    e.tensor_reduce(ST[:, 7, t:t + 1], both[t][0][:, :], AX.X, ALU.max,
                                    apply_absolute_value=True).then_inc(S["st2"], 1)
                e.wait_ge(S["st2"], k + 2)
                e.wait_ge(S["st1"], 7 * b + 7)
                e.tensor_tensor(st(8), st(7), st(6), ALU.mult).then_inc(S["st2"], 1)
                e.wait_ge(S["st2"], k + 3)
                e.tensor_scalar(st(9), st(8), EPS, 1.0 / QB, ALU.max, ALU.mult).then_inc(S["st2"], 1)
                e.wait_ge(S["st2"], k + 4)
                e.reciprocal(st(10), st(9)).then_inc(S["st2"], 1)
                e.wait_ge(S["st2"], k + 5)
                e.tensor_tensor(st(11), st(10), st(6), ALU.mult).then_inc(S["st2"], 1)

            def round2(e, t):
                e.wait_ge(S["st2"], 6 * b + 6)
                e.activation(UF[:, t, :], both[t][0][:, :], ACT.Identity, bias=MAG[:, 0:1],
                             scale=st(11)[:, t:t + 1]).then_inc(S["q2f"], 1)

            def quant2(e):
                e.wait_ge(S["q2f"], 2 * b + 2)
                e.tensor_scalar(Q2[:, :, :], UF, MAGIC, None, ALU.subtract).then_inc(S["q2"], 1)
            for t in range(2):
                at("tensor", "had2", b, lambda e, t=t: had2(e, t), t)
                at("scalar", "round2", b, lambda e, t=t: round2(e, t), t)
            at("vector", "stats2", b, stats2)
            at("vector", "quant2", b, quant2)

            turned2 = pa[:, :].bitcast(BF16).rearrange("p (c t) -> p c t", c=4)

            def turn2(e):
                e.wait_ge(S["q2"], b + 1)
                bank_free(e, pa_name, ("turn2", b, 0))
                for t in range(2):
                    for c in range(4):
                        mm = e.transpose(turned2[:, c, t * P:(t + 1) * P], Q2[:, t, c * P:(c + 1) * P], IDB)
                mm.then_inc(S["q2t"], 1)

            def turn2_out(e):
                e.wait_ge(S["q2t"], b + 1)
                e.activation(Q2T, turned2, ACT.Copy).then_inc(S["q2c"], 1)

            def narrow(e):
                e.wait_ge(S["q2c"], b + 1)
                bank_free(e, pa_name, ("narrow", b, 0))
                for t in range(2):
                    for c in range(4):
                        mm = e.matmul(pa[:, t * D:(t + 1) * D], Q2T[:, c, t * P:(t + 1) * P],
                                      WD[:, c, :], start=(c == 0), stop=(c == 3))
                mm.then_inc(S["dn"], 1)

            def finish_scale(e):
                e.wait_ge(S["st2"], 6 * b + 6)
                if pv:
                    e.wait_ge(S["fin"], 2 * pv)
                e.tensor_scalar(st(12), st(9), SW[:, 3:4], None, ALU.mult).then_inc(S["fs"], 1)

            def finish(e):
                e.wait_ge(S["fs"], b + 1)
                e.wait_ge(S["dn"], b + 1)
                for t in range(2):
                    e.scalar_tensor_tensor(out=x1[:, t, :], in0=pa[:, t * D:(t + 1) * D],
                                           scalar=st(12)[:, t:t + 1], in1=x1[:, t, :],
                                           op0=ALU.mult, op1=ALU.add).then_inc(S["fin"], 1)
            at("tensor", "turn2", b, turn2)
            at("scalar", "turn2_out", b, turn2_out)
            at("tensor", "narrow", b, narrow)
            at("vector", "finish_scale", b, finish_scale)
            at("vector", "finish", b, finish)

            def store(e):
                e.wait_ge(S["fin"], 2 * b + 2)
                e.dma_start(out[b * 256:(b + 1) * 256, :].rearrange("(t p) d -> p t d", p=P), x1).then_inc(s_o[b], 16)
            at("sync", "store", b, store)

        def uses():
            table = []

            def use(bank, row, name, i, reader, count):
                table.append((bank, when[(name, row, i)], (name, row, i), reader, count))

            table.append(("AUX0", when[("weight_total", 0, 0)], ("weight_total", 0, 0), "sw", 1))
            for p in range(NSB):
                use("LB", p, "rank", 0, "pl", 18 * p + 7)
                use("LB", p, "sum", 0, "slt", 2 * p + 2)
            for r in range(NSB * SPAIRS):
                use("TR", r + 0, "xt", 0, "xtl", r + 1)
                use("HT2", r + 1, "ht", 0, "hl", PLACE[False, r] + 1)
            for b in range(NBLK):
                use("TR", b, "xa", 0, "xam", b + 1)
                for k in range(2):
                    use("HT2", b, "tok", k, "tko", 2 * b + k + 1)
                use("AUX0", b, "gate", 0, "glf", b + 1)
                for k in range(2):
                    use(f"AUX{k}", b, "h0w", k, "h0l", 2 * b + k + 1)
            for b in range(2 * NBLK):
                banks = [n for _, n in BANKS[SET[b]]]
                split = len([c for c in range(b) if c not in NATIVE])
                use(banks[0], b, "mix", 0, *(("yh", b + 1) if b in NATIVE else ("yl", split + 1)))
                use(banks[0], b, "had1", 0, "qf", 2 * b + 2)
                use(banks[0], b, "turn1", 0, "q1c", b + 1)
                use(banks[0], b, "turn2", 0, "q2c", b + 1)
                use(banks[0], b, "narrow", 0, "fin", 2 * b + 2)
                for k in range(2):
                    use(banks[k], b, "wide", k, "rl", 2 * b + k + 1)
                    use(banks[k], b, "had2", k, "q2f", 2 * b + k + 1)
            return table

        BANKS = [((AUX[0], "AUX0"), (LB, "LB")), ((AUX[1], "AUX1"), (LB, "LB")),
                 ((UP[0], "UP0"), (TR, "TR")), ((UP[1], "UP1"), (HT2, "HT2"))]
        FROM_STEPS = {"UP0": ("t3", NST), "UP1": ("t3", NST), "TR": ("xtl", NSB * SPAIRS), "HT2": ("hl", NST)}
        done = 0
        for b in range(NBLK):
            plan_adapter(b)
            if b % BPS == BPS - 1:
                plan_route(b // BPS)
            more = PAIRS_AFTER[b] if b < NBLK - 1 else NSB * SPAIRS - done
            for r in range(done, done + more):
                plan_pair(r)
            done += more
        for p in range(NSB):
            plan_collect(p)
        for b in range(2 * NBLK):
            plan_layer2(b)

        last_reader = {}
        lists = {}
        for bank, t, key, reader, count in uses():
            lists.setdefault(bank, []).append((t, key, reader, count))
        for bank, lst in lists.items():
            lst.sort()
            for prev, this in zip(lst, lst[1:]):
                last_reader[(bank, this[1])] = prev[2:]
            later = [v[1] for v in lst if v[1][0] not in ("xa", "xt", "tok", "ht")]
            if bank in FROM_STEPS:
                last_reader[(bank, later[0])] = FROM_STEPS[bank]

        def bank_free(e, bank, key):
            got = last_reader.get((bank, key))
            if got:
                e.wait_ge(S[got[0]], got[1])

        def last(e):
            for b in range(2 * NBLK):
                e.wait_ge(s_o[b], 16)
            e.wait_ge(S["gw"], 16)
            for b in range(NBLK):
                e.wait_ge(s_hd[b], 16)
            for j in range(2):
                e.wait_ge(s_y[j], 16 * ((NSB * SPAIRS + 1 - j) // 2))
        put("sync", 10000, last)

        block = ctx.enter_context(nc.Block())

        def run(engine, e):
            for _, _, fn in sorted(plan[engine], key=lambda v: v[:2]):
                fn(e)

        @block.sync
        def _(e):
            run("sync", e)

        @block.gpsimd
        def _(e):
            run("gpsimd", e)

        @block.scalar
        def _(e):
            run("scalar", e)

        @block.vector
        def _(e):
            run("vector", e)

        @block.tensor
        def _(e):
            run("tensor", e)


def kernel(x, itok_B_0_6, itok_B_1_198, L0_cond_W, L0_cond_A, L0_cond_Bm, L0_cond_scalings, L0_ffn_gate_w,
           L0_ffn_w1, L0_ffn_w2, L0_ffn_w3, L0_ffn_ws1, L0_ffn_ws2, L0_ffn_ws3, L1_cond_weights,
           L1_ffn_w_up, L1_ffn_w_down):
    import numpy as np
    import concourse.bacc as bacc
    from concourse import mybir as mb
    from concourse.bass_utils import run_bass_kernel_spmd

    consts = np.zeros((128, 728), np.float32)
    consts[:, 0:128] = np.eye(128)
    had = np.ones((1, 1), np.float32)
    while had.shape[0] < 128:
        had = np.block([[had, had], [had, -had]])
    consts[:, 128:256] = had
    consts[:, 256:264] = 8 - np.arange(8)
    consts[:, 264] = np.arange(128) // 16
    consts[:, 265:265 + STILES] = 128 * np.arange(STILES)
    consts[:, 568:696] = np.arange(128)
    for k in range(2):
        consts[:, 696 + k * TPS:696 + (k + 1) * TPS] = np.arange(128)[:, None] + 128 * np.arange(TPS)
    consts[:, 312:440], consts[:, 440:568] = had, -had
    consts16 = np.zeros((128, 3, 128), mb.dt.np(mb.dt.bfloat16))
    consts16[:, 0, :] = np.triu(np.ones((128, 128)), 1)
    consts16[:, 1, :] = 1
    consts16[:, 2, :] = np.eye(128)

    def wide(a, k):
        return np.asarray(a).T.reshape(k, 128, -1).transpose(1, 0, 2)

    def pair(a, b):
        return np.concatenate([wide(a, 2), wide(b, 2)], axis=2).reshape(128, 512)

    w1, w2, w3 = np.asarray(L0_ffn_w1), np.asarray(L0_ffn_w2), np.asarray(L0_ffn_w3)
    x2 = np.asarray(x).reshape(4096, 256)
    ins = [
        ("xT", x2.T), ("x", x2),
        ("adapter", np.asarray(itok_B_0_6)), ("cond", np.asarray(itok_B_1_198)),
        ("WA", np.concatenate([
            wide(L0_cond_W, 2).reshape(128, 512), wide(np.asarray(L0_cond_A).reshape(128, 256), 2).reshape(128, 256),
            np.asarray(L0_cond_Bm).transpose(0, 2, 1).reshape(128, 256), wide(L0_ffn_gate_w, 2).reshape(128, 16),
            pair(L0_ffn_ws1, L0_ffn_ws3), np.asarray(L0_ffn_ws2).T], axis=1)),
        ("WE", np.stack([np.concatenate([pair(w1[i], w3[i]), w2[i].T], axis=1) for i in range(8)])),
        ("scal", np.repeat(np.asarray(L0_cond_scalings), 16).reshape(128, 1)),
        ("cw", np.asarray(L1_cond_weights).reshape(200, 1024)),
        ("wuT", np.asarray(L1_ffn_w_up).T), ("wdT", np.asarray(L1_ffn_w_down).T),
        ("consts", consts), ("consts16", consts16),
    ]
    nc = bacc.Bacc("TRN2", target_bir_lowering=False, num_devices=1)
    arrays, args = {}, []
    for name, a in ins:
        a = np.ascontiguousarray(a)
        arrays["in_" + name] = a
        args.append(nc.dram_tensor("in_" + name, a.shape, mb.dt.from_np(a.dtype), kind="ExternalInput").ap())
    out = nc.dram_tensor("out_0", (4096, 256), mb.dt.float32, kind="ExternalOutput").ap()
    adapter_moe_quant_ffn(nc, *args, out)
    r = run_bass_kernel_spmd(nc, [arrays], core_ids=[0])
    return r.results[0]["out_0"].reshape(128, 32, 256)
```
